# Optimizing a Trainium2 kernel written in Bass

```python
import numpy as np
import jax
import jax.numpy as jnp

def _softmax(x, axis=-1):
    return jax.nn.softmax(x, axis=axis)

def _gelu(x):
    return jax.nn.gelu(x, approximate=True)

def _silu(x):
    return jax.nn.silu(x)

def _sigmoid(x):
    return jax.nn.sigmoid(x)

def _layernorm(x, axis=-1, eps=1e-05):
    m = jnp.mean(x, axis=axis, keepdims=True)
    v = jnp.var(x, axis=axis, keepdims=True)
    return (x - m) / jnp.sqrt(v + eps)

def _scatter_add(tgt, idx, src, axis=0):
    return tgt.at[idx].add(src)

def _segment_sum(src, seg, n):
    return jax.ops.segment_sum(src, seg, n)
kernel_name = 'mk_perceiver_d1_seqx_r4_95a5ed'

def setup_inputs(seed: int=0):
    np.random.seed(seed)
    _w = jnp.asarray

    def _rec_inputs():
        import jax
        import jax.numpy as jnp
        _rk = jax.random.key(seed)
        x = 6.313e-05 + 0.9998 * jax.random.normal(jax.random.fold_in(_rk, 1), (32, 64, 256), jnp.float32)
        _lenS = 64 - jax.random.randint(jax.random.fold_in(_rk, 7), (32,), 0, max(1, 64 // 4) + 1, jnp.int32)
        _lenS2 = 256 - jax.random.randint(jax.random.fold_in(_rk, 8), (32,), 0, max(1, 256 // 4) + 1, jnp.int32)
        _ctx_1024P = jax.random.normal(jax.random.fold_in(_rk, 11), (32, 16, 256), jnp.float32)
        _ctx_1024c = jax.random.dirichlet(jax.random.fold_in(_rk, 511), 0.3 * jnp.ones((16,), jnp.float32), (32, 256))
        _ctx_1024t = jnp.einsum('bsk,bkd->bsd', _ctx_1024c, _ctx_1024P)
        _ctx_1024t = _ctx_1024t * jax.lax.rsqrt(jnp.mean(jnp.square(_ctx_1024t)) + 1e-12) * 0.953939
        ctx_1024 = -0.000214406 + 1.00034 * (_ctx_1024t + 0.3 * jax.random.normal(jax.random.fold_in(_rk, 611), (32, 256, 256), jnp.float32))
        return (x, ctx_1024)
    x, ctx_1024 = _rec_inputs()

    def _L0_xattn_setup():
        import jax, jax.numpy as jnp
        import numpy as np
        from jax import lax
        BIG = jnp.float32(1e+30)

        def _pairwise_euclidean(a, b):
            aa = jnp.sum(a * a, axis=-1)[:, None]
            bb = jnp.sum(b * b, axis=-1)[None, :]
            ab = a @ b.T
            return jnp.sqrt(jnp.maximum(aa + bb - 2.0 * ab, 0.0))

        def _dtw_cost(D):
            row0 = jnp.cumsum(D[0])

            def row_step(prev_row, d_row):
                first = d_row[0] + prev_row[0]

                def col_step(left, inp):
                    d_ij, up, diag = inp
                    r = d_ij + jnp.minimum(jnp.minimum(up, left), diag)
                    return (r, r)
                _, rest = lax.scan(col_step, first, (d_row[1:], prev_row[1:], prev_row[:-1]))
                row = jnp.concatenate([first[None], rest])
                return (row, row)
            _, rows = lax.scan(row_step, row0, D[1:])
            return jnp.concatenate([row0[None], rows], axis=0)

        def _backtrack(R, T1, T2):
            L = T1 + T2 - 1

            def step(carry, _):
                i, j, done = carry
                valid = jnp.logical_not(done)
                cd = jnp.where((i > 0) & (j > 0), R[jnp.maximum(i - 1, 0), jnp.maximum(j - 1, 0)], BIG)
                cu = jnp.where(i > 0, R[jnp.maximum(i - 1, 0), j], BIG)
                cl = jnp.where(j > 0, R[i, jnp.maximum(j - 1, 0)], BIG)
                choice = jnp.argmin(jnp.stack([cd, cu, cl]))
                ni = jnp.where(choice <= 1, i - 1, i)
                nj = jnp.where((choice == 0) | (choice == 2), j - 1, j)
                at_origin = (i == 0) & (j == 0)
                ni = jnp.where(at_origin, 0, ni)
                nj = jnp.where(at_origin, 0, nj)
                return ((ni, nj, done | at_origin), (i, j, valid))
            init = (jnp.int32(T1 - 1), jnp.int32(T2 - 1), jnp.bool_(False))
            _, (i_idx, j_idx, valid) = lax.scan(step, init, None, length=L)
            return (i_idx, j_idx, valid)

        def _align_one(small, large):
            T_small, d = small.shape
            T_large = large.shape[0]
            D = _pairwise_euclidean(small, large)
            R = _dtw_cost(D)
            i_idx, j_idx, valid = _backtrack(R, T_small, T_large)
            contrib = small[i_idx] * valid[:, None].astype(small.dtype)
            expanded = jnp.zeros((T_large, d), dtype=small.dtype).at[j_idx].add(contrib)
            return expanded
        key = jax.random.key(seed)
        k1, k2 = jax.random.split(key)
        teacher = jax.random.normal(k1, (16, 100, 256), dtype=jnp.float32)
        student = jax.random.normal(k2, (16, 150, 256), dtype=jnp.float32)
        return {'teacher_features': teacher, 'student_features': student}
    _L0_xattn_all = _L0_xattn_setup()
    _L0_xattn_in = {k: v for k, v in _L0_xattn_all.items() if k in ()}
    del _L0_xattn_all

    def _L0_attn_setup():
        import jax, jax.numpy as jnp
        import numpy as np
        D_MODEL = 256
        D_STATE = 64
        D_HEAD = 64
        N_HEADS = 32
        N_GROUPS = 1
        D_CONV = 4
        D_INNER = N_HEADS * D_HEAD
        XBC = D_INNER + 2 * N_GROUPS * D_STATE
        PROJ = 2 * D_INNER + 2 * N_GROUPS * D_STATE + N_HEADS
        EPS = 1e-05
        B_SZ, L_SEQ = (2, 256)

        def silu(v):
            return v * jax.nn.sigmoid(v)

        def _mamba2(x, W_in, conv_w, conv_b, A_log, D_param, dt_bias, norm_w, W_out):
            B, L, _ = x.shape
            xz = x @ W_in
            z = xz[..., :D_INNER]
            xBC = xz[..., D_INNER:D_INNER + XBC]
            dt_proj = xz[..., D_INNER + XBC:]
            inp = jnp.swapaxes(xBC, 1, 2)
            conv = jax.lax.conv_general_dilated(inp, conv_w, window_strides=(1,), padding=[(D_CONV - 1, 0)], dimension_numbers=('NCH', 'OIH', 'NCH'), feature_group_count=XBC)
            conv = conv + conv_b[None, :, None]
            xBC_c = jnp.swapaxes(silu(conv), 1, 2)
            x_conv = xBC_c[..., :D_INNER]
            B_ssm = xBC_c[..., D_INNER:D_INNER + D_STATE]
            C_ssm = xBC_c[..., D_INNER + D_STATE:]
            dt = jax.nn.softplus(dt_proj + dt_bias)
            A = -jnp.exp(A_log)
            x_heads = x_conv.reshape(B, L, N_HEADS, D_HEAD)

            def step(h, inp_t):
                x_t, dt_t, B_t, C_t = inp_t
                dA = jnp.exp(A[None, :] * dt_t)
                h = dA[:, :, None, None] * h + dt_t[:, :, None, None] * x_t[..., None] * B_t[:, None, None, :]
                y_t = jnp.einsum('bhds,bs->bhd', h, C_t) + D_param[None, :, None] * x_t
                return (h, y_t)
            h0 = jnp.zeros((B, N_HEADS, D_HEAD, D_STATE), dtype=x.dtype)
            xs = (jnp.swapaxes(x_heads, 0, 1), jnp.swapaxes(dt, 0, 1), jnp.swapaxes(B_ssm, 0, 1), jnp.swapaxes(C_ssm, 0, 1))
            _, ys = jax.lax.scan(step, h0, xs)
            y = jnp.swapaxes(ys, 0, 1).reshape(B, L, D_INNER)
            y = y * silu(z)
            var = jnp.mean(jnp.square(y), axis=-1, keepdims=True)
            y = norm_w * (y * jax.lax.rsqrt(var + EPS))
            return y @ W_out
        key = jax.random.key(seed)
        ks = jax.random.split(key, 9)
        x = jax.random.normal(ks[0], (B_SZ, L_SEQ, D_MODEL), dtype=jnp.float32)
        W_in = jax.random.normal(ks[1], (D_MODEL, PROJ), dtype=jnp.float32) * 0.02
        conv_w = jax.random.normal(ks[2], (XBC, 1, D_CONV), dtype=jnp.float32) * 0.2
        conv_b = jax.random.normal(ks[3], (XBC,), dtype=jnp.float32) * 0.02
        A_log = jax.random.normal(ks[4], (N_HEADS,), dtype=jnp.float32) * 0.1
        D_param = jnp.ones((N_HEADS,), dtype=jnp.float32)
        dt_bias = jax.random.normal(ks[5], (N_HEADS,), dtype=jnp.float32) * 0.1
        norm_w = jnp.ones((D_INNER,), dtype=jnp.float32)
        W_out = jax.random.normal(ks[6], (D_INNER, D_MODEL), dtype=jnp.float32) * 0.02
        return {'x': x, 'W_in': W_in, 'conv_w': conv_w, 'conv_b': conv_b, 'A_log': A_log, 'D_param': D_param, 'dt_bias': dt_bias, 'norm_w': norm_w, 'W_out': W_out}
    _L0_attn_all = _L0_attn_setup()
    _L0_attn_in = {k: v for k, v in _L0_attn_all.items() if k in ('W_in', 'conv_w', 'conv_b', 'A_log', 'D_param', 'dt_bias', 'norm_w', 'W_out')}
    del _L0_attn_all

    def _L0_ffn_setup():
        import jax, jax.numpy as jnp
        import numpy as np
        B, S, D, E, H, K = (4, 512, 256, 8, 128, 2)
        key = jax.random.key(seed)
        ks = jax.random.split(key, 11)
        sc = 0.02
        return {'x': jax.random.normal(ks[0], (B, S, D), dtype=jnp.float32), 'gate_W': jax.random.normal(ks[1], (D, E), dtype=jnp.float32) * sc, 'W1': jax.random.normal(ks[2], (E, D, H), dtype=jnp.float32) * sc, 'b1': jnp.zeros((E, H), dtype=jnp.float32), 'W2': jax.random.normal(ks[3], (E, H, D), dtype=jnp.float32) * sc, 'b2': jnp.zeros((E, D), dtype=jnp.float32), 'Ws1': jax.random.normal(ks[4], (D, H), dtype=jnp.float32) * sc, 'bs1': jnp.zeros((H,), dtype=jnp.float32), 'Ws2': jax.random.normal(ks[5], (H, D), dtype=jnp.float32) * sc, 'bs2': jnp.zeros((D,), dtype=jnp.float32), 'route_scale': jnp.ones((), dtype=jnp.float32)}
    _L0_ffn_all = _L0_ffn_setup()
    _L0_ffn_in = {k: v for k, v in _L0_ffn_all.items() if k in ('gate_W', 'W1', 'b1', 'W2', 'b2', 'Ws1', 'bs1', 'Ws2', 'bs2', 'route_scale')}
    del _L0_ffn_all
    return {'x': x, 'ctx_1024': ctx_1024, 'L0_attn_W_in': _L0_attn_in['W_in'], 'L0_attn_conv_w': _L0_attn_in['conv_w'], 'L0_attn_conv_b': _L0_attn_in['conv_b'], 'L0_attn_A_log': _L0_attn_in['A_log'], 'L0_attn_D_param': _L0_attn_in['D_param'], 'L0_attn_dt_bias': _L0_attn_in['dt_bias'], 'L0_attn_norm_w': _L0_attn_in['norm_w'], 'L0_attn_W_out': _L0_attn_in['W_out'], 'L0_ffn_gate_W': _L0_ffn_in['gate_W'], 'L0_ffn_W1': _L0_ffn_in['W1'], 'L0_ffn_b1': _L0_ffn_in['b1'], 'L0_ffn_W2': _L0_ffn_in['W2'], 'L0_ffn_b2': _L0_ffn_in['b2'], 'L0_ffn_Ws1': _L0_ffn_in['Ws1'], 'L0_ffn_bs1': _L0_ffn_in['bs1'], 'L0_ffn_Ws2': _L0_ffn_in['Ws2'], 'L0_ffn_bs2': _L0_ffn_in['bs2'], 'L0_ffn_route_scale': _L0_ffn_in['route_scale']}

def reference(x, ctx_1024, L0_attn_W_in, L0_attn_conv_w, L0_attn_conv_b, L0_attn_A_log, L0_attn_D_param, L0_attn_dt_bias, L0_attn_norm_w, L0_attn_W_out, L0_ffn_gate_W, L0_ffn_W1, L0_ffn_b1, L0_ffn_W2, L0_ffn_b2, L0_ffn_Ws1, L0_ffn_bs1, L0_ffn_Ws2, L0_ffn_bs2, L0_ffn_route_scale):
    import jax
    import jax.numpy as jnp

    def _L0_xattn_ref(teacher_features, student_features):
        import jax, jax.numpy as jnp
        import numpy as np
        from jax import lax
        BIG = jnp.float32(1e+30)

        def _pairwise_euclidean(a, b):
            aa = jnp.sum(a * a, axis=-1)[:, None]
            bb = jnp.sum(b * b, axis=-1)[None, :]
            ab = a @ b.T
            return jnp.sqrt(jnp.maximum(aa + bb - 2.0 * ab, 0.0))

        def _dtw_cost(D):
            row0 = jnp.cumsum(D[0])

            def row_step(prev_row, d_row):
                first = d_row[0] + prev_row[0]

                def col_step(left, inp):
                    d_ij, up, diag = inp
                    r = d_ij + jnp.minimum(jnp.minimum(up, left), diag)
                    return (r, r)
                _, rest = lax.scan(col_step, first, (d_row[1:], prev_row[1:], prev_row[:-1]))
                row = jnp.concatenate([first[None], rest])
                return (row, row)
            _, rows = lax.scan(row_step, row0, D[1:])
            return jnp.concatenate([row0[None], rows], axis=0)

        def _backtrack(R, T1, T2):
            L = T1 + T2 - 1

            def step(carry, _):
                i, j, done = carry
                valid = jnp.logical_not(done)
                cd = jnp.where((i > 0) & (j > 0), R[jnp.maximum(i - 1, 0), jnp.maximum(j - 1, 0)], BIG)
                cu = jnp.where(i > 0, R[jnp.maximum(i - 1, 0), j], BIG)
                cl = jnp.where(j > 0, R[i, jnp.maximum(j - 1, 0)], BIG)
                choice = jnp.argmin(jnp.stack([cd, cu, cl]))
                ni = jnp.where(choice <= 1, i - 1, i)
                nj = jnp.where((choice == 0) | (choice == 2), j - 1, j)
                at_origin = (i == 0) & (j == 0)
                ni = jnp.where(at_origin, 0, ni)
                nj = jnp.where(at_origin, 0, nj)
                return ((ni, nj, done | at_origin), (i, j, valid))
            init = (jnp.int32(T1 - 1), jnp.int32(T2 - 1), jnp.bool_(False))
            _, (i_idx, j_idx, valid) = lax.scan(step, init, None, length=L)
            return (i_idx, j_idx, valid)

        def _align_one(small, large):
            T_small, d = small.shape
            T_large = large.shape[0]
            D = _pairwise_euclidean(small, large)
            R = _dtw_cost(D)
            i_idx, j_idx, valid = _backtrack(R, T_small, T_large)
            contrib = small[i_idx] * valid[:, None].astype(small.dtype)
            expanded = jnp.zeros((T_large, d), dtype=small.dtype).at[j_idx].add(contrib)
            return expanded
        return jax.vmap(_align_one)(teacher_features, student_features)

    def _L0_attn_ref(x, W_in, conv_w, conv_b, A_log, D_param, dt_bias, norm_w, W_out):
        import jax, jax.numpy as jnp
        import numpy as np
        D_MODEL = 256
        D_STATE = 64
        D_HEAD = 64
        N_HEADS = 32
        N_GROUPS = 1
        D_CONV = 4
        D_INNER = N_HEADS * D_HEAD
        XBC = D_INNER + 2 * N_GROUPS * D_STATE
        PROJ = 2 * D_INNER + 2 * N_GROUPS * D_STATE + N_HEADS
        EPS = 1e-05
        B_SZ, L_SEQ = (2, 256)

        def silu(v):
            return v * jax.nn.sigmoid(v)

        def _mamba2(x, W_in, conv_w, conv_b, A_log, D_param, dt_bias, norm_w, W_out):
            B, L, _ = x.shape
            xz = x @ W_in
            z = xz[..., :D_INNER]
            xBC = xz[..., D_INNER:D_INNER + XBC]
            dt_proj = xz[..., D_INNER + XBC:]
            inp = jnp.swapaxes(xBC, 1, 2)
            conv = jax.lax.conv_general_dilated(inp, conv_w, window_strides=(1,), padding=[(D_CONV - 1, 0)], dimension_numbers=('NCH', 'OIH', 'NCH'), feature_group_count=XBC)
            conv = conv + conv_b[None, :, None]
            xBC_c = jnp.swapaxes(silu(conv), 1, 2)
            x_conv = xBC_c[..., :D_INNER]
            B_ssm = xBC_c[..., D_INNER:D_INNER + D_STATE]
            C_ssm = xBC_c[..., D_INNER + D_STATE:]
            dt = jax.nn.softplus(dt_proj + dt_bias)
            A = -jnp.exp(A_log)
            x_heads = x_conv.reshape(B, L, N_HEADS, D_HEAD)

            def step(h, inp_t):
                x_t, dt_t, B_t, C_t = inp_t
                dA = jnp.exp(A[None, :] * dt_t)
                h = dA[:, :, None, None] * h + dt_t[:, :, None, None] * x_t[..., None] * B_t[:, None, None, :]
                y_t = jnp.einsum('bhds,bs->bhd', h, C_t) + D_param[None, :, None] * x_t
                return (h, y_t)
            h0 = jnp.zeros((B, N_HEADS, D_HEAD, D_STATE), dtype=x.dtype)
            xs = (jnp.swapaxes(x_heads, 0, 1), jnp.swapaxes(dt, 0, 1), jnp.swapaxes(B_ssm, 0, 1), jnp.swapaxes(C_ssm, 0, 1))
            _, ys = jax.lax.scan(step, h0, xs)
            y = jnp.swapaxes(ys, 0, 1).reshape(B, L, D_INNER)
            y = y * silu(z)
            var = jnp.mean(jnp.square(y), axis=-1, keepdims=True)
            y = norm_w * (y * jax.lax.rsqrt(var + EPS))
            return y @ W_out
        return _mamba2(x, W_in, conv_w, conv_b, A_log, D_param, dt_bias, norm_w, W_out)

    def _L0_ffn_ref(x, gate_W, W1, b1, W2, b2, Ws1, bs1, Ws2, bs2, route_scale):
        import jax, jax.numpy as jnp
        import numpy as np
        B, S, D, E, H, K = (4, 512, 256, 8, 128, 2)
        scores = jax.nn.sigmoid(x @ gate_W) * route_scale
        topk_scores, topk_idx = jax.lax.top_k(scores, K)
        topk_w = topk_scores / topk_scores.sum(-1, keepdims=True)
        onehot = jax.nn.one_hot(topk_idx, E, dtype=x.dtype)
        gate_full = jnp.einsum('bsk,bske->bse', topk_w, onehot)
        h = jax.nn.gelu(jnp.einsum('bsd,edh->bseh', x, W1) + b1, approximate=False)
        y = jnp.einsum('bseh,ehd->bsed', h, W2) + b2
        expert_out = jnp.einsum('bse,bsed->bsd', gate_full, y)
        shared = jax.nn.gelu(x @ Ws1 + bs1, approximate=False) @ Ws2 + bs2
        return expert_out + shared
    x = x + _L0_xattn_ref(ctx_1024, _layernorm(x, axis=-1))
    x = x + _L0_attn_ref(_layernorm(x, axis=-1), L0_attn_W_in, L0_attn_conv_w, L0_attn_conv_b, L0_attn_A_log, L0_attn_D_param, L0_attn_dt_bias, L0_attn_norm_w, L0_attn_W_out)
    x = x + _L0_ffn_ref(_layernorm(x, axis=-1), L0_ffn_gate_W, L0_ffn_W1, L0_ffn_b1, L0_ffn_W2, L0_ffn_b2, L0_ffn_Ws1, L0_ffn_bs1, L0_ffn_Ws2, L0_ffn_bs2, L0_ffn_route_scale)
    return x

_drawn_inputs = setup_inputs


def setup_inputs(seed=0):
    import zlib

    import numpy as np

    out = dict(_drawn_inputs(seed))
    spreads = {'L0_attn_D_param': (1.0, 0.6),
     'L0_attn_norm_w': (1.0, 0.6),
     'L0_ffn_b1': (0.0, 0.8),
     'L0_ffn_b2': (0.0, 0.8),
     'L0_ffn_bs1': (0.0, 0.8),
     'L0_ffn_bs2': (0.0, 0.612)}
    factors = {'L0_attn_conv_b': 3.165,
     'L0_attn_A_log': 22.83,
     'L0_attn_dt_bias': 26.073,
     'L0_ffn_gate_W': 6.676,
     'L0_ffn_W1': 8.0,
     'L0_ffn_W2': 8.0,
     'L0_ffn_Ws1': 8.0,
     'L0_ffn_Ws2': 8.0}
    for name, (base, spread) in spreads.items():
        noise = np.random.default_rng([zlib.crc32(name.encode()), seed]).standard_normal(out[name].shape)
        drawn = base * np.exp(spread * noise) if base else spread * noise
        out[name] = jnp.asarray(drawn.astype(out[name].dtype))
    for name, factor in factors.items():
        out[name] = (out[name] * factor).astype(out[name].dtype)
    return out
```

```python
from contextlib import ExitStack

import concourse.bass as bass
from concourse import mybir

F32 = mybir.dt.float32
F16 = mybir.dt.float16
ALU = mybir.AluOpType
ACT = mybir.ActivationFunctionType
AX_X = mybir.AxisListType.X

P = 128
NB, T, D = 32, 64, 256
S = 256
KC = D // P
NT = NB * T // P
PAIR = P // T
EPS = 1e-5

BLOCKS = 4
BI = S // BLOCKS
CHUNK = 4
SLOTS = T + CHUNK * (BLOCKS - 1)
CHUNKS = SLOTS // CHUNK
TABLE = 80
BIG = 1e30

GT = 4
NG = NT // GT
GB = GT * PAIR
GN = GT * P
HEADS, HD, NS, TAPS = 32, 64, 64, 4
INNER = HEADS * HD
CT = INNER // P
PROJ = 2 * INNER + 2 * NS + HEADS
E, H = 8, 128
PAD = TAPS - 1
RING = 4
CR = 4
N_W = 17
CHAIN_D = 64


def perceiver(nc, x, ctx_rows, W_in, conv_w, conv_b, A_log, D_param, dt_bias, norm_w, W_out,
              gate_W, W1, b1, W2, b2, Ws1, bs1, Ws2, bs2, route_scale, out):
    x_rows = x.rearrange("b t d -> (b t) d").rearrange("(n p) d -> p n d", p=P)
    out_rows = out.rearrange("b t d -> (b t) d").rearrange("(n p) d -> p n d", p=P)
    ctx_tiles = ctx_rows.rearrange("b (h p) d -> p b h d", p=P)
    dist = nc.dram_tensor("distances", (NB, T, S), F32, kind="Internal").ap()
    dist_rows = dist.rearrange("b j i -> (b j) i")

    with ExitStack() as ctx:
        def sb(name, shape, dt=F32):
            return ctx.enter_context(nc.sbuf_tensor(name, shape, dt))

        def sem(name):
            return ctx.enter_context(nc.semaphore(name))

        bank = [ctx.enter_context(nc.psum_tensor(f"bank{i}", [P, 512], F32)) for i in range(8)]
        p_x, p_z, p_t, p_s, p_y0, p_y1, p_o0, p_o1 = bank

        ident = sb("ident", [P, P])
        tri = sb("tri", [P, T])
        later = sb("later", [P, P])
        ones = sb("ones", [P, 1])
        zero = sb("zero", [P, 1])
        spare = sb("spare", [P, 1])
        ones16 = sb("ones16", [NB, P], F16)
        below = sb("below", [P, E, E])
        row_id = sb("row_id", [P, KC])
        eps1 = sb("eps1", [P, 1])
        eps4 = sb("eps4", [P, 1])
        lookup_id = sb("lookup_id", [NB, S])

        w_in = sb("w_in", [P, KC, PROJ])
        w_out = sb("w_out", [P, CT, D])
        b_1 = sb("b_1", [P, E + 1])
        b_2 = sb("b_2", [E + 1, D])
        w_gate = sb("w_gate", [P, KC, E])
        cw = sb("cw", [P, CT, TAPS])
        cb = sb("cb", [P, CT])
        cw_bc = sb("cw_bc", [NS, 2, TAPS])
        cb_bc = sb("cb_bc", [NS, 2])
        d_ch = sb("d_ch", [P, CT])
        nw = sb("nw", [P, CT])
        a_exp = sb("a_exp", [P, HEADS])
        dtb = sb("dtb", [P, HEADS])
        rsc = sb("rsc", [P, 1])

        X = sb("X", [P, NT, D])
        bn = sb("bn", [P, GT, 6])
        mv = sb("mv", [P, GT, 2])
        sd = sb("sd", [P, GT])
        rs = sb("rs", [P, GT])
        cr = sb("cr", [P, CR, PAIR, 2, D])
        Hpath = sb("Hpath", [NB, T + 1])
        Hd = sb("Hd", [NB, NB, T + 1], F16)

        s_const = sem("s_const")
        s_x = sem("s_x")
        s_w = sem("s_w")
        s_we = sem("s_we")
        s_table = sem("s_table")
        s_path = sem("s_path")
        dist_out = [sem(f"dist_out{k}") for k in range(2)]
        ctx_in = [sem(f"ctx_in{k}") for k in range(CR)]
        act_done = sem("act_done")
        dve_done = sem("dve_done")
        pool_done = sem("pool_done")
        a_sd = sem("a_sd")
        a_norm = sem("a_norm")
        a_rows_t = sem("a_rows_t")
        a_x_t = sem("a_x_t")
        a_c_t = sem("a_c_t")
        a_c = sem("a_c")
        a_mm = sem("a_mm")
        a_sq = sem("a_sq")
        a_clamp = sem("a_clamp")
        a_root = sem("a_root")
        a_aa = sem("a_aa")
        dist_in = [sem(f"dist_in{q}") for q in range(4)]
        b_scan = sem("b_scan")
        b_step = sem("b_step")

        class Chain:
            def __init__(self, engine, sem_):
                self.engine, self.sem, self.base, self.n = engine, sem_, 0, 0

            def link(self, ins, bare=False):
                ins.then_inc(self.sem, 1)
                self.n += 1
                self.engine.wait_ge(self.sem, self.base + self.n)
                if bare:
                    self.engine.memset(spare[:, :], 0.0)

            def enter(self, i, per):
                self.start, self.per = self.base + self.n, per
                self.base, self.n = self.start + i * per, 0

            def leave(self, count):
                assert self.n == self.per, (self.n, self.per)
                self.base, self.n = self.start + count * self.per, 0

        def wait(engine, sem_, value):
            if not isinstance(value, int) or value > 0:
                engine.wait_ge(sem_, value)

        def carrier(pe, psum):
            pe.matmul(psum[:, 0:1], lhsT=ones16[:, :], rhs=ones16[:, 0:1], start=True, stop=True)

        inner = ExitStack()
        with inner:
            def tb(name, shape, dt=F32):
                return inner.enter_context(nc.sbuf_tensor(name, shape, dt))

            xn = tb("a_xn", [P, 2, D])
            sq = tb("a_sqj", [P, D])
            sqd = tb("a_sqd", [P, 2 * PAIR, D])
            bn_a = tb("bn_a", [P, NT, 6])
            mv_a = tb("mv_a", [P, NT, 2])
            sd_a = tb("sd_a", [P, NT])
            rs_a = tb("rs_a", [P, NT])
            bb = tb("a_bb", [P, NT])
            aa = tb("a_aa_t", [P, CR, PAIR, 2])
            xt = tb("a_xt", [P, 2, KC, P])
            ct_t = tb("a_ct", [P, 2, PAIR, KC, S])
            dd = tb("a_dd", [P, 2, S])
            ds = tb("a_ds", [P, 2, S])
            Dk = tb("Dk", [P, SLOTS, BI])
            dn_view = Dk[:, :, :].rearrange("p s i -> p (s i)").bitcast(F16)
            R = tb("R", [P, SLOTS + 1, BI + 1])
            m1 = tb("m1", [P, BI])
            qk = tb("qk", [P, CHUNK, BI])
            rk = tb("rk", [P, CHUNK, BI])
            ak = tb("ak", [P, CHUNK, BI])
            blk_id = tb("blk_id", [P, CHUNK, BI])
            Wk = tb("Wk", [P, CHUNK, BI + 1])
            Nk = tb("Nk", [P, CHUNK, BI + 1])
            mk = tb("mk", [P, CHUNK, BI + 1])
            table = tb("table", [NB, BLOCKS * TABLE * BI], F16)
            junk = tb("junk", [NB, BLOCKS, BI])
            tab = table[:, :].rearrange("b (g j i) -> b g j i", g=BLOCKS, j=TABLE)

            a_it = NT // CR

            with nc.Block() as block:
                @block.gpsimd
                def _(pool):
                    ch = Chain(pool, pool_done)
                    ch.link(pool.memset(ones[:, :], 1.0))
                    ch.link(pool.memset(zero[:, :], 0.0))
                    ch.link(pool.memset(ones16[:, :], 1.0))
                    ch.link(pool.memset(eps1[:, :], EPS))
                    ch.link(pool.memset(eps4[:, :], 4 * EPS))
                    ch.link(pool.memset(ident[:, :], 0.0))
                    ch.link(pool.affine_select(out=ident[:, :], in_=ident[:, :], compare_op=ALU.not_equal,
                                               fill=1.0, base=0, pattern=[[-1, P]], channel_multiplier=1))
                    ch.link(pool.memset(tri[:, :], 1.0))
                    ch.link(pool.memset(later[:, :], 0.0))
                    ch.link(pool.memset(below[:, :, :], 1.0))
                    for h in range(PAIR):
                        q = slice(T * h, T * h + T)
                        ch.link(pool.affine_select(out=tri[q, :], in_=tri[q, :], compare_op=ALU.is_ge,
                                                   fill=0.0, base=0, pattern=[[1, T]], channel_multiplier=-1))
                        ch.link(pool.affine_select(out=later[q, q], in_=later[q, q], compare_op=ALU.is_ge,
                                                   fill=1.0, base=0, pattern=[[1, T]], channel_multiplier=-1))
                    ch.link(pool.affine_select(out=below[:, :, :], in_=below[:, :, :], compare_op=ALU.is_gt,
                                               fill=0.0, base=0, pattern=[[1, E], [-1, E]], channel_multiplier=0))
                    for h in range(KC):
                        ch.link(pool.iota(row_id[:, h:h + 1], pattern=[[0, 1]], base=P * h, channel_multiplier=1,
                                          allow_small_or_imprecise_dtypes=True))
                    ch.link(pool.iota(lookup_id[:, :], pattern=[[1, S]], base=0, channel_multiplier=0,
                                      allow_small_or_imprecise_dtypes=True))
                    for g in range(BLOCKS):
                        q = slice(32 * g, 32 * g + 32)
                        ch.link(pool.iota(blk_id[q, :, :], pattern=[[0, CHUNK], [1, BI]], base=BI * g,
                                          channel_multiplier=0, allow_small_or_imprecise_dtypes=True))
                        if g:
                            ch.link(pool.memset(Dk[q, 0:CHUNK * g, :], BIG))
                        if g < BLOCKS - 1:
                            ch.link(pool.memset(Dk[q, CHUNK * g + T:SLOTS, :], BIG))
                    ch.link(pool.memset(R[:, 0, :], BIG))
                    ch.link(pool.memset(R[:, 1:SLOTS + 1, 0:1], BIG))
                    ch.link(pool.memset(R[0:NB, 0, 0:1], 0.0))
                    ch.link(pool.memset(Wk[:, :, 0:1], 0.0))
                    ch.link(pool.memset(mk[:, :, :], 1.0))
                    ch.link(pool.memset(mk[:, :, 0:1], 0.0))
                    ch.link(pool.memset(Hpath[:, 0:1], 0.0))
                    pool.memset(Hpath[:, T:T + 1], float(S - 1)).then_inc(s_const, 1)

                @block.sync
                def _(sp):
                    sp.dma_start(X[:, :, :], x_rows).then_inc(s_x, 16)

                    def stream(it):
                        for k in range(CR):
                            n = it * CR + k
                            wait(sp, ctx_in[k], it * 16)
                            wait(sp, a_c_t, (n - CR + 1) * 2)
                            wait(sp, a_mm, n - CR + 1)
                            sp.dma_start(cr[:, k], ctx_tiles[:, bass.ds(n * PAIR, PAIR)]).then_inc(ctx_in[k], 16)

                    def weights():
                        def ld(dst, src):
                            sp.dma_start(dst, src, allow_slow_non_contiguous=True).then_inc(s_w, 16)
                            return 1
                        n = ld(w_in[:, :, :], W_in.rearrange("(c p) n -> p c n", p=P))
                        n += ld(w_out[:, :, :], W_out.rearrange("(c p) n -> p c n", p=P))
                        n += ld(b_1[:, 0:E], b1.rearrange("e h -> h e"))
                        n += ld(b_1[:, E:E + 1], bs1.rearrange("(h o) -> h o", o=1))
                        n += ld(b_2[0:E, :], b2)
                        n += ld(b_2[E:E + 1, :], bs2.rearrange("(o d) -> o d", o=1))
                        n += ld(w_gate[:, :, :], gate_W.rearrange("(c p) e -> p c e", p=P))
                        cwf = conv_w.rearrange("c o k -> c (o k)")
                        n += ld(cw[:, :, :], cwf[0:INNER, :].rearrange("(c p) k -> p c k", p=P))
                        n += ld(cb[:, :], conv_b[0:INNER].rearrange("(c p) -> p c", p=P))
                        n += ld(cw_bc[:, :, :], cwf[INNER:, :].rearrange("(c p) k -> p c k", p=NS))
                        n += ld(cb_bc[:, :], conv_b[INNER:].rearrange("(c p) -> p c", p=NS))
                        for h in range(2):
                            n += ld(d_ch[HD * h:HD * h + HD, :],
                                    D_param.rearrange("(c h) -> h c", h=2)[h:h + 1, :].broadcast_to([HD, CT]))
                        n += ld(nw[:, :], norm_w.rearrange("(c p) -> p c", p=P))
                        n += ld(a_exp[:, :], A_log.rearrange("(o h) -> o h", o=1).broadcast_to([P, HEADS]))
                        n += ld(dtb[:, :], dt_bias.rearrange("(o h) -> o h", o=1).broadcast_to([P, HEADS]))
                        n += ld(rsc[:, :], route_scale.rearrange("(o h) -> o h", o=1).broadcast_to([P, 1]))
                        return n

                    def store(n, par):
                        wait(sp, a_root, n + 1)
                        sp.dma_start(dist_rows[bass.ds(n * P, P), :], ds[:, par, :]).then_inc(dist_out[par], 16)

                    stream(0)
                    with sp.Fori(0, a_it - 1) as it:
                        for k in range(CR):
                            store(it * CR + k, k % 2)
                        stream(it + 1)
                    for k in range(CR):
                        store((a_it - 1) * CR + k, k % 2)
                    for par in range(2):
                        sp.wait_ge(dist_out[par], 16 * NT // 2)
                    sp.wait_ge(s_const, 1)
                    quarter = T // 4
                    for q in range(4):
                        for g in range(BLOCKS):
                            sp.dma_start(Dk[32 * g:32 * g + 32, CHUNK * g + quarter * q:CHUNK * g + quarter * q + quarter, :],
                                         dist[:, quarter * q:quarter * q + quarter, BI * g:BI * g + BI]
                                         ).then_inc(dist_in[q], 16)
                    assert weights() == N_W
                    with sp.Fori(0, CHUNKS) as c:
                        sp.wait_ge(b_step, c + 1)
                        for g in range(BLOCKS):
                            sp.dma_start(table[:, bass.ds((g * TABLE - g * CHUNK + c * CHUNK) * BI, CHUNK * BI)],
                                         dn_view[32 * g:32 * g + 32, bass.ds(c * (2 * CHUNK * BI), CHUNK * BI)]
                                         ).then_inc(s_table, 16)
                    sp.wait_ge(s_w, 16 * N_W)

                @block.vector
                def _(v):
                    ch = Chain(v, dve_done)
                    v.wait_ge(s_x, 16)
                    for t in range(NT):
                        v.bn_stats(bn_a[:, t, :], X[:, t, :]).then_inc(dve_done, 1)
                        ch.n += 1
                    v.wait_ge(dve_done, ch.n)
                    for t in range(NT - 1):
                        v.bn_aggr(mv_a[:, t, :], bn_a[:, t, :])
                    v.bn_aggr(mv_a[:, NT - 1, :], bn_a[:, NT - 1, :]).then_inc(a_norm, 1)
                    v.wait_ge(a_sd, 1)
                    ch.link(v.reciprocal(rs_a[:, :], sd_a[:, :]))

                    def tile(n, k, inside):
                        par = k % 2
                        wait(v, a_x_t, n - 1)
                        wait(v, a_sq, n - 1)
                        v.tensor_scalar(xn[:, par, :], X[:, bass.ds(n, 1), :].rearrange("p o d -> p (o d)"),
                                        mv_a[:, bass.ds(n, 1), 0:1].rearrange("p o d -> p (o d)"),
                                        rs_a[:, bass.ds(n, 1)], ALU.subtract, ALU.mult).then_inc(a_rows_t, 1)
                        v.wait_ge(ctx_in[k], inside * 16 + 16)
                        wait(v, a_mm, n - CR + 1)
                        wait(v, a_aa, n)
                        for b in range(PAIR):
                            for h in range(2):
                                ins = v.tensor_tensor_reduce(sqd[:, 2 * b + h, :], cr[:, k, b, h, :], cr[:, k, b, h, :], 1.0, 0.0,
                                                             ALU.mult, ALU.add, aa[:, k, b, h:h + 1])
                        ins.then_inc(a_aa, 1)
                        for b in range(PAIR):
                            v.wait_ge(a_c_t, n * 2 + b + 1)
                            if b == 0:
                                wait(v, a_mm, n - 1)
                            v.tensor_copy(ct_t[:, par, b].rearrange("p c i -> p (c i)"), bank[2 + b][:, :]).then_inc(a_c, 1)
                        v.wait_ge(a_mm, n + 1)
                        v.wait_ge(a_sq, n + 1)
                        wait(v, a_root, n - 1)
                        v.tensor_scalar(dd[:, par, :], bank[4 + par][:, 0:S], bb[:, bass.ds(n, 1)], 0.0,
                                        ALU.add, ALU.max).then_inc(a_clamp, 1)

                    for k in range(CR):
                        tile(k, k, 0)
                    with v.Fori(1, a_it) as it:
                        for k in range(CR):
                            tile(it * CR + k, k, it)

                    v.wait_ge(s_const, 1)
                    def chunk(c):
                        for u in range(CHUNK):
                            s = c * CHUNK + u
                            old = R[:, bass.ds(s, 1), :].rearrange("p o i -> p (o i)")
                            new = R[:, bass.ds(s + 1, 1), :].rearrange("p o i -> p (o i)")
                            ch.link(v.tensor_tensor(m1[:, :], old[:, 0:BI], old[:, 1:BI + 1], ALU.min))
                            ch.link(v.tensor_tensor_scan(new[:, 1:BI + 1], m1[:, :],
                                                         Dk[:, bass.ds(s, 1), :].rearrange("p o i -> p (o i)"),
                                                         new[:, 0:1], ALU.min, ALU.add))
                        left = R[:, bass.ds(c * CHUNK, CHUNK), 1:BI + 1]
                        diag = R[:, bass.ds(c * CHUNK, CHUNK), 0:BI]
                        up = R[:, bass.ds(c * CHUNK + 1, CHUNK), 0:BI]
                        v.tensor_tensor(qk[:, :, :], up, left, ALU.is_gt).then_inc(dve_done, 1)
                        v.tensor_tensor(ak[:, :, :], diag, left, ALU.is_le).then_inc(dve_done, 1)
                        v.tensor_tensor(rk[:, :, :], up, diag, ALU.is_ge).then_inc(dve_done, 1)
                        ch.n += 3
                        v.wait_ge(dve_done, ch.base + ch.n)
                        v.tensor_tensor(qk[:, :, :], qk[:, :, :], rk[:, :, :], ALU.max).then_inc(dve_done, 1)
                        ch.n += 1
                        ch.link(v.scalar_tensor_tensor(ak[:, :, :], ak[:, :, :], -0.5, blk_id[:, :, :], ALU.mult, ALU.add))
                        ch.link(v.tensor_tensor(Wk[:, :, 1:BI + 1], qk[:, :, :], ak[:, :, :], ALU.mult))
                        ch.link(v.tensor_tensor_scan(Nk[:, :, :].rearrange("p c i -> p (c i)"),
                                                     mk[:, :, :].rearrange("p c i -> p (c i)"),
                                                     Wk[:, :, :].rearrange("p c i -> p (c i)"), 0.0, ALU.mult, ALU.max))
                        dst = dn_view[:, bass.ds(c * (2 * CHUNK * BI), CHUNK * BI)].rearrange("p (c i) -> p c i", i=BI)
                        v.tensor_tensor(dst, Nk[:, :, 1:BI + 1], Nk[:, :, 0:BI], ALU.subtract).then_inc(b_step, 1)

                    def exchange(c):
                        for g in range(BLOCKS - 1):
                            a, b = slice(32 * g, 32 * g + 32), slice(32 * g + 32, 32 * g + 64)
                            v.tensor_copy(R[b, bass.ds((c + 1) * CHUNK + 1, CHUNK), 0:1],
                                          R[a, bass.ds(c * CHUNK + 1, CHUNK), BI:BI + 1])
                            ins = v.tensor_copy(Wk[b, :, 0:1], Nk[a, :, BI:BI + 1])
                        ch.link(ins)

                    per = 2 * CHUNK + 7 + 1
                    lots = [(0, 4), (4, 8), (8, 12), (12, CHUNKS - 1)]
                    for q, (lo, hi) in enumerate(lots):
                        v.wait_ge(dist_in[q], 16 * BLOCKS)
                        with v.Fori(lo, hi) as c:
                            ch.enter(c - lo, per)
                            chunk(c)
                            exchange(c)
                            ch.leave(hi - lo)
                    chunk(CHUNKS - 1)

                    v.wait_ge(s_table, 16 * BLOCKS * CHUNKS)
                    with v.Fori(0, T - 1) as r:
                        ch.enter(r, 1)
                        j = (T - 1) - r
                        ins = v.scalar_tensor_tensor(junk[:, :, :], lookup_id[:, :].rearrange("b (g i) -> b g i", g=BLOCKS),
                                                     Hpath[:, bass.ds(j + 1, 1)],
                                                     tab[:, :, bass.ds(j, 1), :].rearrange("b g o i -> b g (o i)"),
                                                     ALU.is_le, ALU.mult, accum_out=Hpath[:, bass.ds(j, 1)])
                        ch.link(ins)
                        ch.leave(T - 1)
                    v.tensor_tensor(Hd[:, :, :],
                                    Hpath[:, :].rearrange("b (o j) -> b o j", o=1).broadcast_to([NB, NB, T + 1]),
                                    ident[0:NB, 0:NB].rearrange("b (c o) -> b c o", o=1).broadcast_to([NB, NB, T + 1]),
                                    ALU.mult).then_inc(s_path, 1)
                    v.wait_ge(s_w, 16 * N_W)
                    for w in (cw[:, :, :], cb[:, :], cw_bc[:, :, :], cb_bc[:, :]):
                        v.tensor_scalar(w, w, 0.5, None, ALU.mult)
                    for c in range(CT):
                        v.tensor_scalar(w_out[:, c, :], w_out[:, c, :], nw[:, c:c + 1], None, ALU.mult)

                @block.scalar
                def _(act):
                    act.wait_ge(a_norm, 1)
                    act.wait_ge(s_const, 1)
                    act.activation(sd_a[:, :], mv_a[:, :, 1], ACT.Sqrt, bias=eps1[:, :]).then_inc(a_sd, 1)

                    def tile(n, k, inside):
                        par = k % 2
                        act.wait_ge(a_rows_t, n + 1)
                        wait(act, a_sq, n)
                        act.activation(sq[:, :], xn[:, par, :], ACT.Square, accum_out=bb[:, bass.ds(n, 1)]).then_inc(a_sq, 1)
                        act.wait_ge(a_x_t, n + 1)
                        wait(act, a_mm, n - 1)
                        act.activation(xt[:, par].rearrange("p c i -> p (c i)"), bank[par][:, 0:KC * P], ACT.Copy,
                                       scale=-2.0).then_inc(act_done, 1)
                        act.wait_ge(a_clamp, n + 1)
                        wait(act, dist_out[par], (inside * (CR // 2) + k // 2) * 16)
                        act.activation(ds[:, par, :], dd[:, par, :], ACT.Sqrt).then_inc(a_root, 1)

                    for k in range(CR):
                        tile(k, k, 0)
                    with act.Fori(1, a_it) as it:
                        for k in range(CR):
                            tile(it * CR + k, k, it)
                    act.wait_ge(s_w, 16 * N_W)
                    act.activation(a_exp[:, :], a_exp[:, :], ACT.Exp)

                @block.tensor
                def _(pe):
                    pe.wait_ge(s_const, 1)

                    def tile(n, k, inside):
                        par = k % 2
                        pe.wait_ge(a_rows_t, n + 1)
                        wait(pe, act_done, n - 1)
                        for c in range(KC):
                            mm = pe.transpose(bank[par][:, P * c:P * c + P], xn[:, par, P * c:P * c + P], ident[:, :])
                        mm.then_inc(a_x_t, 1)
                        pe.wait_ge(ctx_in[k], inside * 16 + 16)
                        for b in range(PAIR):
                            wait(pe, a_c, n * 2 - 2 + b + 1)
                            for c in range(KC):
                                for h in range(2):
                                    mm = pe.transpose(bank[2 + b][:, S * c + P * h:S * c + P * h + P],
                                                      cr[:, k, b, h, P * c:P * c + P], ident[:, :])
                            mm.then_inc(a_c_t, 1)
                        pe.wait_ge(act_done, n + 1)
                        pe.wait_ge(a_aa, n + 1)
                        wait(pe, a_clamp, n - 1)
                        for b in range(PAIR):
                            pe.wait_ge(a_c, n * 2 + b + 1)
                            q = slice(T * b, T * b + T)
                            for c in range(KC):
                                pe.matmul(bank[4 + par][q, 0:S], lhsT=xt[:, par, c, q], rhs=ct_t[:, par, b, c, :],
                                          start=(c == 0), stop=False)
                            for h in range(2):
                                mm = pe.matmul(bank[4 + par][q, P * h:P * h + P],
                                               lhsT=aa[:, k, b, h:h + 1].broadcast_to([P, T]), rhs=ident[:, :],
                                               start=False, stop=(h == 1))
                        mm.then_inc(a_mm, 1)

                    for k in range(CR):
                        tile(k, k, 0)
                    with pe.Fori(1, a_it) as it:
                        for k in range(CR):
                            tile(it * CR + k, k, it)

        def buf(name, shape, dt=F32):
            return sb("d_" + name, shape, dt)

        w_1 = sb("w_1", [P, KC, E + 1, H])
        w_2 = sb("w_2", [P, E + 1, D])
        U = buf("U", [P, 2, GN])
        mask = buf("mask", [P, 2, GB, T])
        xg = buf("xg", [P, GT, D])
        XT = buf("XT", [P, KC, GN])
        dtv = buf("dtv", [P, GT, HEADS])
        dtn = buf("dtn", [P, GT, HEADS])
        dtu = buf("dtu", [P, GT, HEADS])
        dtl = buf("dtl", [P, GT, HEADS])
        dte = buf("dte", [P, GT, HEADS])
        dtd = buf("dtd", [P, GT, HEADS])
        dt_ = buf("dt", [P, GT, HEADS])
        da = buf("da", [P, GT, HEADS])
        bc_raw = buf("bc_raw", [NS, 2, GB, T + PAD])
        bc_acc = buf("bc_acc", [NS, 2, GB, T])
        bc_th = buf("bc_th", [NS, 2, GB, T])
        BC = buf("BC", [NS, 2, GB, T])
        G = buf("G", [P, GT, T])
        raw = buf("raw", [P, 2, GB, T + PAD])
        acc = buf("acc", [P, 2, GB, T])
        th = buf("th", [P, 2, GN])
        xc = buf("xc", [P, RING, GN])
        zth = buf("zth", [P, 2, GN])
        zs = buf("zs", [P, RING, GN])
        xd = buf("xd", [P, 2, GT, 2, HD])
        steps = buf("steps", [P, 2, GT, 2, T])
        decay = buf("decay", [P, 2, GT, 2, T])
        M = buf("M", [P, 2, GT, 2, T])
        y1 = buf("y1", [P, 2, GN])
        yg = buf("yg", [P, 2, GN])
        ysq = U
        accq = buf("accq", [P, GN])
        e_g = buf("e_g", [P, GT, E])
        sc = buf("sc", [P, GT, E])
        cmp_ = buf("cmp", [P, GT, E, E])
        cmp2 = buf("cmp2", [P, GT, E, E])
        cnt = buf("cnt", [P, GT, E])
        tot = buf("tot", [P, GT])
        gate = buf("gate", [P, GT, E + 1])
        gT = bc_th[0:E + 1, 0].rearrange("p q t -> p (q t)")
        hh = mask[:, :, :, :].rearrange("p h b t -> p h (b t)")

        names = ("d_const pads spread mask_ready expanded ln_var ln_sd ln_rows ln_t ln_xt_a ln_xt_v dt_logit dt_neg dt_ln "
                 "dt_ready bc_proj bc_in bc_conv bc_tanh bc_ready g_mm g_ready x_proj z_proj x_acc conv_done th_done "
                 "xc_done zth_done zs_done x_t xd_done r_done seg e_done m_done y_mm y_done yg_done sq_done accq_done "
                 "o_mm ssq r_sd logits sig gate_ready gate_t gt_ready h_mm h_done f_mm f_acc d_chain out_done act_link").split()
        sm = {n: sem("d_" + n) for n in names}
        AL = "p (q t) -> p q t"
        SHARE = E
        order = [SHARE] + list(range(E))
        PER_F = 2 + GT * E
        x_ch = lambda c: INNER + P * c
        z_ch = lambda c: P * c

        with nc.Block() as block:
            @block.sync
            def _(sp):
                for k in range(CR):
                    sp.dma_start(cr[:, k], ctx_tiles[:, PAIR * k:PAIR * k + PAIR]).then_inc(ctx_in[k], 16)
                for c in range(KC):
                    sp.dma_start(w_1[:, c, 0:E, :], W1[:, P * c:P * c + P, :].rearrange("e p h -> p e h")).then_inc(s_we, 16)
                    sp.dma_start(w_1[:, c, E, :], Ws1[P * c:P * c + P, :]).then_inc(s_we, 16)
                sp.dma_start(w_2[:, 0:E, :], W2.rearrange("e h d -> h e d")).then_inc(s_we, 16)
                sp.dma_start(w_2[:, E, :], Ws2).then_inc(s_we, 16)
                with sp.Fori(0, NG - 1) as g:
                    for k in range(CR):
                        sp.wait_ge(sm["expanded"], g * GT + k + 1)
                        sp.dma_start(cr[:, k], ctx_tiles[:, bass.ds(((g + 1) * GT + k) * PAIR, PAIR)]).then_inc(ctx_in[k], 16)
                    sp.wait_ge(sm["f_acc"], (g + 1) * PER_F + 1)
                    sp.dma_start(out_rows[:, bass.ds(g * GT, GT), :], X[:, bass.ds(g * GT, GT), :]).then_inc(sm["out_done"], 16)
                sp.wait_ge(sm["f_acc"], NG * PER_F + 1)
                sp.dma_start(out_rows[:, NT - GT:NT, :], X[:, NT - GT:NT, :]).then_inc(sm["out_done"], 16)
                sp.wait_ge(sm["out_done"], 16 * NG)

            @block.tensor
            def _(pe):
                pe.wait_ge(s_path, 1)
                pe.wait_ge(sm["d_const"], 1)

                def ln_transpose(g, u):
                    for t in range(GT):
                        pe.wait_ge(sm["ln_rows"], (g * 2 + u) * GT + t + 1)
                        for c in range(KC):
                            mm = pe.transpose((p_x, p_z)[c][:, P * t:P * t + P], xg[:, t, P * c:P * c + P], ident[:, :])
                    mm.then_inc(sm["ln_t"], 1)

                with pe.Fori(0, NG) as g:
                    pe.wait_ge(sm["f_acc"], g * PER_F + 1)
                    pe.matmul(p_t[:, :], lhsT=ones16[:, :], rhs=Hd[:, bass.ds(g * GB, GB), 1:T + 1], start=True, stop=True)
                    pe.matmul(p_s[:, :], lhsT=ones16[:, :], rhs=Hd[:, bass.ds(g * GB, GB), 0:T], start=True,
                              stop=True).then_inc(sm["spread"], 1)
                    pe.wait_ge(sm["mask_ready"], g + 1)
                    for t in range(GT):
                        pe.wait_ge(ctx_in[t], 16 * (NT // CR) + g * 16 + 16)
                        for b in range(PAIR):
                            for h in range(2):
                                mm = pe.matmul((p_x, p_z, p_y0, p_y1)[t][T * b:T * b + T, 0:D],
                                               lhsT=mask[:, h, PAIR * t + b, :], rhs=cr[:, t, b, h, :],
                                               start=(h == 0), stop=(h == 1))
                        mm.then_inc(sm["expanded"], 1)
                    ln_transpose(g, 0)
                    pe.wait_ge(sm["ln_xt_a"], g * 2 + 1)
                    pe.wait_ge(sm["ln_xt_v"], g * 2 + 1)
                    for t in range(GT):
                        for c in range(KC):
                            mm = pe.matmul(p_t[:, HEADS * t:HEADS * t + HEADS], lhsT=XT[:, c, P * t:P * t + P],
                                           rhs=w_in[:, c, PROJ - HEADS:PROJ], start=(c == 0), stop=(c == KC - 1))
                    mm.then_inc(sm["dt_logit"], 1)
                    for j in range(2):
                        o = 2 * INNER + NS * j
                        for c in range(KC):
                            mm = pe.matmul((p_y0, p_y1)[j][0:NS, :], lhsT=w_in[:, c, o:o + NS], rhs=XT[:, c, :],
                                           start=(c == 0), stop=(c == KC - 1))
                        mm.then_inc(sm["bc_proj"], 1)

                    def project(c):
                        if c >= 1:
                            pe.wait_ge(sm["x_acc"], g * CT + c)
                        for k in range(KC):
                            mm = pe.matmul(p_x[:, :], lhsT=w_in[:, k, x_ch(c):x_ch(c) + P], rhs=XT[:, k, :],
                                           start=(k == 0), stop=(k == KC - 1))
                        mm.then_inc(sm["x_proj"], 1)
                        if c >= 1:
                            pe.wait_ge(sm["zs_done"], g * CT + c)
                        for k in range(KC):
                            mm = pe.matmul(p_z[:, :], lhsT=w_in[:, k, z_ch(c):z_ch(c) + P], rhs=XT[:, k, :],
                                           start=(k == 0), stop=(k == KC - 1))
                        mm.then_inc(sm["z_proj"], 1)

                    def segments(c):
                        pe.wait_ge(sm["r_done"], g * CT + c + 1)
                        if c >= 1:
                            pe.wait_ge(sm["e_done"], g * CT + c)
                        pe.matmul(p_s[:, :], lhsT=later[:, :], rhs=steps[:, c % 2].rearrange("p q h t -> p (q h t)"),
                                  start=True, stop=True).then_inc(sm["seg"], 1)

                    def turn(c):
                        pe.wait_ge(sm["xc_done"], g * CT + c + 1)
                        if c >= 1:
                            pe.wait_ge(sm["xd_done"], g * CT + c)
                        for t in range(GT):
                            mm = pe.transpose(p_t[:, P * t:P * t + P], xc[:, c % RING, P * t:P * t + P], ident[:, :])
                        mm.then_inc(sm["x_t"], 1)

                    def mix(c):
                        pe.wait_ge(sm["xd_done"], g * CT + c + 1)
                        pe.wait_ge(sm["m_done"], g * CT + c + 1)
                        if c >= 1:
                            pe.wait_ge(sm["y_done"], g * CT + c)
                        carrier(pe, p_y0)
                        for t in range(GT):
                            for b in range(PAIR):
                                q = slice(T * b, T * b + T)
                                for h in range(2):
                                    mm = pe.matmul((p_y0, p_y1)[b][HD * h:HD * h + HD, T * t:T * t + T],
                                                   lhsT=xd[q, c % 2, t, h, :], rhs=M[q, c % 2, t, h, :],
                                                   start=True, stop=True)
                        mm.then_inc(sm["y_mm"], 1)

                    def output(c):
                        pe.wait_ge(sm["yg_done"], g * CT + c + 1)
                        for t in range(GT):
                            mm = pe.matmul((p_o0, p_o1)[t // 2][:, D * (t % 2):D * (t % 2) + D],
                                           lhsT=yg[:, c % 2, P * t:P * t + P], rhs=w_out[:, c, :],
                                           start=(c == 0 and t % 2 == 0), stop=(c == CT - 1), skip_group_check=True)
                        mm.then_inc(sm["o_mm"], 1)

                    for b in range(GB):
                        if b == 0:
                            pe.wait_ge(sm["bc_ready"], g * 2 + 2)
                            pe.wait_ge(sm["dt_ready"], g + 1)
                            carrier(pe, p_s)
                        mm = pe.matmul(p_s[T * (b % 2):T * (b % 2) + T, T * (b // 2):T * (b // 2) + T],
                                       lhsT=BC[:, 0, b, :], rhs=BC[:, 1, b, :], start=True, stop=True)
                    mm.then_inc(sm["g_mm"], 1)
                    pe.wait_ge(sm["g_ready"], g + 1)
                    for k in range(CT + 3):
                        if k < CT:
                            project(k)
                            segments(k)
                        if 1 <= k <= CT:
                            turn(k - 1)
                        if 2 <= k <= CT + 1:
                            mix(k - 2)
                        if k >= 3:
                            output(k - 3)
                    pe.wait_ge(sm["accq_done"], g * CT + CT)
                    for t in range(GT):
                        mm = pe.matmul(p_t[:, t:t + 1], lhsT=accq[:, P * t:P * t + P], rhs=ones[:, :], start=True, stop=True)
                    mm.then_inc(sm["ssq"], 1)

                    ln_transpose(g, 1)
                    pe.wait_ge(sm["ln_xt_a"], g * 2 + 2)
                    pe.wait_ge(sm["ln_xt_v"], g * 2 + 2)
                    for t in range(GT):
                        for c in range(KC):
                            mm = pe.matmul(p_t[:, E * t:E * t + E], lhsT=XT[:, c, P * t:P * t + P], rhs=w_gate[:, c, :],
                                           start=(c == 0), stop=(c == KC - 1))
                    mm.then_inc(sm["logits"], 1)

                    def hidden(n):
                        e = order[n]
                        if n >= 2:
                            pe.wait_ge(sm["h_done"], g * (E + 1) + n - 1)
                        for c in range(KC):
                            mm = pe.matmul((p_x, p_z)[n % 2][:, :], lhsT=w_1[:, c, e, :], rhs=XT[:, c, :],
                                           start=(c == 0), stop=(c == KC - 1))
                        mm.then_inc(sm["h_mm"], 1)

                    def down(n):
                        e = order[n]
                        pe.wait_ge(sm["h_done"], g * (E + 1) + n + 1)
                        if n >= 2:
                            pe.wait_ge(sm["f_acc"], g * PER_F + 2 + GT * (n - 2) + 1)
                        if n == 0:
                            pe.wait_ge(sm["gt_ready"], g + 1)
                        for t in range(GT):
                            o = ((p_y0, p_y1), (p_o0, p_o1))[n % 2][t // 2][:, D * (t % 2):D * (t % 2) + D]
                            mm = pe.matmul(o, lhsT=hh[:, n % 2, P * t:P * t + P], rhs=w_2[:, e, :], start=True, stop=(n > 0))
                            if n == 0:
                                mm = pe.matmul(o, lhsT=gT[:, P * t:P * t + P], rhs=b_2[:, :], start=False, stop=True)
                        mm.then_inc(sm["f_mm"], 1)

                    pe.wait_ge(s_we, 16 * (2 * KC + 2))
                    hidden(0)
                    hidden(1)
                    pe.wait_ge(sm["gate_ready"], g + 1)
                    for t in range(GT):
                        mm = pe.transpose(p_s[0:E + 1, P * t:P * t + P], gate[:, t, :], ident[:, :])
                    mm.then_inc(sm["gate_t"], 1)
                    for n in range(E + 1):
                        down(n)
                        if n + 2 < E + 1:
                            hidden(n + 2)

            @block.scalar
            def _(act):
                act.wait_ge(sm["d_const"], 1)

                def ln_act(g, u):
                    act.wait_ge(sm["ln_var"], g * 2 + u + 1)
                    act.activation(sd[:, :], mv[:, :, 1], ACT.Sqrt, bias=eps1[:, :]).then_inc(sm["ln_sd"], 1)
                    act.wait_ge(sm["ln_t"], g * 2 + u + 1)
                    act.activation(XT[:, 0, :], p_x[:, :], ACT.Copy).then_inc(sm["ln_xt_a"], 1)

                with act.Fori(0, NG) as g:
                    act.wait_ge(sm["f_acc"], g * PER_F + 1)
                    ln_act(g, 0)
                    act.wait_ge(sm["dt_neg"], g + 1)
                    act.activation(dtu[:, :, :], dtn[:, :, :], ACT.Exp).then_inc(sm["act_link"], 1)
                    act.wait_ge(sm["act_link"], g + 1)
                    act.activation(dtl[:, :, :], dtu[:, :, :], ACT.Ln, bias=ones[:, :]).then_inc(sm["dt_ln"], 1)
                    for j in range(2):
                        act.wait_ge(sm["bc_proj"], g * 2 + j + 1)
                        pj = (p_y0, p_y1)[j][0:NS, :].rearrange(AL, t=T)
                        act.activation(bc_raw[:, j, :, PAD:], pj, ACT.Copy)
                        act.activation(bc_acc[:, j], pj, ACT.Identity, bias=cb_bc[:, j:j + 1],
                                       scale=cw_bc[:, j, PAD:TAPS]).then_inc(sm["bc_in"], 1)
                    for j in range(2):
                        act.wait_ge(sm["bc_conv"], g * 2 + j + 1)
                        act.activation(bc_th[:, j], bc_acc[:, j], ACT.Tanh).then_inc(sm["bc_tanh"], 1)

                    def take_x(c):
                        act.wait_ge(sm["x_proj"], g * CT + c + 1)
                        if c >= 2:
                            act.wait_ge(sm["conv_done"], g * CT + c - 1)
                        if c >= 2:
                            act.wait_ge(sm["xc_done"], g * CT + c - 1)
                        px = p_x[:, :].rearrange(AL, t=T)
                        act.activation(raw[:, c % 2, :, PAD:], px, ACT.Copy)
                        act.activation(acc[:, c % 2], px, ACT.Identity, bias=cb[:, c:c + 1],
                                       scale=cw[:, c, PAD:TAPS]).then_inc(sm["x_acc"], 1)

                    def tanh_z(c):
                        act.wait_ge(sm["z_proj"], g * CT + c + 1)
                        if c >= 2:
                            act.wait_ge(sm["zs_done"], g * CT + c - 1)
                        act.activation(zth[:, c % 2], p_z[:, :], ACT.Tanh, scale=0.5).then_inc(sm["zth_done"], 1)

                    def decays(c):
                        act.wait_ge(sm["seg"], g * CT + c + 1)
                        if c >= 2:
                            act.wait_ge(sm["m_done"], g * CT + c - 1)
                        act.activation(decay[:, c % 2].rearrange("p q h t -> p (q h t)"), p_s[:, :],
                                       ACT.Exp).then_inc(sm["e_done"], 1)

                    def tanh_x(c):
                        act.wait_ge(sm["conv_done"], g * CT + c + 1)
                        if c >= 2:
                            act.wait_ge(sm["xc_done"], g * CT + c - 1)
                        act.activation(th[:, c % 2].rearrange(AL, t=T), acc[:, c % 2], ACT.Tanh).then_inc(sm["th_done"], 1)

                    def square(c):
                        act.wait_ge(sm["yg_done"], g * CT + c + 1)
                        if c >= 2:
                            act.wait_ge(sm["accq_done"], g * CT + c - 1)
                        act.activation(ysq[:, c % 2], yg[:, c % 2], ACT.Square).then_inc(sm["sq_done"], 1)

                    for k in range(CT + 3):
                        if k < CT:
                            take_x(k)
                            tanh_z(k)
                            decays(k)
                            tanh_x(k)
                        if k >= 3:
                            square(k - 3)
                    act.wait_ge(sm["ssq"], g + 1)
                    act.activation(sd[:, :], p_t[:, 0:GT], ACT.Sqrt, bias=eps4[:, :], scale=1.0 / INNER).then_inc(sm["r_sd"], 1)

                    ln_act(g, 1)
                    act.wait_ge(sm["logits"], g + 1)
                    act.activation(e_g[:, :, :], p_t[:, 0:GT * E].rearrange("p (q e) -> p q e", e=E), ACT.Exp,
                                   scale=-1.0).then_inc(sm["sig"], 1)
                    for n in range(E + 1):
                        act.wait_ge(sm["h_mm"], g * (E + 1) + n + 1)
                        if n >= 2:
                            act.wait_ge(sm["f_mm"], g * (E + 1) + n - 1)
                        act.activation(hh[:, n % 2], (p_x, p_z)[n % 2][:, :], ACT.Gelu,
                                       bias=b_1[:, order[n]:order[n] + 1]).then_inc(sm["h_done"], 1)

            @block.gpsimd
            def _(pool):
                pool.memset(bc_raw[:, :, :, 0:PAD], 0.0).then_inc(sm["pads"], 1)
                pool.wait_ge(sm["pads"], 1)
                pool.memset(raw[:, :, :, 0:PAD], 0.0)
                pool.memset(gate[:, :, E:E + 1], 1.0).then_inc(sm["d_const"], 1)
                with pool.Fori(0, NG) as g:
                    pool.wait_ge(sm["dt_ready"], g + 1)

                    def make_steps(c):
                        if c >= 2:
                            pool.wait_ge(sm["seg"], g * CT + c - 1)
                        pool.tensor_tensor(steps[:, c % 2],
                                           da[:, :, 2 * c:2 * c + 2].rearrange("p q (h o) -> p q h o", o=1).broadcast_to([P, GT, 2, T]),
                                           tri[:, :].rearrange("p (a b t) -> p a b t", a=1, b=1).broadcast_to([P, GT, 2, T]),
                                           ALU.mult).then_inc(sm["r_done"], 1)

                    def make_mix(c):
                        pool.wait_ge(sm["e_done"], g * CT + c + 1)
                        if c == 0:
                            pool.wait_ge(sm["g_ready"], g + 1)
                        if c >= 2:
                            pool.wait_ge(sm["y_mm"], g * CT + c - 1)
                        pool.tensor_tensor(M[:, c % 2], decay[:, c % 2],
                                           G[:, :, :].rearrange("p q (o t) -> p q o t", o=1).broadcast_to([P, GT, 2, T]),
                                           ALU.mult).then_inc(sm["m_done"], 1)

                    def gate_y(c):
                        pool.wait_ge(sm["y_done"], g * CT + c + 1)
                        if c >= 2:
                            pool.wait_ge(sm["o_mm"], g * CT + c - 1)
                            pool.wait_ge(sm["sq_done"], g * CT + c - 1)
                        pool.tensor_tensor(yg[:, c % 2], y1[:, c % 2], zs[:, c % RING], ALU.mult).then_inc(sm["yg_done"], 1)

                    def sum_squares(c):
                        pool.wait_ge(sm["sq_done"], g * CT + c + 1)
                        if c == 0:
                            pool.tensor_tensor(accq[:, :], ysq[:, 0], zero[:, :].broadcast_to([P, GN]), ALU.add).then_inc(sm["accq_done"], 1)
                        else:
                            pool.wait_ge(sm["accq_done"], g * CT + c)
                            pool.tensor_tensor(accq[:, :], accq[:, :], ysq[:, c % 2], ALU.add).then_inc(sm["accq_done"], 1)

                    make_steps(0)
                    for k in range(CT + 3):
                        if k + 1 < CT:
                            make_steps(k + 1)
                        if k < CT:
                            make_mix(k)
                        if 2 <= k <= CT + 1:
                            gate_y(k - 2)
                        if k >= 3:
                            sum_squares(k - 3)

            @block.vector
            def _(v):
                ch = Chain(v, sm["d_chain"])
                v.memset(spare[:, :], 0.0).then_inc(sm["f_acc"], 1)
                v.wait_ge(sm["f_acc"], 1)
                v.wait_ge(sm["d_const"], 1)

                with v.Fori(0, NG) as g:
                    ch.enter(g, CHAIN_D)

                    def xtile(t):
                        return X[:, bass.ds(g * GT + t, 1), :].rearrange("p o d -> p (o d)")

                    def ln(u):
                        for t in range(GT):
                            ins = v.bn_stats(bn[:, t, :], xtile(t))
                        ch.link(ins, bare=True)
                        for t in range(GT):
                            ins = v.bn_aggr(mv[:, t, :], bn[:, t, :])
                        ins.then_inc(sm["ln_var"], 1)
                        v.wait_ge(sm["ln_sd"], g * 2 + u + 1)
                        ch.link(v.reciprocal(rs[:, :], sd[:, :]))
                        for t in range(GT):
                            v.tensor_scalar(xg[:, t, :], xtile(t), mv[:, t, 0:1], rs[:, t:t + 1], ALU.subtract,
                                            ALU.mult).then_inc(sm["ln_rows"], 1)
                        v.wait_ge(sm["ln_t"], g * 2 + u + 1)
                        v.tensor_copy(XT[:, 1, :], p_z[:, :]).then_inc(sm["ln_xt_v"], 1)

                    v.wait_ge(sm["spread"], g + 1)
                    for h in range(2):
                        ins = v.tensor_scalar(U[:, h, :], p_t[:, :], row_id[:, h:h + 1], None, ALU.is_ge)
                    ch.link(ins)
                    for h in range(2):
                        ins = v.scalar_tensor_tensor(mask[:, h].rearrange("p b t -> p (b t)"), p_s[:, :], row_id[:, h:h + 1],
                                                     U[:, h, :], ALU.is_le, ALU.mult)
                    ins.then_inc(sm["mask_ready"], 1)
                    for t in range(GT):
                        v.wait_ge(sm["expanded"], g * GT + t + 1)
                        ins = v.tensor_tensor(xtile(t), xtile(t), (p_x, p_z, p_y0, p_y1)[t][:, 0:D], ALU.add)
                    ch.link(ins, bare=True)
                    ln(0)

                    v.wait_ge(sm["dt_logit"], g + 1)
                    ch.link(v.tensor_tensor(dtv[:, :, :], p_t[:, 0:GT * HEADS].rearrange("p (q h) -> p q h", h=HEADS),
                                            dtb[:, :].rearrange("p (o h) -> p o h", o=1).broadcast_to([P, GT, HEADS]), ALU.add))
                    v.scalar_tensor_tensor(dtn[:, :, :], dtv[:, :, :], -1.0, dtv[:, :, :], ALU.mult,
                                           ALU.min).then_inc(sm["dt_neg"], 1)
                    v.wait_ge(sm["dt_ln"], g + 1)
                    ch.link(v.tensor_scalar(dtd[:, :, :], dtu[:, :, :], 1.0, -1.0, ALU.add, ALU.add))
                    ch.link(v.tensor_scalar(dte[:, :, :], dtd[:, :, :], 0.0, None, ALU.is_equal))
                    ch.link(v.tensor_tensor(dtd[:, :, :], dtd[:, :, :], dte[:, :, :], ALU.add))
                    ch.link(v.tensor_tensor(dtl[:, :, :], dtl[:, :, :], dte[:, :, :], ALU.add))
                    ch.link(v.reciprocal(dtd[:, :, :], dtd[:, :, :]))
                    ch.link(v.tensor_tensor(dtl[:, :, :], dtl[:, :, :], dtu[:, :, :], ALU.mult))
                    ch.link(v.tensor_tensor(dtl[:, :, :], dtl[:, :, :], dtd[:, :, :], ALU.mult))
                    ch.link(v.scalar_tensor_tensor(dt_[:, :, :], dtv[:, :, :], 0.0, dtl[:, :, :], ALU.max, ALU.add))
                    v.scalar_tensor_tensor(da[:, :, :], dt_[:, :, :], -1.0,
                                           a_exp[:, :].rearrange("p (o h) -> p o h", o=1).broadcast_to([P, GT, HEADS]),
                                           ALU.mult, ALU.mult).then_inc(sm["dt_ready"], 1)

                    for j in range(2):
                        v.wait_ge(sm["bc_in"], g * 2 + j + 1)
                        for k in range(PAD - 1, -1, -1):
                            ins = v.scalar_tensor_tensor(bc_acc[:, j], bc_raw[:, j, :, k:k + T], cw_bc[:, j, k:k + 1],
                                                         bc_acc[:, j], ALU.mult, ALU.add)
                            if k:
                                ch.link(ins)
                        ins.then_inc(sm["bc_conv"], 1)
                    for j in range(2):
                        v.wait_ge(sm["bc_tanh"], g * 2 + j + 1)
                        v.scalar_tensor_tensor(BC[:, j], bc_th[:, j], 1.0, bc_acc[:, j], ALU.add,
                                               ALU.mult).then_inc(sm["bc_ready"], 1)
                    v.wait_ge(sm["g_mm"], g + 1)
                    v.tensor_tensor(G[:, :, :], p_s[:, 0:GT * T].rearrange("p (q t) -> p q t", t=T),
                                    tri[:, :].rearrange("p (o t) -> p o t", o=1).broadcast_to([P, GT, T]),
                                    ALU.mult).then_inc(sm["g_ready"], 1)

                    def conv(c):
                        v.wait_ge(sm["x_acc"], g * CT + c + 1)
                        for k in range(PAD - 1, -1, -1):
                            a = acc[:, c % 2]
                            ins = v.scalar_tensor_tensor(a, raw[:, c % 2, :, k:k + T], cw[:, c, k:k + 1], a, ALU.mult, ALU.add)
                            if k:
                                ch.link(ins)
                        ins.then_inc(sm["conv_done"], 1)

                    def silu_z(c):
                        v.wait_ge(sm["zth_done"], g * CT + c + 1)
                        if c >= RING:
                            v.wait_ge(sm["yg_done"], g * CT + c - RING + 1)
                        v.scalar_tensor_tensor(zs[:, c % RING], zth[:, c % 2], 1.0, p_z[:, :], ALU.add,
                                               ALU.mult).then_inc(sm["zs_done"], 1)

                    def silu_x(c):
                        v.wait_ge(sm["th_done"], g * CT + c + 1)
                        if c >= RING:
                            v.wait_ge(sm["x_t"], g * CT + c - RING + 1)
                        v.scalar_tensor_tensor(xc[:, c % RING].rearrange(AL, t=T), th[:, c % 2].rearrange(AL, t=T), 1.0,
                                               acc[:, c % 2], ALU.add, ALU.mult).then_inc(sm["xc_done"], 1)

                    def scale_x(c):
                        v.wait_ge(sm["x_t"], g * CT + c + 1)
                        if c >= 2:
                            v.wait_ge(sm["y_mm"], g * CT + c - 1)
                        v.tensor_tensor(xd[:, c % 2], p_t[:, :].rearrange("p (q h d) -> p q h d", q=GT, h=2),
                                        dt_[:, :, 2 * c:2 * c + 2].rearrange("p q (h o) -> p q h o", o=1).broadcast_to([P, GT, 2, HD]),
                                        ALU.mult).then_inc(sm["xd_done"], 1)

                    def skip_x(c):
                        v.wait_ge(sm["y_mm"], g * CT + c + 1)
                        if c >= 2:
                            v.wait_ge(sm["yg_done"], g * CT + c - 1)
                        for b in range(PAIR):
                            xv = xc[:, c % RING].rearrange("p (q b t) -> p q b t", q=GT, b=PAIR)[:, :, b, :]
                            yv = y1[:, c % 2].rearrange("p (q b t) -> p q b t", q=GT, b=PAIR)[:, :, b, :]
                            ins = v.scalar_tensor_tensor(yv, xv, d_ch[:, c:c + 1],
                                                         (p_y0, p_y1)[b][:, 0:GT * T].rearrange("p (q t) -> p q t", t=T),
                                                         ALU.mult, ALU.add)
                        ins.then_inc(sm["y_done"], 1)

                    for k in range(CT + 3):
                        if k < CT:
                            conv(k)
                            silu_z(k)
                        if 1 <= k <= CT:
                            scale_x(k - 1)
                        if k < CT:
                            silu_x(k)
                        if 2 <= k <= CT + 1:
                            skip_x(k - 2)
                    v.wait_ge(sm["r_sd"], g + 1)
                    ch.link(v.reciprocal(rs[:, :], sd[:, :]))
                    v.wait_ge(sm["o_mm"], g * CT + CT)
                    for t in range(GT):
                        ins = v.scalar_tensor_tensor(xtile(t), (p_o0, p_o1)[t // 2][:, D * (t % 2):D * (t % 2) + D],
                                                     rs[:, t:t + 1], xtile(t), ALU.mult, ALU.add)
                    ch.link(ins, bare=True)
                    ln(1)

                    v.wait_ge(sm["sig"], g + 1)
                    ch.link(v.tensor_scalar(e_g[:, :, :], e_g[:, :, :], 1.0, None, ALU.add))
                    ch.link(v.reciprocal(e_g[:, :, :], e_g[:, :, :]))
                    ch.link(v.tensor_scalar(sc[:, :, :], e_g[:, :, :], rsc[:, 0:1], None, ALU.mult))
                    mine = sc[:, :, :].rearrange("p q (e o) -> p q e o", o=1).broadcast_to([P, GT, E, E])
                    other = sc[:, :, :].rearrange("p q (o f) -> p q o f", o=1).broadcast_to([P, GT, E, E])
                    v.tensor_tensor(cmp_[:, :, :, :], other, mine, ALU.is_equal).then_inc(sm["d_chain"], 1)
                    ch.n += 1
                    ch.link(v.tensor_tensor(cmp2[:, :, :, :], other, mine, ALU.is_gt))
                    ch.link(v.tensor_tensor(cmp_[:, :, :, :], cmp_[:, :, :, :],
                                            below[:, :, :].rearrange("p (o e) f -> p o e f", o=1).broadcast_to([P, GT, E, E]), ALU.mult))
                    ch.link(v.tensor_tensor(cmp_[:, :, :, :], cmp_[:, :, :, :], cmp2[:, :, :, :], ALU.add))
                    ch.link(v.tensor_reduce(cnt[:, :, :], cmp_[:, :, :, :], AX_X, ALU.add))
                    ch.link(v.scalar_tensor_tensor(e_g[:, :, :], cnt[:, :, :], 2.0, sc[:, :, :], ALU.is_lt, ALU.mult))
                    ch.link(v.tensor_reduce(tot[:, :], e_g[:, :, :], AX_X, ALU.add))
                    ch.link(v.reciprocal(tot[:, :], tot[:, :]))
                    v.tensor_tensor(gate[:, :, 0:E], e_g[:, :, :],
                                    tot[:, :].rearrange("p (q o) -> p q o", o=1).broadcast_to([P, GT, E]),
                                    ALU.mult).then_inc(sm["gate_ready"], 1)
                    v.wait_ge(sm["gate_t"], g + 1)
                    v.tensor_copy(gT[:, :], p_s[0:E + 1, :]).then_inc(sm["gt_ready"], 1)

                    for n in range(E + 1):
                        v.wait_ge(sm["f_mm"], g * (E + 1) + n + 1)
                        banks = ((p_y0, p_y1), (p_o0, p_o1))[n % 2]
                        if n == 0:
                            for h in range(2):
                                xx = X[:, bass.ds(g * GT + 2 * h, 2), :]
                                v.tensor_tensor(xx, xx, banks[h][:, :].rearrange("p (q d) -> p q d", q=2),
                                                ALU.add).then_inc(sm["f_acc"], 1)
                            v.wait_ge(sm["f_acc"], g * PER_F + 2 + 1)
                            continue
                        for t in range(GT):
                            if n >= 2:
                                v.wait_ge(sm["f_acc"], g * PER_F + 2 + GT * (n - 2) + t + 1 + 1)
                            v.scalar_tensor_tensor(xtile(t), banks[t // 2][:, D * (t % 2):D * (t % 2) + D],
                                                   gate[:, t, order[n]:order[n] + 1], xtile(t), ALU.mult,
                                                   ALU.add).then_inc(sm["f_acc"], 1)
                    ch.leave(NG)


_INS = ["x", "ctx_1024", "L0_attn_W_in", "L0_attn_conv_w", "L0_attn_conv_b", "L0_attn_A_log", "L0_attn_D_param",
        "L0_attn_dt_bias", "L0_attn_norm_w", "L0_attn_W_out", "L0_ffn_gate_W", "L0_ffn_W1", "L0_ffn_b1", "L0_ffn_W2",
        "L0_ffn_b2", "L0_ffn_Ws1", "L0_ffn_bs1", "L0_ffn_Ws2", "L0_ffn_bs2", "L0_ffn_route_scale"]


def kernel(**inputs):
    import numpy as _np
    import concourse.bacc as _bacc
    from concourse import mybir as _mybir
    from concourse.bass_utils import run_bass_kernel_spmd as _run

    nc = _bacc.Bacc("TRN2", target_bir_lowering=False, num_devices=1)
    arrays, args = {}, []
    for name in _INS:
        a = _np.ascontiguousarray(inputs[name])
        if name == "L0_ffn_route_scale":
            a = a.reshape(1)
        arrays[f"in_{name}_dram"] = a
        args.append(nc.dram_tensor(f"in_{name}_dram", a.shape, _mybir.dt.from_np(a.dtype), kind="ExternalInput").ap())
    args.append(nc.dram_tensor("out_dram", (NB, T, D), F32, kind="ExternalOutput").ap())
    perceiver(nc, *args)
    r = _run(nc, [arrays], core_ids=[0])
    return r.results[0]["out_dram"]
```

```python
from contextlib import ExitStack

import concourse.bass as bass
from concourse import mybir

F32 = mybir.dt.float32
F16 = mybir.dt.float16
ALU = mybir.AluOpType
ACT = mybir.ActivationFunctionType
AX_X = mybir.AxisListType.X

P = 128
NB, T, D = 32, 64, 256
S = 256
KC = D // P
NT = NB * T // P
PAIR = P // T
EPS = 1e-5

BLOCKS = 4
BI = S // BLOCKS
CHUNK = 4
SLOTS = T + CHUNK * (BLOCKS - 1)
CHUNKS = SLOTS // CHUNK
TABLE = 80
BIG = 1e30

GT = 4
NG = NT // GT
GB = GT * PAIR
GN = GT * P
HEADS, HD, NS, TAPS = 32, 64, 64, 4
INNER = HEADS * HD
CT = INNER // P
PROJ = 2 * INNER + 2 * NS + HEADS
E, H = 8, 128
PAD = TAPS - 1
RING = 3
CR = 4
N_W = 17
CHAIN_D = 64


def perceiver(nc, x, ctx_rows, W_in, conv_w, conv_b, A_log, D_param, dt_bias, norm_w, W_out,
              gate_W, W1, b1, W2, b2, Ws1, bs1, Ws2, bs2, route_scale, out):
    x_rows = x.rearrange("b t d -> (b t) d").rearrange("(n p) d -> p n d", p=P)
    out_rows = out.rearrange("b t d -> (b t) d").rearrange("(n p) d -> p n d", p=P)
    ctx_tiles = ctx_rows.rearrange("b (h p) d -> p b h d", p=P)
    dist = nc.dram_tensor("distances", (NB, T, S), F32, kind="Internal").ap()
    dist_rows = dist.rearrange("b j i -> (b j) i")

    with ExitStack() as ctx:
        def sb(name, shape, dt=F32):
            return ctx.enter_context(nc.sbuf_tensor(name, shape, dt))

        def sem(name):
            return ctx.enter_context(nc.semaphore(name))

        bank = [ctx.enter_context(nc.psum_tensor(f"bank{i}", [P, 512], F32)) for i in range(8)]
        p_x, p_z, p_t, p_s, p_y0, p_y1, p_o0, p_o1 = bank

        ident = sb("ident", [P, P])
        tri = sb("tri", [P, T])
        later = sb("later", [P, P])
        ones = sb("ones", [P, 1])
        zero = sb("zero", [P, 1])
        spare = sb("spare", [P, 1])
        ones16 = sb("ones16", [NB, P], F16)
        below = sb("below", [P, E, E])
        row_id = sb("row_id", [P, KC])
        eps1 = sb("eps1", [P, 1])
        eps4 = sb("eps4", [P, 1])
        lookup_id = sb("lookup_id", [NB, S])

        w_in = sb("w_in", [P, KC, PROJ])
        w_out = sb("w_out", [P, CT, D])
        b_1 = sb("b_1", [P, E + 1])
        b_2 = sb("b_2", [E + 1, D])
        w_gate = sb("w_gate", [P, KC, E])
        cw = sb("cw", [P, CT, TAPS])
        cb = sb("cb", [P, CT])
        cw_bc = sb("cw_bc", [NS, 2, TAPS])
        cb_bc = sb("cb_bc", [NS, 2])
        d_ch = sb("d_ch", [P, CT])
        nw = sb("nw", [P, CT])
        a_exp = sb("a_exp", [P, HEADS])
        dtb = sb("dtb", [P, HEADS])
        rsc = sb("rsc", [P, 1])

        X = sb("X", [P, NT, D])
        bn = sb("bn", [P, GT, 6])
        mv = sb("mv", [P, GT, 2])
        sd = sb("sd", [P, GT])
        rs = sb("rs", [P, GT])
        cr = sb("cr", [P, CR, PAIR, 2, D])
        Hpath = sb("Hpath", [NB, T + 1])
        Hd = sb("Hd", [NB, NB, T + 1], F16)

        s_const = sem("s_const")
        s_x = sem("s_x")
        s_w = sem("s_w")
        s_we = sem("s_we")
        s_table = sem("s_table")
        s_path = sem("s_path")
        dist_out = [sem(f"dist_out{k}") for k in range(2)]
        ctx_in = [sem(f"ctx_in{k}") for k in range(CR)]
        act_done = sem("act_done")
        dve_done = sem("dve_done")
        pool_done = sem("pool_done")
        a_sd = sem("a_sd")
        a_norm = sem("a_norm")
        a_rows_t = sem("a_rows_t")
        a_x_t = sem("a_x_t")
        a_c_t = sem("a_c_t")
        a_c = sem("a_c")
        a_mm = sem("a_mm")
        a_sq = sem("a_sq")
        a_clamp = sem("a_clamp")
        a_root = sem("a_root")
        a_aa = sem("a_aa")
        a_aa_act = sem("a_aa_act")
        dist_in = [sem(f"dist_in{q}") for q in range(4)]
        b_scan = sem("b_scan")
        b_step = sem("b_step")

        class Chain:
            def __init__(self, engine, sem_):
                self.engine, self.sem, self.base, self.n = engine, sem_, 0, 0

            def link(self, ins, bare=False):
                ins.then_inc(self.sem, 1)
                self.n += 1
                self.engine.wait_ge(self.sem, self.base + self.n)
                if bare:
                    self.engine.memset(spare[:, :], 0.0)

            def enter(self, i, per):
                self.start, self.per = self.base + self.n, per
                self.base, self.n = self.start + i * per, 0

            def leave(self, count):
                assert self.n == self.per, (self.n, self.per)
                self.base, self.n = self.start + count * self.per, 0

        def wait(engine, sem_, value):
            if not isinstance(value, int) or value > 0:
                engine.wait_ge(sem_, value)

        def carrier(pe, psum):
            pe.matmul(psum[:, 0:1], lhsT=ones16[:, :], rhs=ones16[:, 0:1], start=True, stop=True)

        inner = ExitStack()
        with inner:
            def tb(name, shape, dt=F32):
                return inner.enter_context(nc.sbuf_tensor(name, shape, dt))

            xn = tb("a_xn", [P, 2, D])
            sq = tb("a_sqj", [P, D])
            sqd = tb("a_sqd", [P, 2 * PAIR, D])
            bn_a = tb("bn_a", [P, NT, 6])
            mv_a = tb("mv_a", [P, NT, 2])
            sd_a = tb("sd_a", [P, NT])
            rs_a = tb("rs_a", [P, NT])
            bb = tb("a_bb", [P, NT])
            aa = tb("a_aa_t", [P, CR, PAIR, 2])
            xt = tb("a_xt", [P, 2, KC, P])
            ct_t = tb("a_ct", [P, 2, PAIR, KC, S])
            dd = tb("a_dd", [P, 2, S])
            ds = tb("a_ds", [P, 2, S])
            Dk = tb("Dk", [P, SLOTS, BI])
            dn_view = Dk[:, :, :].rearrange("p s i -> p (s i)").bitcast(F16)
            R = tb("R", [P, SLOTS + 1, BI + 1])
            m1 = tb("m1", [P, BI])
            qk = tb("qk", [P, CHUNK, BI])
            rk = tb("rk", [P, CHUNK, BI])
            ak = tb("ak", [P, CHUNK, BI])
            ek = tb("ek", [P, CHUNK, BI])
            blk_id = tb("blk_id", [P, CHUNK, BI])
            Wk = tb("Wk", [P, CHUNK, BI + 1])
            Nk = tb("Nk", [P, CHUNK, BI + 1])
            mk = tb("mk", [P, CHUNK, BI + 1])
            table = tb("table", [NB, BLOCKS * TABLE * BI], F16)
            junk = tb("junk", [NB, BLOCKS, BI])
            tab = table[:, :].rearrange("b (g j i) -> b g j i", g=BLOCKS, j=TABLE)

            a_it = NT // CR

            def ahead(engine, fetch, finish):
                def tiles(it, last=False):
                    for k in range(CR):
                        n = it * CR + k
                        if not (last and k == CR - 1):
                            fetch(n + 1, (k + 1) % CR, it + (k + 1) // CR)
                        finish(n, k)

                fetch(0, 0, 0)
                tiles(0)
                with engine.Fori(1, a_it - 1) as it:
                    tiles(it)
                tiles(a_it - 1, last=True)

            def stores_before(n, par):
                return (n - par) * 8

            with nc.Block() as block:
                @block.gpsimd
                def _(pool):
                    ch = Chain(pool, pool_done)
                    ch.link(pool.memset(ones[:, :], 1.0))
                    ch.link(pool.memset(zero[:, :], 0.0))
                    ch.link(pool.memset(ones16[:, :], 1.0))
                    ch.link(pool.memset(eps1[:, :], EPS))
                    ch.link(pool.memset(eps4[:, :], 4 * EPS))
                    ch.link(pool.memset(ident[:, :], 0.0))
                    ch.link(pool.affine_select(out=ident[:, :], in_=ident[:, :], compare_op=ALU.not_equal,
                                               fill=1.0, base=0, pattern=[[-1, P]], channel_multiplier=1))
                    ch.link(pool.memset(tri[:, :], 1.0))
                    ch.link(pool.memset(later[:, :], 0.0))
                    ch.link(pool.memset(below[:, :, :], 1.0))
                    for h in range(PAIR):
                        q = slice(T * h, T * h + T)
                        ch.link(pool.affine_select(out=tri[q, :], in_=tri[q, :], compare_op=ALU.is_ge,
                                                   fill=0.0, base=0, pattern=[[1, T]], channel_multiplier=-1))
                        ch.link(pool.affine_select(out=later[q, q], in_=later[q, q], compare_op=ALU.is_ge,
                                                   fill=1.0, base=0, pattern=[[1, T]], channel_multiplier=-1))
                    ch.link(pool.affine_select(out=below[:, :, :], in_=below[:, :, :], compare_op=ALU.is_gt,
                                               fill=0.0, base=0, pattern=[[1, E], [-1, E]], channel_multiplier=0))
                    for h in range(KC):
                        ch.link(pool.iota(row_id[:, h:h + 1], pattern=[[0, 1]], base=P * h, channel_multiplier=1,
                                          allow_small_or_imprecise_dtypes=True))
                    ch.link(pool.iota(lookup_id[:, :], pattern=[[1, S]], base=0, channel_multiplier=0,
                                      allow_small_or_imprecise_dtypes=True))
                    for g in range(BLOCKS):
                        q = slice(32 * g, 32 * g + 32)
                        ch.link(pool.iota(blk_id[q, :, :], pattern=[[0, CHUNK], [1, BI]], base=BI * g,
                                          channel_multiplier=0, allow_small_or_imprecise_dtypes=True))
                        if g:
                            ch.link(pool.memset(Dk[q, 0:CHUNK * g, :], BIG))
                        if g < BLOCKS - 1:
                            ch.link(pool.memset(Dk[q, CHUNK * g + T:SLOTS, :], BIG))
                    ch.link(pool.memset(R[:, 0, :], BIG))
                    ch.link(pool.memset(R[:, 1:SLOTS + 1, 0:1], BIG))
                    ch.link(pool.memset(R[0:NB, 0, 0:1], 0.0))
                    ch.link(pool.memset(Wk[:, :, 0:1], 0.0))
                    ch.link(pool.memset(mk[:, :, :], 1.0))
                    ch.link(pool.memset(mk[:, :, 0:1], 0.0))
                    ch.link(pool.memset(Hpath[:, 0:1], 0.0))
                    pool.memset(Hpath[:, T:T + 1], float(S - 1)).then_inc(s_const, 1)

                @block.sync
                def _(sp):
                    sp.dma_start(X[:, :, :], x_rows).then_inc(s_x, 16)

                    def load(n, k, before):
                        wait(sp, ctx_in[k], before * 16)
                        wait(sp, a_c_t, (n - CR + 1) * 2)
                        wait(sp, a_mm, n - CR + 1)
                        sp.dma_start(cr[:, k], ctx_tiles[:, bass.ds(n * PAIR, PAIR)]).then_inc(ctx_in[k], 16)

                    def weights():
                        def ld(dst, src):
                            sp.dma_start(dst, src, allow_slow_non_contiguous=True).then_inc(s_w, 16)
                            return 1
                        n = ld(w_in[:, :, :], W_in.rearrange("(c p) n -> p c n", p=P))
                        n += ld(w_out[:, :, :], W_out.rearrange("(c p) n -> p c n", p=P))
                        n += ld(b_1[:, 0:E], b1.rearrange("e h -> h e"))
                        n += ld(b_1[:, E:E + 1], bs1.rearrange("(h o) -> h o", o=1))
                        n += ld(b_2[0:E, :], b2)
                        n += ld(b_2[E:E + 1, :], bs2.rearrange("(o d) -> o d", o=1))
                        n += ld(w_gate[:, :, :], gate_W.rearrange("(c p) e -> p c e", p=P))
                        cwf = conv_w.rearrange("c o k -> c (o k)")
                        n += ld(cw[:, :, :], cwf[0:INNER, :].rearrange("(c p) k -> p c k", p=P))
                        n += ld(cb[:, :], conv_b[0:INNER].rearrange("(c p) -> p c", p=P))
                        n += ld(cw_bc[:, :, :], cwf[INNER:, :].rearrange("(c p) k -> p c k", p=NS))
                        n += ld(cb_bc[:, :], conv_b[INNER:].rearrange("(c p) -> p c", p=NS))
                        for h in range(2):
                            n += ld(d_ch[HD * h:HD * h + HD, :],
                                    D_param.rearrange("(c h) -> h c", h=2)[h:h + 1, :].broadcast_to([HD, CT]))
                        n += ld(nw[:, :], norm_w.rearrange("(c p) -> p c", p=P))
                        n += ld(a_exp[:, :], A_log.rearrange("(o h) -> o h", o=1).broadcast_to([P, HEADS]))
                        n += ld(dtb[:, :], dt_bias.rearrange("(o h) -> o h", o=1).broadcast_to([P, HEADS]))
                        n += ld(rsc[:, :], route_scale.rearrange("(o h) -> o h", o=1).broadcast_to([P, 1]))
                        return n

                    def store(n, par):
                        wait(sp, a_root, n + 1)
                        sp.dma_start(dist_rows[bass.ds(n * P, P), :], ds[:, par, :]).then_inc(dist_out[par], 16)

                    for k in range(CR):
                        load(k, k, 0)
                    with sp.Fori(0, a_it - 1) as it:
                        for k in range(CR):
                            load((it + 1) * CR + k, k, it + 1)
                            store(it * CR + k, k % 2)
                    for k in range(CR):
                        store((a_it - 1) * CR + k, k % 2)
                    for par in range(2):
                        sp.wait_ge(dist_out[par], 16 * NT // 2)
                    sp.wait_ge(s_const, 1)
                    quarter = T // 4
                    for q in range(4):
                        for g in range(BLOCKS):
                            sp.dma_start(Dk[32 * g:32 * g + 32, CHUNK * g + quarter * q:CHUNK * g + quarter * q + quarter, :],
                                         dist[:, quarter * q:quarter * q + quarter, BI * g:BI * g + BI]
                                         ).then_inc(dist_in[q], 16)
                    assert weights() == N_W
                    with sp.Fori(0, CHUNKS) as c:
                        sp.wait_ge(b_step, c + 1)
                        for g in range(BLOCKS):
                            sp.dma_start(table[:, bass.ds((g * TABLE - g * CHUNK + c * CHUNK) * BI, CHUNK * BI)],
                                         dn_view[32 * g:32 * g + 32, bass.ds(c * (2 * CHUNK * BI), CHUNK * BI)]
                                         ).then_inc(s_table, 16)
                    sp.wait_ge(s_w, 16 * N_W)

                @block.vector
                def _(v):
                    ch = Chain(v, dve_done)
                    v.wait_ge(s_x, 16)
                    for t in range(NT):
                        v.bn_stats(bn_a[:, t, :], X[:, t, :]).then_inc(dve_done, 1)
                        ch.n += 1
                    v.wait_ge(dve_done, ch.n)
                    for t in range(NT - 1):
                        v.bn_aggr(mv_a[:, t, :], bn_a[:, t, :])
                    v.bn_aggr(mv_a[:, NT - 1, :], bn_a[:, NT - 1, :]).then_inc(a_norm, 1)
                    v.wait_ge(a_sd, 1)
                    ch.link(v.reciprocal(rs_a[:, :], sd_a[:, :]))

                    def fetch(n, k, inside):
                        par = k % 2
                        wait(v, a_x_t, n - 1)
                        wait(v, a_sq, n - 1)
                        v.tensor_scalar(xn[:, par, :], X[:, bass.ds(n, 1), :].rearrange("p o d -> p (o d)"),
                                        mv_a[:, bass.ds(n, 1), 0:1].rearrange("p o d -> p (o d)"),
                                        rs_a[:, bass.ds(n, 1)], ALU.subtract, ALU.mult).then_inc(a_rows_t, 1)
                        for b in range(PAIR):
                            v.wait_ge(a_c_t, n * 2 + b + 1)
                            if b == 0:
                                wait(v, a_mm, n - 1)
                            v.tensor_copy(ct_t[:, par, b].rearrange("p c i -> p (c i)"), bank[2 + b][:, :]).then_inc(a_c, 1)
                            if b == 0:
                                v.wait_ge(ctx_in[k], inside * 16 + 16)
                                wait(v, a_mm, n - CR + 1)
                                wait(v, a_aa, n)
                                for h in range(2):
                                    ins = v.tensor_tensor_reduce(sqd[:, h, :], cr[:, k, 0, h, :], cr[:, k, 0, h, :], 1.0, 0.0,
                                                                 ALU.mult, ALU.add, aa[:, k, 0, h:h + 1])
                                ins.then_inc(a_aa, 1)

                    def clamp(n, k):
                        par = k % 2
                        v.wait_ge(a_mm, n + 1)
                        v.wait_ge(a_sq, n + 1)
                        wait(v, a_root, n - 1)
                        v.tensor_scalar(dd[:, par, :], bank[4 + par][:, 0:S], bb[:, bass.ds(n, 1)], 0.0,
                                        ALU.add, ALU.max).then_inc(a_clamp, 1)

                    ahead(v, fetch, clamp)

                    v.wait_ge(s_const, 1)
                    def do(ins):
                        ins.then_inc(dve_done, 1)
                        ch.n += 1
                        return ch.n

                    def need(count):
                        v.wait_ge(dve_done, count)

                    def choices(c):
                        left = R[:, c * CHUNK:c * CHUNK + CHUNK, 1:BI + 1]
                        diag = R[:, c * CHUNK:c * CHUNK + CHUNK, 0:BI]
                        up = R[:, c * CHUNK + 1:c * CHUNK + 1 + CHUNK, 0:BI]
                        q = do(v.tensor_tensor(qk[:, :, :], up, left, ALU.is_gt))
                        yield
                        r = do(v.tensor_tensor(rk[:, :, :], up, diag, ALU.is_ge))
                        yield
                        a = do(v.tensor_tensor(ak[:, :, :], diag, left, ALU.is_le))
                        yield
                        need(r)
                        q = do(v.tensor_tensor(qk[:, :, :], qk[:, :, :], rk[:, :, :], ALU.max))
                        yield
                        need(a)
                        e = do(v.scalar_tensor_tensor(ek[:, :, :], ak[:, :, :], -0.5, blk_id[:, :, :], ALU.mult, ALU.add))
                        yield
                        need(e)
                        w = do(v.tensor_tensor(Wk[:, :, 1:BI + 1], qk[:, :, :], ek[:, :, :], ALU.mult))
                        yield
                        need(w)
                        n = do(v.tensor_tensor_scan(Nk[:, :, :].rearrange("p c i -> p (c i)"),
                                                    mk[:, :, :].rearrange("p c i -> p (c i)"),
                                                    Wk[:, :, :].rearrange("p c i -> p (c i)"), 0.0, ALU.mult, ALU.max))
                        yield
                        need(n)
                        dst = dn_view[:, c * (2 * CHUNK * BI):c * (2 * CHUNK * BI) + CHUNK * BI]
                        v.tensor_tensor(dst.rearrange("p (c i) -> p c i", i=BI), Nk[:, :, 1:BI + 1], Nk[:, :, 0:BI],
                                        ALU.subtract).then_inc(b_step, 1)
                        if c < CHUNKS - 1:
                            for g in range(BLOCKS - 1):
                                do(v.tensor_copy(Wk[32 * g + 32:32 * g + 64, :, 0:1], Nk[32 * g:32 * g + 32, :, BI:BI + 1]))
                        yield

                    moves, row = iter(()), 0
                    for c in range(CHUNKS):
                        if c * CHUNK % (T // 4) == 0 and c * CHUNK < T:
                            v.wait_ge(dist_in[c * CHUNK // (T // 4)], 16 * BLOCKS)
                        for u in range(CHUNK):
                            s = c * CHUNK + u
                            if row:
                                need(row)
                            low = do(v.tensor_tensor(m1[:, :], R[:, s, 0:BI], R[:, s, 1:BI + 1], ALU.min))
                            next(moves, None)
                            need(low)
                            row = do(v.tensor_tensor_scan(R[:, s + 1, 1:BI + 1], m1[:, :], Dk[:, s, :], R[:, s + 1, 0:1],
                                                          ALU.min, ALU.add))
                            next(moves, None)
                        if c < CHUNKS - 1:
                            need(row)
                            for g in range(BLOCKS - 1):
                                row = do(v.tensor_copy(R[32 * g + 32:32 * g + 64, (c + 1) * CHUNK + 1:(c + 2) * CHUNK + 1, 0:1],
                                                       R[32 * g:32 * g + 32, c * CHUNK + 1:(c + 1) * CHUNK + 1, BI:BI + 1]))
                        moves = choices(c)
                    need(row)
                    for _ in moves:
                        pass

                    v.wait_ge(s_table, 16 * BLOCKS * CHUNKS)
                    for j in range(T - 1, 0, -1):
                        ch.link(v.scalar_tensor_tensor(junk[:, :, :], lookup_id[:, :].rearrange("b (g i) -> b g i", g=BLOCKS),
                                                       Hpath[:, j + 1:j + 2], tab[:, :, j, :], ALU.is_le, ALU.mult,
                                                       accum_out=Hpath[:, j:j + 1]))
                    v.tensor_tensor(Hd[:, :, :],
                                    Hpath[:, :].rearrange("b (o j) -> b o j", o=1).broadcast_to([NB, NB, T + 1]),
                                    ident[0:NB, 0:NB].rearrange("b (c o) -> b c o", o=1).broadcast_to([NB, NB, T + 1]),
                                    ALU.mult).then_inc(s_path, 1)
                    v.wait_ge(s_w, 16 * N_W)
                    for w in (cw[:, :, :], cb[:, :], cw_bc[:, :, :], cb_bc[:, :]):
                        v.tensor_scalar(w, w, 0.5, None, ALU.mult)
                    for c in range(CT):
                        v.tensor_scalar(w_out[:, c, :], w_out[:, c, :], nw[:, c:c + 1], None, ALU.mult)

                @block.scalar
                def _(act):
                    act.wait_ge(a_norm, 1)
                    act.wait_ge(s_const, 1)
                    act.activation(sd_a[:, :], mv_a[:, :, 1], ACT.Sqrt, bias=eps1[:, :]).then_inc(a_sd, 1)

                    def fetch(n, k, inside):
                        par = k % 2
                        act.wait_ge(a_rows_t, n + 1)
                        wait(act, a_sq, n)
                        act.activation(sq[:, :], xn[:, par, :], ACT.Square, accum_out=bb[:, bass.ds(n, 1)]).then_inc(a_sq, 1)
                        act.wait_ge(a_x_t, n + 1)
                        wait(act, a_mm, n - 1)
                        act.activation(xt[:, par].rearrange("p c i -> p (c i)"), bank[par][:, 0:KC * P], ACT.Copy,
                                       scale=-2.0).then_inc(act_done, 1)
                        act.wait_ge(ctx_in[k], inside * 16 + 16)
                        wait(act, a_mm, n - CR + 1)
                        wait(act, a_aa_act, n)
                        for h in range(2):
                            ins = act.activation(sqd[:, 2 + h, :], cr[:, k, 1, h, :], ACT.Square, accum_out=aa[:, k, 1, h:h + 1])
                        ins.then_inc(a_aa_act, 1)

                    def root(n, k):
                        par = k % 2
                        act.wait_ge(a_clamp, n + 1)
                        wait(act, dist_out[par], stores_before(n, par))
                        act.activation(ds[:, par, :], dd[:, par, :], ACT.Sqrt).then_inc(a_root, 1)

                    ahead(act, fetch, root)
                    act.wait_ge(s_w, 16 * N_W)
                    act.activation(a_exp[:, :], a_exp[:, :], ACT.Exp)

                @block.tensor
                def _(pe):
                    pe.wait_ge(s_const, 1)

                    def fetch(n, k, inside):
                        par = k % 2
                        pe.wait_ge(a_rows_t, n + 1)
                        wait(pe, act_done, n - 1)
                        for c in range(KC):
                            mm = pe.transpose(bank[par][:, P * c:P * c + P], xn[:, par, P * c:P * c + P], ident[:, :])
                        mm.then_inc(a_x_t, 1)
                        pe.wait_ge(ctx_in[k], inside * 16 + 16)
                        for b in range(PAIR):
                            wait(pe, a_c, n * 2 - 2 + b + 1)
                            for c in range(KC):
                                for h in range(2):
                                    mm = pe.transpose(bank[2 + b][:, S * c + P * h:S * c + P * h + P],
                                                      cr[:, k, b, h, P * c:P * c + P], ident[:, :])
                            mm.then_inc(a_c_t, 1)

                    def products(n, k):
                        par = k % 2
                        pe.wait_ge(act_done, n + 1)
                        pe.wait_ge(a_aa, n + 1)
                        pe.wait_ge(a_aa_act, n + 1)
                        wait(pe, a_clamp, n - 1)
                        for b in range(PAIR):
                            pe.wait_ge(a_c, n * 2 + b + 1)
                            q = slice(T * b, T * b + T)
                            for c in range(KC):
                                pe.matmul(bank[4 + par][q, 0:S], lhsT=xt[:, par, c, q], rhs=ct_t[:, par, b, c, :],
                                          start=(c == 0), stop=False)
                            for h in range(2):
                                mm = pe.matmul(bank[4 + par][q, P * h:P * h + P],
                                               lhsT=aa[:, k, b, h:h + 1].broadcast_to([P, T]), rhs=ident[:, :],
                                               start=False, stop=(h == 1))
                        mm.then_inc(a_mm, 1)

                    ahead(pe, fetch, products)

        def buf(name, shape, dt=F32):
            return sb("d_" + name, shape, dt)

        w_1 = sb("w_1", [P, KC, E + 1, H])
        w_2 = sb("w_2", [P, E + 1, D])
        U = buf("U", [P, 2, GN])
        mask = buf("mask", [P, 2, GB, T])
        xg = buf("xg", [P, GT, D])
        XT = buf("XT", [P, KC, GN])
        XF = buf("XF", [P, KC, GN])
        dtv = buf("dtv", [P, GT, HEADS])
        dtn = buf("dtn", [P, GT, HEADS])
        dtu = buf("dtu", [P, GT, HEADS])
        dtl = buf("dtl", [P, GT, HEADS])
        dte = buf("dte", [P, GT, HEADS])
        dtd = buf("dtd", [P, GT, HEADS])
        dt_ = buf("dt", [P, GT, HEADS])
        da = buf("da", [P, GT, HEADS])
        bc_raw = buf("bc_raw", [NS, 2, GB, T + PAD])
        bc_acc = buf("bc_acc", [NS, 2, GB, T])
        bc_th = buf("bc_th", [NS, 2, GB, T])
        BC = bc_acc
        G = buf("G", [P, GT, T])
        raw = buf("raw", [P, 2, GB, T + PAD])
        acc = buf("acc", [P, 2, GB, T])
        th = buf("th", [P, 2, GN])
        xc = buf("xc", [P, RING, GN])
        zth = buf("zth", [P, 2, GN])
        zs = buf("zs", [P, RING, GN])
        xd = buf("xd", [P, 2, GT, 2, HD])
        steps = buf("steps", [P, 2, GT, 2, T])
        decay = buf("decay", [P, 2, GT, 2, T])
        M = buf("M", [P, 2, GT, 2, T])
        y1 = buf("y1", [P, 2, GN])
        yg = buf("yg", [P, 2, GN])
        ysq = U
        accq = buf("accq", [P, GN])
        e_g = buf("e_g", [P, GT, E])
        sc = buf("sc", [P, GT, E])
        cmp_ = buf("cmp", [P, GT, E, E])
        cmp2 = buf("cmp2", [P, GT, E, E])
        cnt = buf("cnt", [P, GT, E])
        tot = buf("tot", [P, GT])
        gate = buf("gate", [P, GT, E + 1])
        gT = bc_th[0:E + 1, 0].rearrange("p q t -> p (q t)")
        hh = buf("hh", [P, 2, GN])

        names = ("d_const pads spread mask_ready expanded ln_var ln_sd ln_rows ln_t ln_xt_a ln_xt_v dt_logit dt_neg dt_ln "
                 "dt_ready bc_proj bc_in bc_conv bc_tanh bc_ready g_mm g_ready x_proj z_proj x_acc conv_done th_done "
                 "xc_done zth_done zs_done x_t xd_done r_done seg e_done m_done y_mm y_done yg_done sq_done accq_done "
                 "o_mm ssq r_sd logits sig gate_ready gate_t gt_ready h_mm h_done f_mm f_acc d_chain out_done act_link").split()
        sm = {n: sem("d_" + n) for n in names}
        AL = "p (q t) -> p q t"
        SHARE = E
        order = [SHARE] + list(range(E))
        PER_F = 2 + GT * E
        x_ch = lambda c: INNER + P * c
        z_ch = lambda c: P * c

        PE_PARTS = (1, 1, 1, 0, 1, 1, 1, 0, 1)
        ACT_PARTS = (0, 0, 0, 0, 1, 1, 1, 1, 1)
        DVE_PARTS = (1, 0, 1, 1, 1, 1, 1, 0, 1)

        def groups(engine, prepare, mamba, experts, chain=None, per=0):
            for _ in prepare(0):
                pass
            mamba(0)
            with engine.Fori(1, NG) as g:
                if chain:
                    chain.enter(g - 1, per)
                parts = prepare(g)
                experts(g - 1, parts)
                for _ in parts:
                    pass
                mamba(g)
                if chain:
                    chain.leave(NG - 1)
            experts(NG - 1, iter(()))

        with nc.Block() as block:
            @block.sync
            def _(sp):
                for k in range(CR):
                    sp.dma_start(cr[:, k], ctx_tiles[:, PAIR * k:PAIR * k + PAIR]).then_inc(ctx_in[k], 16)
                for c in range(KC):
                    sp.dma_start(w_1[:, c, 0:E, :], W1[:, P * c:P * c + P, :].rearrange("e p h -> p e h")).then_inc(s_we, 16)
                    sp.dma_start(w_1[:, c, E, :], Ws1[P * c:P * c + P, :]).then_inc(s_we, 16)
                sp.dma_start(w_2[:, 0:E, :], W2.rearrange("e h d -> h e d")).then_inc(s_we, 16)
                sp.dma_start(w_2[:, E, :], Ws2).then_inc(s_we, 16)
                with sp.Fori(0, NG - 1) as g:
                    for k in range(CR):
                        sp.wait_ge(sm["expanded"], g * GT + k + 1)
                        sp.dma_start(cr[:, k], ctx_tiles[:, bass.ds(((g + 1) * GT + k) * PAIR, PAIR)]).then_inc(ctx_in[k], 16)
                    sp.wait_ge(sm["f_acc"], (g + 1) * PER_F + 1)
                    sp.dma_start(out_rows[:, bass.ds(g * GT, GT), :], X[:, bass.ds(g * GT, GT), :]).then_inc(sm["out_done"], 16)
                sp.wait_ge(sm["f_acc"], NG * PER_F + 1)
                sp.dma_start(out_rows[:, NT - GT:NT, :], X[:, NT - GT:NT, :]).then_inc(sm["out_done"], 16)
                sp.wait_ge(sm["out_done"], 16 * NG)

            @block.tensor
            def _(pe):
                pe.wait_ge(s_path, 1)
                pe.wait_ge(sm["d_const"], 1)

                def ln_transpose(g, u):
                    for t in range(GT):
                        pe.wait_ge(sm["ln_rows"], (g * 2 + u) * GT + t + 1)
                        for c in range(KC):
                            mm = pe.transpose(((p_t, p_s), (p_x, p_z))[u][c][:, P * t:P * t + P], xg[:, t, P * c:P * c + P], ident[:, :])
                    mm.then_inc(sm["ln_t"], 1)

                def prepare(g):
                    pe.matmul(p_t[:, :], lhsT=ones16[:, :], rhs=Hd[:, bass.ds(g * GB, GB), 1:T + 1], start=True, stop=True)
                    pe.matmul(p_s[:, :], lhsT=ones16[:, :], rhs=Hd[:, bass.ds(g * GB, GB), 0:T], start=True,
                              stop=True).then_inc(sm["spread"], 1)
                    yield
                    pe.wait_ge(sm["mask_ready"], g + 1)
                    for t in range(GT):
                        pe.wait_ge(ctx_in[t], 16 * (NT // CR) + g * 16 + 16)
                        for b in range(PAIR):
                            for h in range(2):
                                mm = pe.matmul((p_t, p_s)[t // 2][T * b:T * b + T, D * (t % 2):D * (t % 2) + D],
                                               lhsT=mask[:, h, PAIR * t + b, :], rhs=cr[:, t, b, h, :],
                                               start=(h == 0), stop=(h == 1))
                        mm.then_inc(sm["expanded"], 1)
                        if t % 2:
                            yield
                    ln_transpose(g, 0)
                    yield
                    pe.wait_ge(sm["ln_xt_a"], g * 2 + 1)
                    pe.wait_ge(sm["ln_xt_v"], g * 2 + 1)
                    for t in range(GT):
                        for c in range(KC):
                            mm = pe.matmul(p_t[:, HEADS * t:HEADS * t + HEADS], lhsT=XT[:, c, P * t:P * t + P],
                                           rhs=w_in[:, c, PROJ - HEADS:PROJ], start=(c == 0), stop=(c == KC - 1))
                    mm.then_inc(sm["dt_logit"], 1)
                    for j in range(2):
                        if j:
                            yield
                            pe.wait_ge(sm["dt_neg"], g + 1)
                        o = 2 * INNER + NS * j
                        for c in range(KC):
                            mm = pe.matmul((p_s, p_t)[j][0:NS, :], lhsT=w_in[:, c, o:o + NS], rhs=XT[:, c, :],
                                           start=(c == 0), stop=(c == KC - 1))
                        mm.then_inc(sm["bc_proj"], 1)
                    yield
                    for b in range(GB):
                        if b == 0:
                            pe.wait_ge(sm["bc_ready"], g * 2 + 2)
                            pe.wait_ge(sm["dt_ready"], g + 1)
                            carrier(pe, p_s)
                        mm = pe.matmul(p_s[T * (b % 2):T * (b % 2) + T, T * (b // 2):T * (b // 2) + T],
                                       lhsT=BC[:, 0, b, :], rhs=BC[:, 1, b, :], start=True, stop=True)
                    mm.then_inc(sm["g_mm"], 1)

                def mamba(g):
                    def project(c):
                        if c >= 1:
                            pe.wait_ge(sm["x_acc"], g * CT + c)
                        for k in range(KC):
                            mm = pe.matmul(p_x[:, :], lhsT=w_in[:, k, x_ch(c):x_ch(c) + P], rhs=XT[:, k, :],
                                           start=(k == 0), stop=(k == KC - 1))
                        mm.then_inc(sm["x_proj"], 1)
                        if c >= 1:
                            pe.wait_ge(sm["zs_done"], g * CT + c)
                        for k in range(KC):
                            mm = pe.matmul(p_z[:, :], lhsT=w_in[:, k, z_ch(c):z_ch(c) + P], rhs=XT[:, k, :],
                                           start=(k == 0), stop=(k == KC - 1))
                        mm.then_inc(sm["z_proj"], 1)

                    def segments(c):
                        pe.wait_ge(sm["r_done"], g * CT + c + 1)
                        if c >= 1:
                            pe.wait_ge(sm["e_done"], g * CT + c)
                        pe.matmul(p_s[:, :], lhsT=later[:, :], rhs=steps[:, c % 2].rearrange("p q h t -> p (q h t)"),
                                  start=True, stop=True).then_inc(sm["seg"], 1)

                    def turn(c):
                        pe.wait_ge(sm["xc_done"], g * CT + c + 1)
                        if c >= 1:
                            pe.wait_ge(sm["xd_done"], g * CT + c)
                        for t in range(GT):
                            mm = pe.transpose(p_t[:, P * t:P * t + P], xc[:, c % RING, P * t:P * t + P], ident[:, :])
                        mm.then_inc(sm["x_t"], 1)

                    def mix(c):
                        pe.wait_ge(sm["xd_done"], g * CT + c + 1)
                        pe.wait_ge(sm["m_done"], g * CT + c + 1)
                        if c >= 1:
                            pe.wait_ge(sm["y_done"], g * CT + c)
                        carrier(pe, p_y0)
                        for t in range(GT):
                            for b in range(PAIR):
                                q = slice(T * b, T * b + T)
                                for h in range(2):
                                    mm = pe.matmul((p_y0, p_y1)[b][HD * h:HD * h + HD, T * t:T * t + T],
                                                   lhsT=xd[q, c % 2, t, h, :], rhs=M[q, c % 2, t, h, :],
                                                   start=True, stop=True)
                        mm.then_inc(sm["y_mm"], 1)

                    def output(c):
                        pe.wait_ge(sm["yg_done"], g * CT + c + 1)
                        for t in range(GT):
                            mm = pe.matmul((p_o0, p_o1)[t // 2][:, D * (t % 2):D * (t % 2) + D],
                                           lhsT=yg[:, c % 2, P * t:P * t + P], rhs=w_out[:, c, :],
                                           start=(c == 0 and t % 2 == 0), stop=(c == CT - 1), skip_group_check=True)
                        mm.then_inc(sm["o_mm"], 1)

                    pe.wait_ge(sm["f_acc"], g * PER_F + 1)
                    pe.wait_ge(sm["g_ready"], g + 1)
                    for k in range(CT + 3):
                        if k < CT:
                            project(k)
                            segments(k)
                        if 1 <= k <= CT:
                            turn(k - 1)
                        if 2 <= k <= CT + 1:
                            mix(k - 2)
                        if k >= 3:
                            output(k - 3)
                    pe.wait_ge(sm["accq_done"], g * CT + CT)
                    for t in range(GT):
                        mm = pe.matmul(p_t[:, t:t + 1], lhsT=accq[:, P * t:P * t + P], rhs=ones[:, :], start=True, stop=True)
                    mm.then_inc(sm["ssq"], 1)


                def experts(g, others):
                    ln_transpose(g, 1)
                    pe.wait_ge(sm["ln_xt_a"], g * 2 + 2)
                    pe.wait_ge(sm["ln_xt_v"], g * 2 + 2)
                    for t in range(GT):
                        for c in range(KC):
                            mm = pe.matmul(p_t[:, E * t:E * t + E], lhsT=XF[:, c, P * t:P * t + P], rhs=w_gate[:, c, :],
                                           start=(c == 0), stop=(c == KC - 1))
                    mm.then_inc(sm["logits"], 1)

                    def hidden(n):
                        e = order[n]
                        if n >= 2:
                            pe.wait_ge(sm["h_done"], g * (E + 1) + n - 1)
                        for c in range(KC):
                            mm = pe.matmul((p_x, p_z)[n % 2][:, :], lhsT=w_1[:, c, e, :], rhs=XF[:, c, :],
                                           start=(c == 0), stop=(c == KC - 1))
                        mm.then_inc(sm["h_mm"], 1)

                    def down(n):
                        e = order[n]
                        pe.wait_ge(sm["h_done"], g * (E + 1) + n + 1)
                        if n >= 2:
                            pe.wait_ge(sm["f_acc"], g * PER_F + 2 + GT * (n - 2) + 1)
                        if n == 0:
                            pe.wait_ge(sm["gt_ready"], g + 1)
                        for t in range(GT):
                            o = ((p_y0, p_y1), (p_o0, p_o1))[n % 2][t // 2][:, D * (t % 2):D * (t % 2) + D]
                            mm = pe.matmul(o, lhsT=hh[:, n % 2, P * t:P * t + P], rhs=w_2[:, e, :], start=True, stop=(n > 0))
                            if n == 0:
                                mm = pe.matmul(o, lhsT=gT[:, P * t:P * t + P], rhs=b_2[:, :], start=False, stop=True)
                        mm.then_inc(sm["f_mm"], 1)

                    pe.wait_ge(s_we, 16 * (2 * KC + 2))
                    hidden(0)
                    hidden(1)
                    pe.wait_ge(sm["gate_ready"], g + 1)
                    for t in range(GT):
                        mm = pe.transpose(p_s[0:E + 1, P * t:P * t + P], gate[:, t, :], ident[:, :])
                    mm.then_inc(sm["gate_t"], 1)
                    for n in range(E + 1):
                        down(n)
                        if n + 2 < E + 1:
                            hidden(n + 2)
                        for _ in range(PE_PARTS[n]):
                            next(others, None)

                groups(pe, prepare, mamba, experts)


            @block.scalar
            def _(act):
                act.wait_ge(sm["d_const"], 1)

                def ln_root(g, u):
                    act.wait_ge(sm["ln_var"], g * 2 + u + 1)
                    act.activation(sd[:, :], mv[:, :, 1], ACT.Sqrt, bias=eps1[:, :]).then_inc(sm["ln_sd"], 1)

                def ln_take(g, u):
                    act.wait_ge(sm["ln_t"], g * 2 + u + 1)
                    act.activation((XT, XF)[u][:, 0, :], (p_t, p_x)[u][:, :], ACT.Copy).then_inc(sm["ln_xt_a"], 1)

                def prepare(g):
                    ln_root(g, 0)
                    yield
                    ln_take(g, 0)
                    yield
                    act.wait_ge(sm["dt_neg"], g + 1)
                    act.activation(dtu[:, :, :], dtn[:, :, :], ACT.Exp).then_inc(sm["act_link"], 1)
                    act.wait_ge(sm["act_link"], g + 1)
                    act.activation(dtl[:, :, :], dtu[:, :, :], ACT.Ln, bias=ones[:, :]).then_inc(sm["dt_ln"], 1)
                    for j in range(2):
                        if j:
                            yield
                        act.wait_ge(sm["bc_proj"], g * 2 + j + 1)
                        pj = (p_s, p_t)[j][0:NS, :].rearrange(AL, t=T)
                        act.activation(bc_raw[:, j, :, PAD:], pj, ACT.Copy)
                        act.activation(bc_acc[:, j], pj, ACT.Identity, bias=cb_bc[:, j:j + 1],
                                       scale=cw_bc[:, j, PAD:TAPS]).then_inc(sm["bc_in"], 1)
                    yield
                    for j in range(2):
                        act.wait_ge(sm["bc_conv"], g * 2 + j + 1)
                        act.activation(bc_th[:, j], bc_acc[:, j], ACT.Tanh).then_inc(sm["bc_tanh"], 1)

                def mamba(g):
                    act.wait_ge(sm["f_acc"], g * PER_F + 1)

                    def take_x(c):
                        act.wait_ge(sm["x_proj"], g * CT + c + 1)
                        if c >= 2:
                            act.wait_ge(sm["conv_done"], g * CT + c - 1)
                        if c >= 2:
                            act.wait_ge(sm["xc_done"], g * CT + c - 1)
                        px = p_x[:, :].rearrange(AL, t=T)
                        act.activation(raw[:, c % 2, :, PAD:], px, ACT.Copy)
                        act.activation(acc[:, c % 2], px, ACT.Identity, bias=cb[:, c:c + 1],
                                       scale=cw[:, c, PAD:TAPS]).then_inc(sm["x_acc"], 1)

                    def tanh_z(c):
                        act.wait_ge(sm["z_proj"], g * CT + c + 1)
                        if c >= 2:
                            act.wait_ge(sm["zs_done"], g * CT + c - 1)
                        act.activation(zth[:, c % 2], p_z[:, :], ACT.Tanh, scale=0.5).then_inc(sm["zth_done"], 1)

                    def decays(c):
                        act.wait_ge(sm["seg"], g * CT + c + 1)
                        if c >= 2:
                            act.wait_ge(sm["m_done"], g * CT + c - 1)
                        act.activation(decay[:, c % 2].rearrange("p q h t -> p (q h t)"), p_s[:, :],
                                       ACT.Exp).then_inc(sm["e_done"], 1)

                    def tanh_x(c):
                        act.wait_ge(sm["conv_done"], g * CT + c + 1)
                        if c >= 2:
                            act.wait_ge(sm["xc_done"], g * CT + c - 1)
                        act.activation(th[:, c % 2].rearrange(AL, t=T), acc[:, c % 2], ACT.Tanh).then_inc(sm["th_done"], 1)

                    def square(c):
                        act.wait_ge(sm["yg_done"], g * CT + c + 1)
                        if c >= 2:
                            act.wait_ge(sm["accq_done"], g * CT + c - 1)
                        act.activation(ysq[:, c % 2], yg[:, c % 2], ACT.Square).then_inc(sm["sq_done"], 1)

                    for k in range(CT + 3):
                        if k < CT:
                            take_x(k)
                            tanh_z(k)
                            decays(k)
                            tanh_x(k)
                        if k >= 3:
                            square(k - 3)
                    act.wait_ge(sm["ssq"], g + 1)
                    act.activation(sd[:, :], p_t[:, 0:GT], ACT.Sqrt, bias=eps4[:, :], scale=1.0 / INNER).then_inc(sm["r_sd"], 1)

                def experts(g, others):
                    ln_root(g, 1)
                    ln_take(g, 1)
                    act.wait_ge(sm["logits"], g + 1)
                    act.activation(e_g[:, :, :], p_t[:, 0:GT * E].rearrange("p (q e) -> p q e", e=E), ACT.Exp,
                                   scale=-1.0).then_inc(sm["sig"], 1)
                    for n in range(E + 1):
                        act.wait_ge(sm["h_mm"], g * (E + 1) + n + 1)
                        if n >= 2:
                            act.wait_ge(sm["f_mm"], g * (E + 1) + n - 1)
                        act.activation(hh[:, n % 2], (p_x, p_z)[n % 2][:, :], ACT.Gelu,
                                       bias=b_1[:, order[n]:order[n] + 1]).then_inc(sm["h_done"], 1)
                        for _ in range(ACT_PARTS[n]):
                            next(others, None)

                groups(act, prepare, mamba, experts)

            @block.gpsimd
            def _(pool):
                pool.memset(bc_raw[:, :, :, 0:PAD], 0.0).then_inc(sm["pads"], 1)
                pool.wait_ge(sm["pads"], 1)
                pool.memset(raw[:, :, :, 0:PAD], 0.0)
                pool.memset(gate[:, :, E:E + 1], 1.0).then_inc(sm["d_const"], 1)
                with pool.Fori(0, NG) as g:
                    pool.wait_ge(sm["dt_ready"], g + 1)

                    def make_steps(c):
                        if c >= 2:
                            pool.wait_ge(sm["seg"], g * CT + c - 1)
                        pool.tensor_tensor(steps[:, c % 2],
                                           da[:, :, 2 * c:2 * c + 2].rearrange("p q (h o) -> p q h o", o=1).broadcast_to([P, GT, 2, T]),
                                           tri[:, :].rearrange("p (a b t) -> p a b t", a=1, b=1).broadcast_to([P, GT, 2, T]),
                                           ALU.mult).then_inc(sm["r_done"], 1)

                    def make_mix(c):
                        pool.wait_ge(sm["e_done"], g * CT + c + 1)
                        if c == 0:
                            pool.wait_ge(sm["g_ready"], g + 1)
                        if c >= 2:
                            pool.wait_ge(sm["y_mm"], g * CT + c - 1)
                        pool.tensor_tensor(M[:, c % 2], decay[:, c % 2],
                                           G[:, :, :].rearrange("p q (o t) -> p q o t", o=1).broadcast_to([P, GT, 2, T]),
                                           ALU.mult).then_inc(sm["m_done"], 1)

                    def gate_y(c):
                        pool.wait_ge(sm["y_done"], g * CT + c + 1)
                        if c >= 2:
                            pool.wait_ge(sm["o_mm"], g * CT + c - 1)
                            pool.wait_ge(sm["sq_done"], g * CT + c - 1)
                        pool.tensor_tensor(yg[:, c % 2], y1[:, c % 2], zs[:, c % RING], ALU.mult).then_inc(sm["yg_done"], 1)

                    def sum_squares(c):
                        pool.wait_ge(sm["sq_done"], g * CT + c + 1)
                        if c == 0:
                            pool.tensor_tensor(accq[:, :], ysq[:, 0], zero[:, :].broadcast_to([P, GN]), ALU.add).then_inc(sm["accq_done"], 1)
                        else:
                            pool.wait_ge(sm["accq_done"], g * CT + c)
                            pool.tensor_tensor(accq[:, :], accq[:, :], ysq[:, c % 2], ALU.add).then_inc(sm["accq_done"], 1)

                    make_steps(0)
                    for k in range(CT + 3):
                        if k + 1 < CT:
                            make_steps(k + 1)
                        if k < CT:
                            make_mix(k)
                        if 2 <= k <= CT + 1:
                            gate_y(k - 2)
                        if k >= 3:
                            sum_squares(k - 3)

            @block.vector
            def _(v):
                ch = Chain(v, sm["d_chain"])
                v.memset(spare[:, :], 0.0).then_inc(sm["f_acc"], 1)
                v.wait_ge(sm["f_acc"], 1)
                v.wait_ge(sm["d_const"], 1)

                def xtile(g, t):
                    return X[:, bass.ds(g * GT + t, 1), :].rearrange("p o d -> p (o d)")

                def ln_stats(g):
                    for t in range(GT):
                        ins = v.bn_stats(bn[:, t, :], xtile(g, t))
                    ch.link(ins, bare=True)
                    for t in range(GT):
                        ins = v.bn_aggr(mv[:, t, :], bn[:, t, :])
                    ins.then_inc(sm["ln_var"], 1)

                def ln_rows(g, u):
                    v.wait_ge(sm["ln_sd"], g * 2 + u + 1)
                    ch.link(v.reciprocal(rs[:, :], sd[:, :]))
                    for t in range(GT):
                        v.tensor_scalar(xg[:, t, :], xtile(g, t), mv[:, t, 0:1], rs[:, t:t + 1], ALU.subtract,
                                        ALU.mult).then_inc(sm["ln_rows"], 1)

                def ln_take(g, u):
                    v.wait_ge(sm["ln_t"], g * 2 + u + 1)
                    v.tensor_copy((XT, XF)[u][:, 1, :], (p_s, p_z)[u][:, :]).then_inc(sm["ln_xt_v"], 1)

                def prepare(g):
                    v.wait_ge(sm["spread"], g + 1)
                    for h in range(2):
                        ins = v.tensor_scalar(U[:, h, :], p_t[:, :], row_id[:, h:h + 1], None, ALU.is_ge)
                    ch.link(ins)
                    for h in range(2):
                        ins = v.scalar_tensor_tensor(mask[:, h].rearrange("p b t -> p (b t)"), p_s[:, :], row_id[:, h:h + 1],
                                                     U[:, h, :], ALU.is_le, ALU.mult)
                    ins.then_inc(sm["mask_ready"], 1)
                    yield
                    for t in range(GT):
                        v.wait_ge(sm["expanded"], g * GT + t // 2 * 2 + 2)
                        ins = v.tensor_tensor(xtile(g, t), xtile(g, t), (p_t, p_s)[t // 2][:, D * (t % 2):D * (t % 2) + D], ALU.add)
                    ch.link(ins, bare=True)
                    ln_stats(g)
                    yield
                    ln_rows(g, 0)
                    yield
                    ln_take(g, 0)
                    yield

                    v.wait_ge(sm["dt_logit"], g + 1)
                    ch.link(v.tensor_tensor(dtv[:, :, :], p_t[:, 0:GT * HEADS].rearrange("p (q h) -> p q h", h=HEADS),
                                            dtb[:, :].rearrange("p (o h) -> p o h", o=1).broadcast_to([P, GT, HEADS]), ALU.add))
                    v.scalar_tensor_tensor(dtn[:, :, :], dtv[:, :, :], -1.0, dtv[:, :, :], ALU.mult,
                                           ALU.min).then_inc(sm["dt_neg"], 1)
                    yield
                    v.wait_ge(sm["dt_ln"], g + 1)
                    ch.link(v.tensor_scalar(dtd[:, :, :], dtu[:, :, :], 1.0, -1.0, ALU.add, ALU.add))
                    ch.link(v.tensor_scalar(dte[:, :, :], dtd[:, :, :], 0.0, None, ALU.is_equal))
                    ch.link(v.tensor_tensor(dtd[:, :, :], dtd[:, :, :], dte[:, :, :], ALU.add))
                    ch.link(v.tensor_tensor(dtl[:, :, :], dtl[:, :, :], dte[:, :, :], ALU.add))
                    ch.link(v.reciprocal(dtd[:, :, :], dtd[:, :, :]))
                    ch.link(v.tensor_tensor(dtl[:, :, :], dtl[:, :, :], dtu[:, :, :], ALU.mult))
                    ch.link(v.tensor_tensor(dtl[:, :, :], dtl[:, :, :], dtd[:, :, :], ALU.mult))
                    ch.link(v.scalar_tensor_tensor(dt_[:, :, :], dtv[:, :, :], 0.0, dtl[:, :, :], ALU.max, ALU.add))
                    v.scalar_tensor_tensor(da[:, :, :], dt_[:, :, :], -1.0,
                                           a_exp[:, :].rearrange("p (o h) -> p o h", o=1).broadcast_to([P, GT, HEADS]),
                                           ALU.mult, ALU.mult).then_inc(sm["dt_ready"], 1)

                    for j in range(2):
                        v.wait_ge(sm["bc_in"], g * 2 + j + 1)
                        for k in range(PAD - 1, -1, -1):
                            ins = v.scalar_tensor_tensor(bc_acc[:, j], bc_raw[:, j, :, k:k + T], cw_bc[:, j, k:k + 1],
                                                         bc_acc[:, j], ALU.mult, ALU.add)
                            if k:
                                ch.link(ins)
                        ins.then_inc(sm["bc_conv"], 1)
                    yield
                    for j in range(2):
                        v.wait_ge(sm["bc_tanh"], g * 2 + j + 1)
                        v.scalar_tensor_tensor(BC[:, j], bc_th[:, j], 1.0, bc_acc[:, j], ALU.add,
                                               ALU.mult).then_inc(sm["bc_ready"], 1)
                    yield
                    v.wait_ge(sm["g_mm"], g + 1)
                    v.tensor_tensor(G[:, :, :], p_s[:, 0:GT * T].rearrange("p (q t) -> p q t", t=T),
                                    tri[:, :].rearrange("p (o t) -> p o t", o=1).broadcast_to([P, GT, T]),
                                    ALU.mult).then_inc(sm["g_ready"], 1)

                def mamba(g):
                    def conv(c):
                        v.wait_ge(sm["x_acc"], g * CT + c + 1)
                        for k in range(PAD - 1, -1, -1):
                            a = acc[:, c % 2]
                            ins = v.scalar_tensor_tensor(a, raw[:, c % 2, :, k:k + T], cw[:, c, k:k + 1], a, ALU.mult, ALU.add)
                            if k:
                                ch.link(ins)
                        ins.then_inc(sm["conv_done"], 1)

                    def silu_z(c):
                        v.wait_ge(sm["zth_done"], g * CT + c + 1)
                        if c >= RING:
                            v.wait_ge(sm["yg_done"], g * CT + c - RING + 1)
                        v.scalar_tensor_tensor(zs[:, c % RING], zth[:, c % 2], 1.0, p_z[:, :], ALU.add,
                                               ALU.mult).then_inc(sm["zs_done"], 1)

                    def silu_x(c):
                        v.wait_ge(sm["th_done"], g * CT + c + 1)
                        if c >= RING:
                            v.wait_ge(sm["x_t"], g * CT + c - RING + 1)
                        v.scalar_tensor_tensor(xc[:, c % RING].rearrange(AL, t=T), th[:, c % 2].rearrange(AL, t=T), 1.0,
                                               acc[:, c % 2], ALU.add, ALU.mult).then_inc(sm["xc_done"], 1)

                    def scale_x(c):
                        v.wait_ge(sm["x_t"], g * CT + c + 1)
                        if c >= 2:
                            v.wait_ge(sm["y_mm"], g * CT + c - 1)
                        v.tensor_tensor(xd[:, c % 2], p_t[:, :].rearrange("p (q h d) -> p q h d", q=GT, h=2),
                                        dt_[:, :, 2 * c:2 * c + 2].rearrange("p q (h o) -> p q h o", o=1).broadcast_to([P, GT, 2, HD]),
                                        ALU.mult).then_inc(sm["xd_done"], 1)

                    def skip_x(c):
                        v.wait_ge(sm["y_mm"], g * CT + c + 1)
                        if c >= 2:
                            v.wait_ge(sm["yg_done"], g * CT + c - 1)
                        for b in range(PAIR):
                            xv = xc[:, c % RING].rearrange("p (q b t) -> p q b t", q=GT, b=PAIR)[:, :, b, :]
                            yv = y1[:, c % 2].rearrange("p (q b t) -> p q b t", q=GT, b=PAIR)[:, :, b, :]
                            ins = v.scalar_tensor_tensor(yv, xv, d_ch[:, c:c + 1],
                                                         (p_y0, p_y1)[b][:, 0:GT * T].rearrange("p (q t) -> p q t", t=T),
                                                         ALU.mult, ALU.add)
                        ins.then_inc(sm["y_done"], 1)

                    for k in range(CT + 3):
                        if k < CT:
                            conv(k)
                            silu_z(k)
                        if 1 <= k <= CT:
                            scale_x(k - 1)
                        if k < CT:
                            silu_x(k)
                        if 2 <= k <= CT + 1:
                            skip_x(k - 2)
                    v.wait_ge(sm["r_sd"], g + 1)
                    ch.link(v.reciprocal(rs[:, :], sd[:, :]))
                    v.wait_ge(sm["o_mm"], g * CT + CT)
                    for t in range(GT):
                        ins = v.scalar_tensor_tensor(xtile(g, t), (p_o0, p_o1)[t // 2][:, D * (t % 2):D * (t % 2) + D],
                                                     rs[:, t:t + 1], xtile(g, t), ALU.mult, ALU.add)
                    ch.link(ins, bare=True)
                    ln_stats(g)

                def experts(g, others):
                    ln_rows(g, 1)
                    ln_take(g, 1)
                    v.wait_ge(sm["sig"], g + 1)
                    ch.link(v.tensor_scalar(e_g[:, :, :], e_g[:, :, :], 1.0, None, ALU.add))
                    ch.link(v.reciprocal(e_g[:, :, :], e_g[:, :, :]))
                    ch.link(v.tensor_scalar(sc[:, :, :], e_g[:, :, :], rsc[:, 0:1], None, ALU.mult))
                    mine = sc[:, :, :].rearrange("p q (e o) -> p q e o", o=1).broadcast_to([P, GT, E, E])
                    other = sc[:, :, :].rearrange("p q (o f) -> p q o f", o=1).broadcast_to([P, GT, E, E])
                    v.tensor_tensor(cmp_[:, :, :, :], other, mine, ALU.is_equal).then_inc(sm["d_chain"], 1)
                    ch.n += 1
                    ch.link(v.tensor_tensor(cmp2[:, :, :, :], other, mine, ALU.is_gt))
                    ch.link(v.tensor_tensor(cmp_[:, :, :, :], cmp_[:, :, :, :],
                                            below[:, :, :].rearrange("p (o e) f -> p o e f", o=1).broadcast_to([P, GT, E, E]), ALU.mult))
                    ch.link(v.tensor_tensor(cmp_[:, :, :, :], cmp_[:, :, :, :], cmp2[:, :, :, :], ALU.add))
                    ch.link(v.tensor_reduce(cnt[:, :, :], cmp_[:, :, :, :], AX_X, ALU.add))
                    ch.link(v.scalar_tensor_tensor(e_g[:, :, :], cnt[:, :, :], 2.0, sc[:, :, :], ALU.is_lt, ALU.mult))
                    ch.link(v.tensor_reduce(tot[:, :], e_g[:, :, :], AX_X, ALU.add))
                    ch.link(v.reciprocal(tot[:, :], tot[:, :]))
                    v.tensor_tensor(gate[:, :, 0:E], e_g[:, :, :],
                                    tot[:, :].rearrange("p (q o) -> p q o", o=1).broadcast_to([P, GT, E]),
                                    ALU.mult).then_inc(sm["gate_ready"], 1)
                    v.wait_ge(sm["gate_t"], g + 1)
                    v.tensor_copy(gT[:, :], p_s[0:E + 1, :]).then_inc(sm["gt_ready"], 1)

                    for n in range(E + 1):
                        v.wait_ge(sm["f_mm"], g * (E + 1) + n + 1)
                        banks = ((p_y0, p_y1), (p_o0, p_o1))[n % 2]
                        if n == 0:
                            for h in range(2):
                                xx = X[:, bass.ds(g * GT + 2 * h, 2), :]
                                v.tensor_tensor(xx, xx, banks[h][:, :].rearrange("p (q d) -> p q d", q=2),
                                                ALU.add).then_inc(sm["f_acc"], 1)
                            v.wait_ge(sm["f_acc"], g * PER_F + 2 + 1)
                        for t in range(GT if n else 0):
                            if n >= 2:
                                v.wait_ge(sm["f_acc"], g * PER_F + 2 + GT * (n - 2) + t + 1 + 1)
                            v.scalar_tensor_tensor(xtile(g, t), banks[t // 2][:, D * (t % 2):D * (t % 2) + D],
                                                   gate[:, t, order[n]:order[n] + 1], xtile(g, t), ALU.mult,
                                                   ALU.add).then_inc(sm["f_acc"], 1)
                        for _ in range(DVE_PARTS[n]):
                            next(others, None)

                groups(v, prepare, mamba, experts, ch, CHAIN_D)


_INS = ["x", "ctx_1024", "L0_attn_W_in", "L0_attn_conv_w", "L0_attn_conv_b", "L0_attn_A_log", "L0_attn_D_param",
        "L0_attn_dt_bias", "L0_attn_norm_w", "L0_attn_W_out", "L0_ffn_gate_W", "L0_ffn_W1", "L0_ffn_b1", "L0_ffn_W2",
        "L0_ffn_b2", "L0_ffn_Ws1", "L0_ffn_bs1", "L0_ffn_Ws2", "L0_ffn_bs2", "L0_ffn_route_scale"]


def kernel(**inputs):
    import numpy as _np
    import concourse.bacc as _bacc
    from concourse import mybir as _mybir
    from concourse.bass_utils import run_bass_kernel_spmd as _run

    nc = _bacc.Bacc("TRN2", target_bir_lowering=False, num_devices=1)
    arrays, args = {}, []
    for name in _INS:
        a = _np.ascontiguousarray(inputs[name])
        if name == "L0_ffn_route_scale":
            a = a.reshape(1)
        arrays[f"in_{name}_dram"] = a
        args.append(nc.dram_tensor(f"in_{name}_dram", a.shape, _mybir.dt.from_np(a.dtype), kind="ExternalInput").ap())
    args.append(nc.dram_tensor("out_dram", (NB, T, D), F32, kind="ExternalOutput").ap())
    perceiver(nc, *args)
    r = _run(nc, [arrays], core_ids=[0])
    return r.results[0]["out_dram"]
```

```python
from contextlib import ExitStack

import concourse.bass as bass
from concourse import mybir

F32 = mybir.dt.float32
F16 = mybir.dt.float16
F32R = mybir.dt.float32r
ALU = mybir.AluOpType
ACT = mybir.ActivationFunctionType
AX_X = mybir.AxisListType.X

P = 128
NB, T, D = 32, 64, 256
S = 256
KC = D // P
NT = NB * T // P
PAIR = P // T
EPS = 1e-5

BLOCKS = 4
BI = S // BLOCKS
CHUNK = 4
SLOTS = T + CHUNK * (BLOCKS - 1)
CHUNKS = SLOTS // CHUNK
TABLE = 80
BIG = 1e30

GT = 4
NG = NT // GT
GB = GT * PAIR
GN = GT * P
HEADS, HD, NS, TAPS = 32, 64, 64, 4
INNER = HEADS * HD
CT = INNER // P
PROJ = 2 * INNER + 2 * NS + HEADS
E, H = 8, 128
ER = 3
REST = PROJ - 2 * INNER
PIECE = 512
IN_PIECES = KC * (2 * INNER // PIECE)
PIECES = IN_PIECES + 1 + E + 1
RAW = 4
LR = 2
PAD = TAPS - 1
RING = 3
CR = 4
N_W = 16
CHAIN_D = 66


def perceiver(nc, x, ctx_rows, W_in, conv_w, conv_b, A_log, D_param, dt_bias, norm_w, W_out,
              gate_W, W1, b1, W2, b2, Ws1, bs1, Ws2, bs2, route_scale, out):
    x_rows = x.rearrange("b t d -> (b t) d").rearrange("(n p) d -> p n d", p=P)
    out_rows = out.rearrange("b t d -> (b t) d").rearrange("(n p) d -> p n d", p=P)
    ctx_tiles = ctx_rows.rearrange("b (h p) d -> p b h d", p=P)
    dist = nc.dram_tensor("distances", (NB, T, S), F32, kind="Internal").ap()
    w_low = nc.dram_tensor("w_low", (CT, P, 2, KC, P), F32, kind="Internal").ap()
    e_upper = nc.dram_tensor("e_upper", (P, E + 1, 2, D), F32, kind="Internal").ap()
    e_lower = nc.dram_tensor("e_lower", (E + 1, P, 2, D), F32, kind="Internal").ap()
    dist_rows = dist.rearrange("b j i -> (b j) i")

    with ExitStack() as ctx:
        def sb(name, shape, dt=F32):
            return ctx.enter_context(nc.sbuf_tensor(name, shape, dt))

        def sem(name):
            return ctx.enter_context(nc.semaphore(name))

        bank = [ctx.enter_context(nc.psum_tensor(f"bank{i}", [P, 512], F32)) for i in range(8)]
        p_x, p_z, p_t, p_s, p_y0, p_y1, p_o0, p_o1 = bank

        ident = sb("ident", [P, P])
        tri = sb("tri", [P, T])
        later = sb("later", [P, P], F32R)
        ones = sb("ones", [P, 1])
        zero = sb("zero", [P, 1])
        spare = sb("spare", [P, 1])
        ones16 = sb("ones16", [NB, P], F16)
        below = sb("below", [P, E, E])
        row_id = sb("row_id", [P, KC])
        eps1 = sb("eps1", [P, 1])
        eps4 = sb("eps4", [P, 1])
        lookup_id = sb("lookup_id", [NB, S])

        w_in = sb("w_in", [P, KC, PROJ], F32R)
        w_rest = sb("w_rest", [P, KC, REST], F32R)
        w_out = sb("w_out", [P, CT, D])
        b_1 = sb("b_1", [P, E + 1])
        b_2 = sb("b_2", [E + 1, D])
        w_gate = sb("w_gate", [P, KC, E])
        w_gate_up = sb("w_gate_up", [P, KC, E], F32R)
        w_gate_low = sb("w_gate_low", [P, KC, E], F32R)
        cw = sb("cw", [P, CT, TAPS])
        cb = sb("cb", [P, CT])
        cw_bc = sb("cw_bc", [2 * NS, TAPS])
        cb_bc = sb("cb_bc", [2 * NS, 1])
        d_ch = sb("d_ch", [P, CT])
        nw = sb("nw", [P, CT])
        a_exp = sb("a_exp", [P, HEADS])
        dtb = sb("dtb", [P, HEADS])
        rsc = sb("rsc", [P, 1])

        X = sb("X", [P, NT, D])
        bn = sb("bn", [P, 2, GT, 6])
        mv = sb("mv", [P, 2, GT, 2])
        sd = sb("sd", [P, 3, GT])
        rs = sb("rs", [P, 3, GT])
        cr = sb("cr", [P, CR, PAIR, 2, D])
        Hpath = sb("Hpath", [NB, T + 1])
        Hd = sb("Hd", [NB, NB, T + 1], F16)

        s_const = sem("s_const")
        s_ident = sem("s_ident")
        s_x = [sem(f"s_x{q}") for q in range(4)]
        s_w = sem("s_w")
        s_we = sem("s_we")
        s_table = sem("s_table")
        s_path = sem("s_path")
        dist_out = [sem(f"dist_out{k}") for k in range(2)]
        ctx_in = [sem(f"ctx_in{k}") for k in range(CR)]
        act_done = sem("act_done")
        dve_done = sem("dve_done")
        pool_done = sem("pool_done")
        a_sd = sem("a_sd")
        a_norm = sem("a_norm")
        a_rows_t = sem("a_rows_t")
        a_x_t = sem("a_x_t")
        a_c_t = sem("a_c_t")
        a_c = [sem(f"a_c{b}") for b in range(PAIR)]
        a_mm = sem("a_mm")
        a_sq = sem("a_sq")
        a_clamp = sem("a_clamp")
        a_root = sem("a_root")
        a_aa = sem("a_aa")
        a_aa_act = sem("a_aa_act")
        raw_in = [sem(f"raw_in{k}") for k in range(RAW)]
        half_out = [sem(f"half_out{k}") for k in range(2)]
        w_upper = sem("w_upper")
        w_lower = sem("w_lower")
        dist_in = [sem(f"dist_in{q}") for q in range(4)]
        b_scan = sem("b_scan")
        b_step = sem("b_step")

        class Chain:
            def __init__(self, engine, sem_):
                self.engine, self.sem, self.base, self.n = engine, sem_, 0, 0

            def link(self, ins, bare=False):
                ins.then_inc(self.sem, 1)
                self.n += 1
                self.engine.wait_ge(self.sem, self.base + self.n)
                if bare:
                    self.engine.memset(spare[:, :], 0.0)

            def enter(self, i, per):
                self.start, self.per = self.base + self.n, per
                self.base, self.n = self.start + i * per, 0

            def leave(self, count):
                assert self.n == self.per, (self.n, self.per)
                self.base, self.n = self.start + count * self.per, 0

        def wait(engine, sem_, value):
            if not isinstance(value, int) or value > 0:
                engine.wait_ge(sem_, value)

        def carrier(pe, psum):
            pe.matmul(psum[:, 0:1], lhsT=ones16[:, :], rhs=ones16[:, 0:1], start=True, stop=True)

        def keep_warm(pe, n):
            for _ in range(n):
                pe.matmul(p_y1[:, :], lhsT=later[:, :], rhs=w_in[:, 0, 0:512], start=True, stop=True)

        inner = ExitStack()
        with inner:
            def tb(name, shape, dt=F32):
                return inner.enter_context(nc.sbuf_tensor(name, shape, dt))

            later_f = tb("later_f", [P, P])
            xn = tb("a_xn", [P, 2, D])
            sq = tb("a_sqj", [P, D])
            sqd = tb("a_sqd", [P, 2 * PAIR, D])
            bn_a = tb("bn_a", [P, NT, 6])
            mv_a = tb("mv_a", [P, NT, 2])
            sd_a = tb("sd_a", [P, NT])
            rs_a = tb("rs_a", [P, NT])
            bb = tb("a_bb", [P, NT])
            aa = tb("a_aa_t", [P, CR, PAIR, 2])
            xt = tb("a_xt", [P, 2, KC, P])
            ct_t = tb("a_ct", [P, 2, PAIR, KC, S])
            dd = tb("a_dd", [P, 2, S])
            ds = tb("a_ds", [P, 2, S])
            Dk = tb("Dk", [P, SLOTS, BI])
            dn_view = Dk[:, :, :].rearrange("p s i -> p (s i)").bitcast(F16)
            R = tb("R", [P, SLOTS + 1, BI + 1])
            m1 = tb("m1", [P, BI])
            qk = tb("qk", [P, CHUNK, BI], F16)
            rk = tb("rk", [P, CHUNK, BI], F16)
            ak = tb("ak", [P, CHUNK, BI], F16)
            ek = tb("ek", [P, CHUNK, BI], F16)
            blk_id = tb("blk_id", [P, CHUNK, BI], F16)
            Wk = tb("Wk", [P, CHUNK, BI + 1], F16)
            Nk = tb("Nk", [P, CHUNK, BI + 1], F16)
            mk = tb("mk", [P, CHUNK, BI + 1], F16)
            table = tb("table", [NB, BLOCKS * TABLE * BI], F16)
            junk = tb("junk", [NB, BLOCKS, BI])
            tab = table[:, :].rearrange("b (g j i) -> b g j i", g=BLOCKS, j=TABLE)

            slot = cr[:, :].rearrange("p r b h d -> p (r b) (h d)")
            assert CR * PAIR == RAW + 4

            def piece_views(i):
                raw_piece, upper, lower = slot[:, i % RAW, :], slot[:, RAW + i % 2, :], slot[:, RAW + 2 + i % 2, :]
                if i < IN_PIECES:
                    c, o = piece_columns(i)
                    return raw_piece, w_in[:, c, o:o + PIECE], lower
                if i == IN_PIECES:
                    raw_piece = raw_piece[:, 0:KC * REST].rearrange("p (c n) -> p c n", c=KC)
                    return raw_piece, w_in[:, :, 2 * INNER:PROJ], w_rest[:, :, :]
                return raw_piece, upper.bitcast(F32R), lower

            def piece_columns(i):
                return i % KC, i // KC * PIECE

            def loads(i):
                return 1 if i <= IN_PIECES else 2

            def stores(i):
                return 1 if i < IN_PIECES else 0 if i == IN_PIECES else 2

            def total(count, i, ring):
                return sum(count(k) for k in range(i % ring, i + 1, ring))

            a_it = NT // CR

            def ahead(engine, fetch, finish):
                def tiles(it, last=False):
                    for k in range(CR):
                        n = it * CR + k
                        if not (last and k == CR - 1):
                            fetch(n + 1, (k + 1) % CR, it + (k + 1) // CR)
                        finish(n, k)

                fetch(0, 0, 0)
                tiles(0)
                with engine.Fori(1, a_it - 1) as it:
                    tiles(it)
                tiles(a_it - 1, last=True)

            def stores_before(n, par):
                return (n - par) * 8

            with nc.Block() as block:
                @block.gpsimd
                def _(pool):
                    ch = Chain(pool, pool_done)
                    ch.link(pool.memset(eps1[:, :], EPS))
                    ch.link(pool.memset(ident[:, :], 0.0))
                    pool.affine_select(out=ident[:, :], in_=ident[:, :], compare_op=ALU.not_equal,
                                       fill=1.0, base=0, pattern=[[-1, P]], channel_multiplier=1).then_inc(s_ident, 1)
                    ch.link(pool.memset(ones[:, :], 1.0))
                    ch.link(pool.memset(zero[:, :], 0.0))
                    ch.link(pool.memset(ones16[:, :], 1.0))
                    ch.link(pool.memset(eps4[:, :], 4 * EPS))
                    ch.link(pool.memset(tri[:, :], 1.0))
                    ch.link(pool.memset(later_f[:, :], 0.0))
                    ch.link(pool.memset(below[:, :, :], 1.0))
                    for h in range(PAIR):
                        q = slice(T * h, T * h + T)
                        ch.link(pool.affine_select(out=tri[q, :], in_=tri[q, :], compare_op=ALU.is_ge,
                                                   fill=0.0, base=0, pattern=[[1, T]], channel_multiplier=-1))
                        ch.link(pool.affine_select(out=later_f[q, q], in_=later_f[q, q], compare_op=ALU.is_ge,
                                                   fill=1.0, base=0, pattern=[[1, T]], channel_multiplier=-1))
                    ch.link(pool.affine_select(out=below[:, :, :], in_=below[:, :, :], compare_op=ALU.is_gt,
                                               fill=0.0, base=0, pattern=[[1, E], [-1, E]], channel_multiplier=0))
                    for h in range(KC):
                        ch.link(pool.iota(row_id[:, h:h + 1], pattern=[[0, 1]], base=P * h, channel_multiplier=1,
                                          allow_small_or_imprecise_dtypes=True))
                    ch.link(pool.iota(lookup_id[:, :], pattern=[[1, S]], base=0, channel_multiplier=0,
                                      allow_small_or_imprecise_dtypes=True))
                    for g in range(BLOCKS):
                        q = slice(32 * g, 32 * g + 32)
                        ch.link(pool.iota(blk_id[q, :, :], pattern=[[0, CHUNK], [1, BI]], base=BI * g,
                                          channel_multiplier=0, allow_small_or_imprecise_dtypes=True))
                        if g:
                            ch.link(pool.memset(Dk[q, 0:CHUNK * g, :], BIG))
                        if g < BLOCKS - 1:
                            ch.link(pool.memset(Dk[q, CHUNK * g + T:SLOTS, :], BIG))
                    ch.link(pool.memset(R[:, 0, :], BIG))
                    ch.link(pool.memset(R[:, 1:SLOTS + 1, 0:1], BIG))
                    ch.link(pool.memset(R[0:NB, 0, 0:1], 0.0))
                    ch.link(pool.memset(Wk[:, :, 0:1], 0.0))
                    ch.link(pool.memset(mk[:, :, :], 1.0))
                    ch.link(pool.memset(mk[:, :, 0:1], 0.0))
                    ch.link(pool.memset(Hpath[:, 0:1], 0.0))
                    pool.memset(Hpath[:, T:T + 1], float(S - 1)).then_inc(s_const, 1)
                    for i in range(PIECES):
                        raw_piece, upper, lower = piece_views(i)
                        pool.wait_ge(w_upper, i + 1)
                        if i >= 2:
                            pool.wait_ge(half_out[i % 2], 16 * total(stores, i - 2, 2))
                        pool.tensor_tensor(lower, raw_piece, upper.bitcast(F32), ALU.subtract).then_inc(w_lower, 1)

                @block.sync
                def _(sp):
                    def tokens(q):
                        t = slice(NT // 4 * q, NT // 4 * q + NT // 4)
                        sp.dma_start(X[:, t, :], x_rows[:, t, :]).then_inc(s_x[q], 16)

                    def load(n, k, before):
                        wait(sp, ctx_in[k], before * 16)
                        wait(sp, a_c_t, (n - CR + 1) * 2)
                        wait(sp, a_mm, n - CR + 1)
                        sp.dma_start(cr[:, k], ctx_tiles[:, bass.ds(n * PAIR, PAIR)]).then_inc(ctx_in[k], 16)

                    def weights():
                        def ld(dst, src):
                            sp.dma_start(dst, src, allow_slow_non_contiguous=True).then_inc(s_w, 16)
                            return 1
                        n = ld(w_out[:, :, :], W_out.rearrange("(c p) n -> p c n", p=P))
                        n += ld(b_1[:, 0:E], b1.rearrange("e h -> h e"))
                        n += ld(b_1[:, E:E + 1], bs1.rearrange("(h o) -> h o", o=1))
                        n += ld(b_2[0:E, :], b2)
                        n += ld(b_2[E:E + 1, :], bs2.rearrange("(o d) -> o d", o=1))
                        n += ld(w_gate[:, :, :], gate_W.rearrange("(c p) e -> p c e", p=P))
                        cwf = conv_w.rearrange("c o k -> c (o k)")
                        n += ld(cw[:, :, :], cwf[0:INNER, :].rearrange("(c p) k -> p c k", p=P))
                        n += ld(cb[:, :], conv_b[0:INNER].rearrange("(c p) -> p c", p=P))
                        n += ld(cw_bc[:, :], cwf[INNER:, :])
                        n += ld(cb_bc[:, :], conv_b[INNER:].rearrange("(p o) -> p o", o=1))
                        for h in range(2):
                            n += ld(d_ch[HD * h:HD * h + HD, :],
                                    D_param.rearrange("(c h) -> h c", h=2)[h:h + 1, :].broadcast_to([HD, CT]))
                        n += ld(nw[:, :], norm_w.rearrange("(c p) -> p c", p=P))
                        n += ld(a_exp[:, :], A_log.rearrange("(o h) -> o h", o=1).broadcast_to([P, HEADS]))
                        n += ld(dtb[:, :], dt_bias.rearrange("(o h) -> o h", o=1).broadcast_to([P, HEADS]))
                        n += ld(rsc[:, :], route_scale.rearrange("(o h) -> o h", o=1).broadcast_to([P, 1]))
                        return n

                    def store(n, par):
                        wait(sp, a_root, n + 1)
                        sp.dma_start(dist_rows[bass.ds(n * P, P), :], ds[:, par, :]).then_inc(dist_out[par], 16)

                    for q in range(4):
                        tokens(q)
                        if q == 0:
                            load(0, 0, 0)
                    for k in range(1, CR):
                        load(k, k, 0)
                    with sp.Fori(0, a_it - 1) as it:
                        for k in range(CR):
                            load((it + 1) * CR + k, k, it + 1)
                            store(it * CR + k, k % 2)
                    for k in range(CR):
                        store((a_it - 1) * CR + k, k % 2)
                    for par in range(2):
                        sp.wait_ge(dist_out[par], 16 * NT // 2)
                    sp.wait_ge(s_const, 1)
                    quarter = T // 4
                    for q in range(4):
                        for g in range(BLOCKS):
                            sp.dma_start(Dk[32 * g:32 * g + 32, CHUNK * g + quarter * q:CHUNK * g + quarter * q + quarter, :],
                                         dist[:, quarter * q:quarter * q + quarter, BI * g:BI * g + BI]
                                         ).then_inc(dist_in[q], 16)
                    assert weights() == N_W
                    def look_ups(c, n):
                        sp.wait_ge(b_step, c + n)
                        for g in range(BLOCKS):
                            steps_ = dn_view[32 * g:32 * g + 32, bass.ds(c * (2 * CHUNK * BI), 2 * n * CHUNK * BI)]
                            dst = table[:, bass.ds((g * TABLE - g * CHUNK + c * CHUNK) * BI, n * CHUNK * BI)]
                            sp.dma_start(dst.rearrange("b (u w) -> b u w", u=n),
                                         steps_.rearrange("b (u w) -> b u w", u=n)[:, :, 0:CHUNK * BI]).then_inc(s_table, 16)

                    with sp.Fori(0, CHUNKS // 2) as c:
                        look_ups(c * 2, 2)
                    assert CHUNKS % 2 == 1
                    look_ups(CHUNKS - 1, 1)
                    sp.wait_ge(s_w, 16 * N_W)

                path_near = 0

                @block.vector
                def _(v):
                    nonlocal path_near
                    ch = Chain(v, dve_done)
                    for t in range(NT):
                        if t % (NT // 4) == 0:
                            v.wait_ge(s_x[t // (NT // 4)], 16)
                        v.bn_stats(bn_a[:, t, :], X[:, t, :]).then_inc(dve_done, 1)
                        ch.n += 1
                    v.wait_ge(dve_done, ch.n)
                    for t in range(NT - 1):
                        v.bn_aggr(mv_a[:, t, :], bn_a[:, t, :])
                    v.bn_aggr(mv_a[:, NT - 1, :], bn_a[:, NT - 1, :]).then_inc(a_norm, 1)
                    v.wait_ge(a_sd, 1)
                    ch.link(v.reciprocal(rs_a[:, :], sd_a[:, :]))

                    def normalise(n, par):
                        wait(v, a_x_t, n - 1)
                        wait(v, a_sq, n - 1)
                        v.tensor_scalar(xn[:, par, :], X[:, bass.ds(n, 1), :].rearrange("p o d -> p (o d)"),
                                        mv_a[:, bass.ds(n, 1), 0:1].rearrange("p o d -> p (o d)"),
                                        rs_a[:, bass.ds(n, 1)], ALU.subtract, ALU.mult).then_inc(a_rows_t, 1)

                    def fetch(n, k, inside):
                        par = k % 2
                        v.wait_ge(a_c_t, n * 2 + 1)
                        wait(v, a_mm, n - 1)
                        v.tensor_copy(ct_t[:, par, 0].rearrange("p c i -> p (c i)"), bank[2][:, :]).then_inc(a_c[0], 1)
                        v.wait_ge(ctx_in[k], inside * 16 + 16)
                        wait(v, a_mm, n - CR + 1)
                        wait(v, a_aa, n)
                        for h in range(2):
                            ins = v.tensor_tensor_reduce(sqd[:, h, :], cr[:, k, 0, h, :], cr[:, k, 0, h, :], 1.0, 0.0,
                                                         ALU.mult, ALU.add, aa[:, k, 0, h:h + 1])
                        ins.then_inc(a_aa, 1)
                        if not isinstance(n, int) or n + 1 < NT:
                            normalise(n + 1, 1 - par)

                    def clamp(n, k):
                        par = k % 2
                        v.wait_ge(a_mm, n + 1)
                        v.wait_ge(a_sq, n + 1)
                        wait(v, a_root, n - 1)
                        v.tensor_scalar(dd[:, par, :], bank[4 + par][:, 0:S], bb[:, bass.ds(n, 1)], 0.0,
                                        ALU.add, ALU.max).then_inc(a_clamp, 1)

                    normalise(0, 0)
                    ahead(v, fetch, clamp)

                    v.wait_ge(s_const, 1)
                    def do(ins):
                        ins.then_inc(dve_done, 1)
                        ch.n += 1
                        return ch.n

                    def need(count):
                        v.wait_ge(dve_done, count)

                    def choices(c):
                        left = R[:, c * CHUNK:c * CHUNK + CHUNK, 1:BI + 1]
                        diag = R[:, c * CHUNK:c * CHUNK + CHUNK, 0:BI]
                        up = R[:, c * CHUNK + 1:c * CHUNK + 1 + CHUNK, 0:BI]
                        q = do(v.tensor_tensor(qk[:, :, :], up, left, ALU.is_gt))
                        yield
                        r = do(v.tensor_tensor(rk[:, :, :], up, diag, ALU.is_ge))
                        yield
                        a = do(v.tensor_tensor(ak[:, :, :], diag, left, ALU.is_le))
                        yield
                        need(r)
                        q = do(v.tensor_tensor(qk[:, :, :], qk[:, :, :], rk[:, :, :], ALU.max))
                        yield
                        need(a)
                        e = do(v.scalar_tensor_tensor(ek[:, :, :], ak[:, :, :], -0.5, blk_id[:, :, :], ALU.mult, ALU.add))
                        yield
                        need(e)
                        w = do(v.tensor_tensor(Wk[:, :, 1:BI + 1], qk[:, :, :], ek[:, :, :], ALU.mult))
                        yield
                        need(w)
                        n = do(v.tensor_tensor_scan(Nk[:, :, :].rearrange("p c i -> p (c i)"),
                                                    mk[:, :, :].rearrange("p c i -> p (c i)"),
                                                    Wk[:, :, :].rearrange("p c i -> p (c i)"), 0.0, ALU.mult, ALU.max))
                        yield
                        need(n)
                        dst = dn_view[:, c * (2 * CHUNK * BI):c * (2 * CHUNK * BI) + CHUNK * BI]
                        v.tensor_tensor(dst.rearrange("p (c i) -> p c i", i=BI), Nk[:, :, 1:BI + 1], Nk[:, :, 0:BI],
                                        ALU.subtract).then_inc(b_step, 1)
                        if c < CHUNKS - 1:
                            for g in range(BLOCKS - 1):
                                do(v.tensor_copy(Wk[32 * g + 32:32 * g + 64, :, 0:1], Nk[32 * g:32 * g + 32, :, BI:BI + 1]))
                        yield

                    moves, row = iter(()), 0
                    for c in range(CHUNKS):
                        if c * CHUNK % (T // 4) == 0 and c * CHUNK < T:
                            v.wait_ge(dist_in[c * CHUNK // (T // 4)], 16 * BLOCKS)
                        for u in range(CHUNK):
                            s = c * CHUNK + u
                            if row:
                                need(row)
                            low = do(v.tensor_tensor(m1[:, :], R[:, s, 0:BI], R[:, s, 1:BI + 1], ALU.min))
                            next(moves, None)
                            need(low)
                            row = do(v.tensor_tensor_scan(R[:, s + 1, 1:BI + 1], m1[:, :], Dk[:, s, :], R[:, s + 1, 0:1],
                                                          ALU.min, ALU.add))
                            next(moves, None)
                        if c < CHUNKS - 1:
                            need(row)
                            for g in range(BLOCKS - 1):
                                row = do(v.tensor_copy(R[32 * g + 32:32 * g + 64, (c + 1) * CHUNK + 1:(c + 2) * CHUNK + 1, 0:1],
                                                       R[32 * g:32 * g + 32, c * CHUNK + 1:(c + 1) * CHUNK + 1, BI:BI + 1]))
                        moves = choices(c)
                    need(row)
                    for _ in moves:
                        pass

                    v.wait_ge(s_w, 16 * N_W)
                    for w in (cw[:, :, :], cb[:, :], cw_bc[:, :], cb_bc[:, :]):
                        v.tensor_scalar(w, w, 0.5, None, ALU.mult)
                    for c in range(CT):
                        v.tensor_scalar(w_out[:, c, :], w_out[:, c, :], nw[:, c:c + 1], None, ALU.mult)
                    v.tensor_copy(later[:, :], later_f[:, :])
                    ch.link(v.tensor_copy(w_gate_up[:, :, :], w_gate[:, :, :]))
                    v.tensor_tensor(w_gate_low[:, :, :], w_gate[:, :, :], w_gate_up[:, :, :].bitcast(F32), ALU.subtract)

                    v.wait_ge(s_table, 16 * BLOCKS * (CHUNKS // 2 + 1))
                    for j in range(T - 1, 0, -1):
                        if j == 12:
                            path_near = ch.n
                        ch.link(v.scalar_tensor_tensor(junk[:, :, :], lookup_id[:, :].rearrange("b (g i) -> b g i", g=BLOCKS),
                                                       Hpath[:, j + 1:j + 2], tab[:, :, j, :], ALU.is_le, ALU.mult,
                                                       accum_out=Hpath[:, j:j + 1]))
                    v.tensor_tensor(Hd[:, :, :],
                                    Hpath[:, :].rearrange("b (o j) -> b o j", o=1).broadcast_to([NB, NB, T + 1]),
                                    ident[0:NB, 0:NB].rearrange("b (c o) -> b c o", o=1).broadcast_to([NB, NB, T + 1]),
                                    ALU.mult).then_inc(s_path, 1)

                @block.scalar
                def _(act):
                    act.wait_ge(a_norm, 1)
                    act.wait_ge(s_ident, 1)
                    act.activation(sd_a[:, :], mv_a[:, :, 1], ACT.Sqrt, bias=eps1[:, :]).then_inc(a_sd, 1)

                    def fetch(n, k, inside):
                        par = k % 2
                        act.wait_ge(a_rows_t, n + 1)
                        wait(act, a_sq, n)
                        act.activation(sq[:, :], xn[:, par, :], ACT.Square, accum_out=bb[:, bass.ds(n, 1)]).then_inc(a_sq, 1)
                        act.wait_ge(a_x_t, n + 1)
                        wait(act, a_mm, n - 1)
                        act.activation(xt[:, par].rearrange("p c i -> p (c i)"), bank[par][:, 0:KC * P], ACT.Copy,
                                       scale=-2.0).then_inc(act_done, 1)
                        act.wait_ge(a_c_t, n * 2 + 2)
                        act.activation(ct_t[:, par, 1].rearrange("p c i -> p (c i)"), bank[3][:, :], ACT.Copy).then_inc(a_c[1], 1)
                        act.wait_ge(ctx_in[k], inside * 16 + 16)
                        wait(act, a_mm, n - CR + 1)
                        wait(act, a_aa_act, n)
                        for h in range(2):
                            ins = act.activation(sqd[:, 2 + h, :], cr[:, k, 1, h, :], ACT.Square, accum_out=aa[:, k, 1, h:h + 1])
                        ins.then_inc(a_aa_act, 1)

                    def root(n, k):
                        par = k % 2
                        act.wait_ge(a_clamp, n + 1)
                        wait(act, dist_out[par], stores_before(n, par))
                        act.activation(ds[:, par, :], dd[:, par, :], ACT.Sqrt).then_inc(a_root, 1)

                    ahead(act, fetch, root)

                    def load_piece(i):
                        dst, sem_ = piece_views(i)[0], raw_in[i % RAW]
                        src = W_in.rearrange("(c p) n -> p c n", p=P)
                        if i < IN_PIECES:
                            c, o = piece_columns(i)
                            act.dma_start(dst, src[:, c, o:o + PIECE]).then_inc(sem_, 16)
                        elif i == IN_PIECES:
                            act.dma_start(dst, src[:, :, 2 * INNER:PROJ]).then_inc(sem_, 16)
                        else:
                            e = i - IN_PIECES - 1
                            up, down = (W1[e], W2[e]) if e < E else (Ws1, Ws2)
                            act.dma_start(dst[:, 0:D].rearrange("p (c h) -> p c h", c=KC),
                                          up.rearrange("(c p) h -> p c h", p=P)).then_inc(sem_, 16)
                            act.dma_start(dst[:, D:2 * D], down).then_inc(sem_, 16)

                    def store_piece(i):
                        raw_piece, upper, lower = piece_views(i)
                        act.wait_ge(w_lower, i + 1)
                        if i < IN_PIECES:
                            c, o = piece_columns(i)
                            which, first = o // INNER, o % INNER // P
                            act.dma_start(w_low[first:first + PIECE // P, :, which, c, :].rearrange("u p n -> p u n"),
                                          lower.rearrange("p (u n) -> p u n", n=P)).then_inc(half_out[i % 2], 16)
                        elif i > IN_PIECES:
                            e = i - IN_PIECES - 1
                            act.dma_start(e_upper[:, e].rearrange("p a d -> p (a d)"),
                                          upper.bitcast(F32)).then_inc(half_out[i % 2], 16)
                            act.dma_start(e_lower[e].rearrange("p a d -> p (a d)"), lower).then_inc(half_out[i % 2], 16)

                    act.wait_ge(a_mm, NT)
                    for i in range(RAW):
                        load_piece(i)
                    for i in range(PIECES + 1):
                        if i < PIECES:
                            raw_piece, upper, _ = piece_views(i)
                            act.wait_ge(raw_in[i % RAW], 16 * total(loads, i, RAW))
                            if i >= IN_PIECES + 3:
                                act.wait_ge(half_out[i % 2], 16 * total(stores, i - 2, 2))
                            act.activation(upper, raw_piece, ACT.Copy).then_inc(w_upper, 1)
                        if i:
                            store_piece(i - 1)
                            if i - 1 + RAW < PIECES:
                                load_piece(i - 1 + RAW)
                    for k in range(2):
                        act.wait_ge(half_out[k], 16 * sum(stores(i) for i in range(k, PIECES, 2)))
                    act.wait_ge(s_w, 16 * N_W)
                    act.activation(a_exp[:, :], a_exp[:, :], ACT.Exp)

                @block.tensor
                def _(pe):
                    pe.wait_ge(s_ident, 1)

                    def fetch(n, k, inside):
                        par = k % 2
                        pe.wait_ge(ctx_in[k], inside * 16 + 16)
                        for b in range(PAIR):
                            wait(pe, a_c[b], n)
                            for c in range(KC):
                                for h in range(2):
                                    mm = pe.transpose(bank[2 + b][:, S * c + P * h:S * c + P * h + P],
                                                      cr[:, k, b, h, P * c:P * c + P], ident[:, :])
                            mm.then_inc(a_c_t, 1)
                        pe.wait_ge(a_rows_t, n + 1)
                        wait(pe, act_done, n - 1)
                        for c in range(KC):
                            mm = pe.transpose(bank[par][:, P * c:P * c + P], xn[:, par, P * c:P * c + P], ident[:, :])
                        mm.then_inc(a_x_t, 1)

                    def products(n, k):
                        par = k % 2
                        pe.wait_ge(act_done, n + 1)
                        pe.wait_ge(a_aa, n + 1)
                        pe.wait_ge(a_aa_act, n + 1)
                        wait(pe, a_clamp, n - 1)
                        for b in range(PAIR):
                            pe.wait_ge(a_c[b], n + 1)
                            q = slice(T * b, T * b + T)
                            for c in range(KC):
                                pe.matmul(bank[4 + par][q, 0:S], lhsT=xt[:, par, c, q], rhs=ct_t[:, par, b, c, :],
                                          start=(c == 0), stop=False)
                            for h in range(2):
                                mm = pe.matmul(bank[4 + par][q, P * h:P * h + P],
                                               lhsT=aa[:, k, b, h:h + 1].broadcast_to([P, T]), rhs=ident[:, :],
                                               start=False, stop=(h == 1))
                        mm.then_inc(a_mm, 1)

                    ahead(pe, fetch, products)
                    pe.wait_ge(w_upper, PIECES)
                    pe.wait_ge(dve_done, path_near)
                    keep_warm(pe, 24)

        def buf(name, shape, dt=F32):
            return sb("d_" + name, shape, dt)

        w_e = sb("w_e", [P, E + 1, 2, D], F32R)
        xg = buf("xg", [P, GT, D])
        U = xg[:, :, :].rearrange("p (h q) d -> p h (q d)", h=2)
        XT = buf("XT", [P, KC, GN], F32R)
        XT_low = buf("XT_low", [P, KC, GN], F32R)
        e_tile = buf("e_tile", [P, ER, 2, D], F32R)
        w_tile = buf("w_tile", [P, LR, 2, KC, P], F32R)
        dtv = buf("dtv", [P, GT, HEADS])
        dtn = buf("dtn", [P, GT, HEADS])
        dtu = buf("dtu", [P, GT, HEADS])
        dtl = buf("dtl", [P, GT, HEADS])
        dte = buf("dte", [P, GT, HEADS])
        dtd = buf("dtd", [P, GT, HEADS])
        dt_ = buf("dt", [P, GT, HEADS])
        da = buf("da", [P, GT, HEADS])
        da_h = buf("da_h", [P, GT, HEADS], F32R)
        da_s = buf("da_s", [P, 2 * GT, HEADS])
        bc_acc = buf("bc_acc", [2 * NS, GB, T])
        BC = buf("BC", [NS, 2, GB, T])
        zth = buf("zth", [P, 2, GN])
        bc_th = zth[:, 0].rearrange("p (q t) -> p q t", t=T)
        G = buf("G", [P, GT, T])
        with ExitStack() as experts_phase:
            def shared(name):
                return experts_phase.enter_context(nc.sbuf_tensor("d_" + name, [P, 2, GN], F32R))

            XF = shared("XF")
            XF_low = shared("XF_low")
            hh_up = shared("hh_up")
            hh_low = shared("hh_low")
        acc = buf("acc", [P, 2, GB, T])
        decay = buf("decay", [P, 2, GT, 2, T])
        M = buf("M", [P, 2, GT, 2, T])
        y1 = buf("y1", [P, 2, GN])
        th = buf("th", [P, 2, GN])
        xc = buf("xc", [P, RING, GN])
        zs = buf("zs", [P, RING, GN])
        xd = buf("xd", [P, 2, GT, 2, HD])
        steps = buf("steps", [P, 2, 2 * GT, 2, T], F32R)
        yg = buf("yg", [P, 2, GN])
        ysq = buf("ysq", [P, 2, GN])
        accq = buf("accq", [P, GN])
        e_g = buf("e_g", [P, GT, E])
        sc = buf("sc", [P, GT, E])
        cnt = buf("cnt", [P, GT, E])
        tot = buf("tot", [P, GT])
        gate = buf("gate", [P, GT, E + 1])
        gT = zth[0:E + 1, 0]
        hh = th
        mask = xc[:, 0:2].rearrange("p h (b t) -> p h b t", t=T)
        cmp_, cmp2 = [xd[:, k, 0:GT // 2].rearrange("p q h d -> p (q h d)").rearrange("p (q e f) -> p q e f", e=E, f=E)
                      for k in range(2)]

        names = ("d_const spread mask_ready expanded ln_var ln_sd ln_rows ln_t ln_xt_a ln_xt_v dt_logit dt_neg dt_ln "
                 "dt_ready bc_proj bc_in bc_conv bc_tanh bc_ready g_mm g_ready x_proj z_proj x_acc conv_done th_done "
                 "xc_done zth_done zs_done x_t xd_done r_done seg e_done m_done y_mm y_done yg_done sq_done accq_done "
                 "o_mm ssq r_sd logits sig gate_ready gate_t gt_ready h_mm h_done h_low f_mm f_acc d_chain out_done act_link").split()
        sm = {n: sem("d_" + n) for n in names}
        tile_in = [sem(f"tile_in{k}") for k in range(LR)]
        expert_in = [sem(f"expert_in{k}") for k in range(ER)]
        assert (E + 1) % ER == 0 and CT % LR == 0
        AL = "p (q t) -> p q t"
        SHARE = E
        order = [0, SHARE] + list(range(1, E))
        PER_F = GT * (E + 1)
        x_ch = lambda c: INNER + P * c
        z_ch = lambda c: P * c

        PE_PARTS = (1, 0, 1, 0, 0, 0, 0, 0, 0)
        ACT_PARTS = (0, 1, 0, 1, 0, 0, 0, 0, 1)
        DVE_PARTS = (0, 1, 1, 1, 0, 1, 0, 1, 0)

        def groups(engine, prepare, mamba, experts, chain=None, per=0):
            for _ in prepare(0):
                pass
            mamba(0)
            with engine.Fori(1, NG) as g:
                if chain:
                    chain.enter(g - 1, per)
                parts = prepare(g)
                experts(g - 1, parts)
                for _ in parts:
                    pass
                mamba(g)
                if chain:
                    chain.leave(NG - 1)
            experts(NG - 1, iter(()))

        with nc.Block() as block:
            @block.sync
            def _(sp):
                for k in range(CR):
                    sp.dma_start(cr[:, k], ctx_tiles[:, PAIR * k:PAIR * k + PAIR]).then_inc(ctx_in[k], 16)
                sp.dma_start(w_e[:, :, :, :].bitcast(F32), e_upper).then_inc(s_we, 16)

                def context(g):
                    for k in range(CR):
                        sp.wait_ge(sm["expanded"], (g - 1) * GT + k + 1)
                        sp.dma_start(cr[:, k], ctx_tiles[:, bass.ds((g * GT + k) * PAIR, PAIR)]).then_inc(ctx_in[k], 16)

                def finished(g):
                    sp.wait_ge(sm["f_acc"], (g + 1) * PER_F + 1)
                    sp.dma_start(out_rows[:, bass.ds(g * GT, GT), :], X[:, bass.ds(g * GT, GT), :]).then_inc(sm["out_done"], 16)

                def lower_halves(g, tiles, first=False):
                    for c in tiles:
                        if c >= LR or not first:
                            sp.wait_ge(sm["z_proj"], g * CT + c - LR + 1)
                        sp.dma_start(w_tile[:, c % LR].bitcast(F32), w_low[c]).then_inc(tile_in[c % LR], 16)

                def expert_halves(g, first=False):
                    for n in range(E + 1):
                        if n >= ER or not first:
                            sp.wait_ge(sm["f_mm"], g * (E + 1) + n - ER + 1)
                        sp.dma_start(e_tile[:, n % ER].bitcast(F32), e_lower[order[n]]).then_inc(expert_in[n % ER], 16)

                def feed(g, first=False, last=False):
                    if not last:
                        context(g + 1)
                    lower_halves(g, range(LR, LR + 1))
                    if not first:
                        finished(g - 1)
                    lower_halves(g, range(LR + 1, CT))
                    if not last:
                        lower_halves(g + 1, range(LR))
                    expert_halves(g, first)

                lower_halves(0, range(LR), first=True)
                feed(0, first=True)
                with sp.Fori(1, NG - 1) as g:
                    feed(g)
                feed(NG - 1, last=True)
                finished(NG - 1)
                sp.wait_ge(sm["out_done"], 16 * NG)

            @block.tensor
            def _(pe):
                pe.wait_ge(s_path, 1)
                pe.wait_ge(sm["d_const"], 1)

                def ln_transpose(g, u):
                    for t in range(GT):
                        pe.wait_ge(sm["ln_rows"], (g * 2 + u) * GT + t + 1)
                        for c in range(KC):
                            mm = pe.transpose(((p_t, p_s), (p_x, p_z))[u][c][:, P * t:P * t + P], xg[:, t, P * c:P * c + P], ident[:, :])
                    mm.then_inc(sm["ln_t"], 1)

                def split_products(psum, weights, tokens):
                    for k in range(KC):
                        w, x = weights(k), tokens(k)
                        pe.matmul(psum, lhsT=w[0], rhs=x[0], start=(k == 0), stop=False)
                        pe.matmul(psum, lhsT=w[0], rhs=x[1], start=False, stop=False)
                        mm = pe.matmul(psum, lhsT=w[1], rhs=x[0], start=False, stop=(k == KC - 1))
                    return mm

                def tokens(k):
                    return XT[:, k, :], XT_low[:, k, :]

                def prepare(g):
                    def warm(n):
                        if isinstance(g, int):
                            keep_warm(pe, n)

                    pe.matmul(p_t[:, :], lhsT=ones16[:, :], rhs=Hd[:, bass.ds(g * GB, GB), 1:T + 1], start=True, stop=True)
                    pe.matmul(p_s[:, :], lhsT=ones16[:, :], rhs=Hd[:, bass.ds(g * GB, GB), 0:T], start=True,
                              stop=True).then_inc(sm["spread"], 1)
                    yield
                    warm(8)
                    pe.wait_ge(sm["mask_ready"], g + 1)
                    for t in range(GT):
                        pe.wait_ge(ctx_in[t], 16 * (NT // CR) + g * 16 + 16)
                        for b in range(PAIR):
                            for h in range(2):
                                mm = pe.matmul((p_t, p_s)[t // 2][T * b:T * b + T, D * (t % 2):D * (t % 2) + D],
                                               lhsT=mask[:, h, PAIR * t + b, :], rhs=cr[:, t, b, h, :],
                                               start=(h == 0), stop=(h == 1))
                        mm.then_inc(sm["expanded"], 1)
                        if t % 2:
                            yield
                    warm(20)
                    ln_transpose(g, 0)
                    yield
                    warm(8)
                    pe.wait_ge(sm["ln_xt_a"], g * 2 + 1)
                    pe.wait_ge(sm["ln_xt_v"], g * 2 + 1)
                    for t in range(GT):
                        mm = split_products(p_t[:, HEADS * t:HEADS * t + HEADS],
                                            lambda k: (XT[:, k, P * t:P * t + P], XT_low[:, k, P * t:P * t + P]),
                                            lambda k: (w_in[:, k, PROJ - HEADS:PROJ], w_rest[:, k, REST - HEADS:REST]))
                    mm.then_inc(sm["dt_logit"], 1)
                    o = 2 * INNER
                    mm = split_products(p_s[:, :], lambda k: (w_in[:, k, o:o + 2 * NS], w_rest[:, k, 0:2 * NS]), tokens)
                    mm.then_inc(sm["bc_proj"], 1)
                    yield

                def output(g, c):
                    pe.wait_ge(sm["yg_done"], g * CT + c + 1)
                    for t in range(GT):
                        mm = pe.matmul((p_o0, p_o1)[t // 2][:, D * (t % 2):D * (t % 2) + D],
                                       lhsT=yg[:, c % 2, P * t:P * t + P], rhs=w_out[:, c, :],
                                       start=(c == 0 and t % 2 == 0), stop=(c == CT - 1), skip_group_check=True)
                    mm.then_inc(sm["o_mm"], 1)

                def mamba(g):
                    def project(c):
                        if c >= 1:
                            pe.wait_ge(sm["conv_done"], g * CT + c)
                        else:
                            wait(pe, sm["h_done"], g * (E + 1))
                        pe.wait_ge(tile_in[c % LR], (g * (CT // LR) + c // LR + 1) * 16)
                        mm = split_products(p_x[:, :], lambda k: (w_in[:, k, x_ch(c):x_ch(c) + P], w_tile[:, c % LR, 1, k, :]), tokens)
                        mm.then_inc(sm["x_proj"], 1)
                        if c >= 1:
                            pe.wait_ge(sm["zs_done"], g * CT + c)
                        mm = split_products(p_z[:, :], lambda k: (w_in[:, k, z_ch(c):z_ch(c) + P], w_tile[:, c % LR, 0, k, :]), tokens)
                        mm.then_inc(sm["z_proj"], 1)

                    def segments(c):
                        pe.wait_ge(sm["r_done"], g * CT + c + 1)
                        if c >= 1:
                            pe.wait_ge(sm["e_done"], g * CT + c)
                        for half in range(2):
                            mm = pe.matmul(p_s[:, :], lhsT=later[:, :],
                                           rhs=steps[:, c % 2, GT * half:GT * half + GT].rearrange("p q h t -> p (q h t)"),
                                           start=(half == 0), stop=(half == 1))
                        mm.then_inc(sm["seg"], 1)

                    def turn(c):
                        pe.wait_ge(sm["xc_done"], g * CT + c + 1)
                        if c >= 1:
                            pe.wait_ge(sm["xd_done"], g * CT + c)
                        else:
                            pe.wait_ge(sm["g_ready"], g + 1)
                        for t in range(GT):
                            mm = pe.transpose(p_t[:, P * t:P * t + P], xc[:, c % RING, P * t:P * t + P], ident[:, :])
                        mm.then_inc(sm["x_t"], 1)

                    def mix(c):
                        pe.wait_ge(sm["xd_done"], g * CT + c + 1)
                        pe.wait_ge(sm["m_done"], g * CT + c + 1)
                        if c >= 1:
                            pe.wait_ge(sm["y_done"], g * CT + c)
                        else:
                            pe.wait_ge(sm["f_acc"], g * PER_F + 1)
                        carrier(pe, p_y0)
                        for t in range(GT):
                            for b in range(PAIR):
                                q = slice(T * b, T * b + T)
                                for h in range(2):
                                    mm = pe.matmul((p_y0, p_y1)[b][HD * h:HD * h + HD, T * t:T * t + T],
                                                   lhsT=xd[q, c % 2, t, h, :], rhs=M[q, c % 2, t, h, :],
                                                   start=True, stop=True)
                        mm.then_inc(sm["y_mm"], 1)

                    def score():
                        for b in range(GB):
                            if b == 0:
                                pe.wait_ge(sm["bc_ready"], g + 1)
                                pe.wait_ge(sm["dt_ready"], g + 1)
                                carrier(pe, p_t)
                            mm = pe.matmul(p_t[T * (b % 2):T * (b % 2) + T, T * (b // 2):T * (b // 2) + T],
                                           lhsT=BC[:, 0, b, :], rhs=BC[:, 1, b, :], start=True, stop=True)
                        mm.then_inc(sm["g_mm"], 1)

                    for k in range(CT + 2):
                        if k < CT:
                            project(k)
                            if k == 0:
                                if isinstance(g, int):
                                    keep_warm(pe, 22)
                                score()
                            segments(k)
                        if 1 <= k <= CT:
                            turn(k - 1)
                        if 2 <= k <= CT + 1:
                            mix(k - 2)
                        if 3 <= k <= CT:
                            output(g, k - 3)

                def experts(g, others):
                    next(others, None)
                    output(g, CT - 2)
                    output(g, CT - 1)
                    keep_warm(pe, 3)
                    pe.wait_ge(sm["accq_done"], g * CT + CT)
                    for t in range(GT):
                        mm = pe.matmul(p_y0[:, t:t + 1], lhsT=accq[:, P * t:P * t + P], rhs=ones[:, :], start=True, stop=True)
                    mm.then_inc(sm["ssq"], 1)
                    for _ in range(2):
                        next(others, None)
                    keep_warm(pe, 9)
                    ln_transpose(g, 1)
                    keep_warm(pe, 6)
                    pe.wait_ge(sm["ln_xt_a"], g * 2 + 2)
                    pe.wait_ge(sm["ln_xt_v"], g * 2 + 2)
                    for t in range(GT):
                        mm = split_products(p_y0[:, E * t:E * t + E],
                                            lambda k: (XF[:, k, P * t:P * t + P], XF_low[:, k, P * t:P * t + P]),
                                            lambda k: (w_gate_up[:, k, :], w_gate_low[:, k, :]))
                    mm.then_inc(sm["logits"], 1)

                    def hidden(n):
                        e = order[n]
                        if n >= 2:
                            pe.wait_ge(sm["h_done"], g * (E + 1) + n - 1)
                        pe.wait_ge(expert_in[n % ER], (g * ((E + 1) // ER) + n // ER + 1) * 16)
                        mm = split_products((p_x, p_z)[n % 2][:, :],
                                            lambda k: (w_e[:, e, 0, H * k:H * k + H], e_tile[:, n % ER, 0, H * k:H * k + H]),
                                            lambda k: (XF[:, k, :], XF_low[:, k, :]))
                        mm.then_inc(sm["h_mm"], 1)

                    def down(n):
                        e = order[n]
                        if n >= 2:
                            pe.wait_ge(sm["f_acc"], g * PER_F + GT * (n - 1) + 1)
                        if order[n] == SHARE:
                            pe.wait_ge(sm["gt_ready"], g + 1)
                        for t in range(GT):
                            o = ((p_y0, p_y1), (p_o0, p_o1))[n % 2][t // 2][:, D * (t % 2):D * (t % 2) + D]
                            if t % 2 == 0:
                                pe.wait_ge(sm["h_low"], (g * (E + 1) + n) * 2 + t // 2 + 1)
                            x = [half[:, n % 2, P * t:P * t + P] for half in (hh_up, hh_low)]
                            w = w_e[:, e, 1, :], e_tile[:, n % ER, 1, :]
                            pe.matmul(o, lhsT=x[0], rhs=w[0], start=True, stop=False)
                            pe.matmul(o, lhsT=x[0], rhs=w[1], start=False, stop=False)
                            mm = pe.matmul(o, lhsT=x[1], rhs=w[0], start=False, stop=(order[n] != SHARE))
                            if order[n] == SHARE:
                                mm = pe.matmul(o, lhsT=gT[:, P * t:P * t + P], rhs=b_2[:, :], start=False, stop=True)
                        mm.then_inc(sm["f_mm"], 1)

                    pe.wait_ge(s_we, 16)
                    hidden(0)
                    hidden(1)
                    keep_warm(pe, 6)
                    for n in range(E + 1):
                        down(n)
                        if n + 2 < E + 1:
                            hidden(n + 2)
                        if order[n + 1:n + 2] == [SHARE]:
                            pe.wait_ge(sm["gate_ready"], g + 1)
                            for t in range(GT):
                                mm = pe.transpose(p_o1[0:E + 1, P * t:P * t + P], gate[:, t, :], ident[:, :])
                            mm.then_inc(sm["gate_t"], 1)
                        for _ in range(PE_PARTS[n]):
                            next(others, None)

                groups(pe, prepare, mamba, experts)


            @block.scalar
            def _(act):
                act.wait_ge(sm["d_const"], 1)

                def ln_root(g, u):
                    act.wait_ge(sm["ln_var"], g * 2 + u + 1)
                    act.activation(sd[:, u, :], mv[:, u, :, 1], ACT.Sqrt, bias=eps1[:, :]).then_inc(sm["ln_sd"], 1)

                def ln_take(g, u):
                    act.wait_ge(sm["ln_t"], g * 2 + u + 1)
                    act.activation((XT, XF)[u][:, 0, :], (p_t, p_x)[u][:, :], ACT.Copy).then_inc(sm["ln_xt_a"], 1)

                def prepare(g):
                    ln_root(g, 0)
                    yield
                    ln_take(g, 0)
                    yield
                    act.wait_ge(sm["dt_neg"], g + 1)
                    act.activation(dtu[:, :, :], dtn[:, :, :], ACT.Exp).then_inc(sm["act_link"], 1)
                    act.wait_ge(sm["act_link"], g + 1)
                    act.activation(dtl[:, :, :], dtu[:, :, :], ACT.Ln, bias=ones[:, :]).then_inc(sm["dt_ln"], 1)
                    act.wait_ge(sm["bc_proj"], g + 1)
                    act.activation(bc_acc[:, :, :], p_s[:, :].rearrange(AL, t=T), ACT.Identity, bias=cb_bc[:, :],
                                   scale=cw_bc[:, PAD:TAPS]).then_inc(sm["bc_in"], 1)
                    yield
                    act.wait_ge(sm["bc_conv"], g + 1)
                    act.activation(bc_th, bc_acc[:, :, :], ACT.Tanh).then_inc(sm["bc_tanh"], 1)

                def mamba(g):
                    def take_x(c):
                        act.wait_ge(sm["x_proj"], g * CT + c + 1)
                        if c >= 2:
                            act.wait_ge(sm["xc_done"], g * CT + c - 1)
                        act.activation(acc[:, c % 2], p_x[:, :].rearrange(AL, t=T), ACT.Identity, bias=cb[:, c:c + 1],
                                       scale=cw[:, c, PAD:TAPS]).then_inc(sm["x_acc"], 1)

                    def tanh_z(c):
                        act.wait_ge(sm["z_proj"], g * CT + c + 1)
                        if c == 0:
                            act.wait_ge(sm["bc_ready"], g + 1)
                        if c >= 2:
                            act.wait_ge(sm["zs_done"], g * CT + c - 1)
                        act.activation(zth[:, c % 2], p_z[:, :], ACT.Tanh, scale=0.5).then_inc(sm["zth_done"], 1)

                    def decays(c):
                        act.wait_ge(sm["seg"], g * CT + c + 1)
                        if c >= 2:
                            act.wait_ge(sm["m_done"], g * CT + c - 1)
                        act.activation(decay[:, c % 2].rearrange("p q h t -> p (q h t)"), p_s[:, :],
                                       ACT.Exp).then_inc(sm["e_done"], 1)

                    def tanh_x(c):
                        act.wait_ge(sm["conv_done"], g * CT + c + 1)
                        if c >= 2:
                            act.wait_ge(sm["xc_done"], g * CT + c - 1)
                        act.activation(th[:, c % 2].rearrange(AL, t=T), acc[:, c % 2], ACT.Tanh).then_inc(sm["th_done"], 1)

                    def square(c):
                        act.wait_ge(sm["yg_done"], g * CT + c + 1)
                        if c >= 2:
                            act.wait_ge(sm["accq_done"], g * CT + c - 1)
                        act.activation(ysq[:, c % 2], yg[:, c % 2], ACT.Square).then_inc(sm["sq_done"], 1)

                    for k in range(CT + 3):
                        if k < CT:
                            take_x(k)
                            tanh_z(k)
                            decays(k)
                            tanh_x(k)
                        if k >= 3:
                            square(k - 3)

                def experts(g, others):
                    act.wait_ge(sm["ssq"], g + 1)
                    act.activation(sd[:, 2, :], p_y0[:, 0:GT], ACT.Sqrt, bias=eps4[:, :], scale=1.0 / INNER).then_inc(sm["r_sd"], 1)
                    ln_root(g, 1)
                    ln_take(g, 1)
                    next(others, None)
                    act.wait_ge(sm["logits"], g + 1)
                    act.activation(e_g[:, :, :], p_y0[:, 0:GT * E].rearrange("p (q e) -> p q e", e=E), ACT.Exp,
                                   scale=-1.0).then_inc(sm["sig"], 1)
                    for n in range(E + 1):
                        act.wait_ge(sm["h_mm"], g * (E + 1) + n + 1)
                        if n >= 2:
                            act.wait_ge(sm["f_mm"], g * (E + 1) + n - 1)
                        for to in (hh_up, hh):
                            ins = act.activation(to[:, n % 2], (p_x, p_z)[n % 2][:, :], ACT.Gelu,
                                                 bias=b_1[:, order[n]:order[n] + 1])
                        ins.then_inc(sm["h_done"], 1)
                        for _ in range(ACT_PARTS[n]):
                            next(others, None)

                groups(act, prepare, mamba, experts)

            @block.gpsimd
            def _(pool):
                pool.memset(gate[:, :, E:E + 1], 1.0).then_inc(sm["d_const"], 1)
                with pool.Fori(0, NG) as g:
                    pool.wait_ge(sm["dt_ready"], g + 1)

                    def make_steps(c):
                        if c >= 2:
                            pool.wait_ge(sm["seg"], g * CT + c - 1)
                        pool.tensor_tensor(steps[:, c % 2],
                                           da_s[:, :, 2 * c:2 * c + 2].rearrange("p q (h o) -> p q h o", o=1).broadcast_to([P, 2 * GT, 2, T]),
                                           tri[:, :].rearrange("p (a b t) -> p a b t", a=1, b=1).broadcast_to([P, 2 * GT, 2, T]),
                                           ALU.mult).then_inc(sm["r_done"], 1)

                    def make_mix(c):
                        pool.wait_ge(sm["e_done"], g * CT + c + 1)
                        if c == 0:
                            pool.wait_ge(sm["g_ready"], g + 1)
                        if c >= 2:
                            pool.wait_ge(sm["y_mm"], g * CT + c - 1)
                        pool.tensor_tensor(M[:, c % 2], decay[:, c % 2],
                                           G[:, :, :].rearrange("p q (o t) -> p q o t", o=1).broadcast_to([P, GT, 2, T]),
                                           ALU.mult).then_inc(sm["m_done"], 1)

                    def gate_y(c):
                        pool.wait_ge(sm["y_done"], g * CT + c + 1)
                        if c >= 2:
                            pool.wait_ge(sm["o_mm"], g * CT + c - 1)
                            pool.wait_ge(sm["sq_done"], g * CT + c - 1)
                        pool.tensor_tensor(yg[:, c % 2], y1[:, c % 2], zs[:, c % RING], ALU.mult).then_inc(sm["yg_done"], 1)

                    def sum_squares(c):
                        pool.wait_ge(sm["sq_done"], g * CT + c + 1)
                        if c == 0:
                            pool.tensor_tensor(accq[:, :], ysq[:, 0], zero[:, :].broadcast_to([P, GN]), ALU.add).then_inc(sm["accq_done"], 1)
                        else:
                            pool.wait_ge(sm["accq_done"], g * CT + c)
                            pool.tensor_tensor(accq[:, :], accq[:, :], ysq[:, c % 2], ALU.add).then_inc(sm["accq_done"], 1)

                    make_steps(0)
                    for k in range(CT + 3):
                        if k + 1 < CT:
                            make_steps(k + 1)
                        if k < CT:
                            make_mix(k)
                        if 2 <= k <= CT + 1:
                            gate_y(k - 2)
                        if k >= 3:
                            sum_squares(k - 3)
                    for n in range(E + 1):
                        pool.wait_ge(sm["h_done"], g * (E + 1) + n + 1)
                        if n >= 2:
                            pool.wait_ge(sm["f_mm"], g * (E + 1) + n - 1)
                        for half in range(2):
                            q = slice(GN // 2 * half, GN // 2 * half + GN // 2)
                            pool.tensor_tensor(hh_low[:, n % 2, q], hh[:, n % 2, q], hh_up[:, n % 2, q].bitcast(F32),
                                               ALU.subtract).then_inc(sm["h_low"], 1)

            @block.vector
            def _(v):
                ch = Chain(v, sm["d_chain"])
                v.memset(spare[:, :], 0.0).then_inc(sm["f_acc"], 1)
                v.wait_ge(sm["f_acc"], 1)
                v.wait_ge(sm["d_const"], 1)

                def xtile(g, t):
                    return X[:, bass.ds(g * GT + t, 1), :].rearrange("p o d -> p (o d)")

                def ln_stats(g, u):
                    for t in range(GT):
                        ins = v.bn_stats(bn[:, u, t, :], xtile(g, t))
                    ch.link(ins, bare=True)
                    for t in range(GT):
                        ins = v.bn_aggr(mv[:, u, t, :], bn[:, u, t, :])
                    ins.then_inc(sm["ln_var"], 1)

                def ln_rows(g, u):
                    v.wait_ge(sm["ln_sd"], g * 2 + u + 1)
                    ch.link(v.reciprocal(rs[:, u, :], sd[:, u, :]))
                    for t in range(GT):
                        v.tensor_scalar(xg[:, t, :], xtile(g, t), mv[:, u, t, 0:1], rs[:, u, t:t + 1], ALU.subtract,
                                        ALU.mult).then_inc(sm["ln_rows"], 1)

                def ln_take(g, u):
                    v.wait_ge(sm["ln_t"], g * 2 + u + 1)
                    up, low_ = ((XT, XT_low), (XF, XF_low))[u]
                    psum = ((p_t, p_s), (p_x, p_z))[u]
                    ch.link(v.tensor_copy(up[:, 1, :], psum[1][:, :]))
                    v.tensor_tensor(low_[:, 1, :], psum[1][:, :], up[:, 1, :].bitcast(F32), ALU.subtract)
                    v.wait_ge(sm["ln_xt_a"], g * 2 + u + 1)
                    v.tensor_tensor(low_[:, 0, :], psum[0][:, :], up[:, 0, :].bitcast(F32), ALU.subtract).then_inc(sm["ln_xt_v"], 1)

                def prepare(g):
                    v.wait_ge(sm["spread"], g + 1)
                    for h in range(2):
                        ins = v.tensor_scalar(U[:, h, :], p_t[:, :], row_id[:, h:h + 1], None, ALU.is_ge)
                    ch.link(ins)
                    for h in range(2):
                        ins = v.scalar_tensor_tensor(mask[:, h].rearrange("p b t -> p (b t)"), p_s[:, :], row_id[:, h:h + 1],
                                                     U[:, h, :], ALU.is_le, ALU.mult)
                    ins.then_inc(sm["mask_ready"], 1)
                    yield
                    for t in range(GT):
                        v.wait_ge(sm["expanded"], g * GT + t // 2 * 2 + 2)
                        ins = v.tensor_tensor(xtile(g, t), xtile(g, t), (p_t, p_s)[t // 2][:, D * (t % 2):D * (t % 2) + D], ALU.add)
                    ch.link(ins, bare=True)
                    ln_stats(g, 0)
                    yield
                    ln_rows(g, 0)
                    yield
                    ln_take(g, 0)
                    yield

                    v.wait_ge(sm["dt_logit"], g + 1)
                    ch.link(v.tensor_tensor(dtv[:, :, :], p_t[:, 0:GT * HEADS].rearrange("p (q h) -> p q h", h=HEADS),
                                            dtb[:, :].rearrange("p (o h) -> p o h", o=1).broadcast_to([P, GT, HEADS]), ALU.add))
                    v.scalar_tensor_tensor(dtn[:, :, :], dtv[:, :, :], -1.0, dtv[:, :, :], ALU.mult,
                                           ALU.min).then_inc(sm["dt_neg"], 1)
                    yield
                    v.wait_ge(sm["dt_ln"], g + 1)
                    ch.link(v.tensor_scalar(dtd[:, :, :], dtu[:, :, :], 1.0, -1.0, ALU.add, ALU.add))
                    ch.link(v.tensor_scalar(dte[:, :, :], dtd[:, :, :], 0.0, None, ALU.is_equal))
                    ch.link(v.tensor_tensor(dtd[:, :, :], dtd[:, :, :], dte[:, :, :], ALU.add))
                    ch.link(v.tensor_tensor(dtl[:, :, :], dtl[:, :, :], dte[:, :, :], ALU.add))
                    ch.link(v.reciprocal(dtd[:, :, :], dtd[:, :, :]))
                    ch.link(v.tensor_tensor(dtl[:, :, :], dtl[:, :, :], dtu[:, :, :], ALU.mult))
                    ch.link(v.tensor_tensor(dtl[:, :, :], dtl[:, :, :], dtd[:, :, :], ALU.mult))
                    ch.link(v.scalar_tensor_tensor(dt_[:, :, :], dtv[:, :, :], 0.0, dtl[:, :, :], ALU.max, ALU.add))
                    ch.link(v.scalar_tensor_tensor(da[:, :, :], dt_[:, :, :], -1.0,
                                                   a_exp[:, :].rearrange("p (o h) -> p o h", o=1).broadcast_to([P, GT, HEADS]),
                                                   ALU.mult, ALU.mult))
                    ch.link(v.tensor_copy(da_h[:, :, :], da[:, :, :]))
                    v.tensor_copy(da_s[:, 0:GT, :], da_h[:, :, :].bitcast(F32))
                    v.tensor_tensor(da_s[:, GT:2 * GT, :], da[:, :, :], da_h[:, :, :].bitcast(F32),
                                    ALU.subtract).then_inc(sm["dt_ready"], 1)

                    yield
                    v.wait_ge(sm["bc_in"], g + 1)
                    for k in range(PAD - 1, -1, -1):
                        back = PAD - k
                        a = bc_acc[:, :, back:T]
                        ins = v.scalar_tensor_tensor(a, p_s[:, :].rearrange(AL, t=T)[:, :, 0:T - back], cw_bc[:, k:k + 1], a,
                                                     ALU.mult, ALU.add)
                        if k:
                            ch.link(ins)
                    ins.then_inc(sm["bc_conv"], 1)
                    yield
                    v.wait_ge(sm["bc_tanh"], g + 1)
                    for j in range(2):
                        q = slice(NS * j, NS * j + NS)
                        ins = v.scalar_tensor_tensor(BC[:, j], bc_th[q], 1.0, bc_acc[q], ALU.add, ALU.mult)
                    ins.then_inc(sm["bc_ready"], 1)

                def mamba(g):
                    def conv(c):
                        v.wait_ge(sm["x_acc"], g * CT + c + 1)
                        for k in range(PAD - 1, -1, -1):
                            back = PAD - k
                            a = acc[:, c % 2, :, back:T]
                            ins = v.scalar_tensor_tensor(a, p_x[:, :].rearrange(AL, t=T)[:, :, 0:T - back], cw[:, c, k:k + 1], a,
                                                         ALU.mult, ALU.add)
                            if k:
                                ch.link(ins)
                        ins.then_inc(sm["conv_done"], 1)

                    def silu_z(c):
                        v.wait_ge(sm["zth_done"], g * CT + c + 1)
                        if c >= RING:
                            v.wait_ge(sm["yg_done"], g * CT + c - RING + 1)
                        v.scalar_tensor_tensor(zs[:, c % RING], zth[:, c % 2], 1.0, p_z[:, :], ALU.add,
                                               ALU.mult).then_inc(sm["zs_done"], 1)

                    def silu_x(c):
                        v.wait_ge(sm["th_done"], g * CT + c + 1)
                        if c >= RING:
                            v.wait_ge(sm["x_t"], g * CT + c - RING + 1)
                        v.scalar_tensor_tensor(xc[:, c % RING].rearrange(AL, t=T), th[:, c % 2].rearrange(AL, t=T), 1.0,
                                               acc[:, c % 2], ALU.add, ALU.mult).then_inc(sm["xc_done"], 1)

                    def scale_x(c):
                        v.wait_ge(sm["x_t"], g * CT + c + 1)
                        if c >= 2:
                            v.wait_ge(sm["y_mm"], g * CT + c - 1)
                        v.tensor_tensor(xd[:, c % 2], p_t[:, :].rearrange("p (q h d) -> p q h d", q=GT, h=2),
                                        dt_[:, :, 2 * c:2 * c + 2].rearrange("p q (h o) -> p q h o", o=1).broadcast_to([P, GT, 2, HD]),
                                        ALU.mult).then_inc(sm["xd_done"], 1)

                    def skip_x(c):
                        v.wait_ge(sm["y_mm"], g * CT + c + 1)
                        if c >= 2:
                            v.wait_ge(sm["yg_done"], g * CT + c - 1)
                        for b in range(PAIR):
                            xv = xc[:, c % RING].rearrange("p (q b t) -> p q b t", q=GT, b=PAIR)[:, :, b, :]
                            yv = y1[:, c % 2].rearrange("p (q b t) -> p q b t", q=GT, b=PAIR)[:, :, b, :]
                            ins = v.scalar_tensor_tensor(yv, xv, d_ch[:, c:c + 1],
                                                         (p_y0, p_y1)[b][:, 0:GT * T].rearrange("p (q t) -> p q t", t=T),
                                                         ALU.mult, ALU.add)
                        ins.then_inc(sm["y_done"], 1)

                    for k in range(CT + 3):
                        if k < CT:
                            conv(k)
                            if k == 0:
                                v.wait_ge(sm["g_mm"], g + 1)
                                v.tensor_tensor(G[:, :, :], p_t[:, 0:GT * T].rearrange("p (q t) -> p q t", t=T),
                                                tri[:, :].rearrange("p (o t) -> p o t", o=1).broadcast_to([P, GT, T]),
                                                ALU.mult).then_inc(sm["g_ready"], 1)
                            silu_z(k)
                        if 1 <= k <= CT:
                            scale_x(k - 1)
                        if k < CT:
                            silu_x(k)
                        if 2 <= k <= CT + 1:
                            skip_x(k - 2)

                def experts(g, others):
                    next(others, None)
                    v.wait_ge(sm["r_sd"], g + 1)
                    ch.link(v.reciprocal(rs[:, 2, :], sd[:, 2, :]))
                    v.wait_ge(sm["o_mm"], g * CT + CT)
                    for t in range(GT):
                        ins = v.scalar_tensor_tensor(xtile(g, t), (p_o0, p_o1)[t // 2][:, D * (t % 2):D * (t % 2) + D],
                                                     rs[:, 2, t:t + 1], xtile(g, t), ALU.mult, ALU.add)
                    ch.link(ins, bare=True)
                    ln_stats(g, 1)
                    ln_rows(g, 1)
                    ln_take(g, 1)
                    next(others, None)

                    v.wait_ge(sm["sig"], g + 1)
                    ch.link(v.tensor_scalar(e_g[:, :, :], e_g[:, :, :], 1.0, None, ALU.add))
                    ch.link(v.reciprocal(e_g[:, :, :], e_g[:, :, :]))
                    ch.link(v.tensor_scalar(sc[:, :, :], e_g[:, :, :], rsc[:, 0:1], None, ALU.mult))
                    mine = sc[:, :, :].rearrange("p q (e o) -> p q e o", o=1).broadcast_to([P, GT, E, E])
                    other = sc[:, :, :].rearrange("p q (o f) -> p q o f", o=1).broadcast_to([P, GT, E, E])
                    v.tensor_tensor(cmp_[:, :, :, :], other, mine, ALU.is_equal).then_inc(sm["d_chain"], 1)
                    ch.n += 1
                    ch.link(v.tensor_tensor(cmp2[:, :, :, :], other, mine, ALU.is_gt))
                    ch.link(v.tensor_tensor(cmp_[:, :, :, :], cmp_[:, :, :, :],
                                            below[:, :, :].rearrange("p (o e) f -> p o e f", o=1).broadcast_to([P, GT, E, E]), ALU.mult))
                    ch.link(v.tensor_tensor(cmp_[:, :, :, :], cmp_[:, :, :, :], cmp2[:, :, :, :], ALU.add))
                    ch.link(v.tensor_reduce(cnt[:, :, :], cmp_[:, :, :, :], AX_X, ALU.add))
                    ch.link(v.scalar_tensor_tensor(e_g[:, :, :], cnt[:, :, :], 2.0, sc[:, :, :], ALU.is_lt, ALU.mult))
                    ch.link(v.tensor_reduce(tot[:, :], e_g[:, :, :], AX_X, ALU.add))
                    ch.link(v.reciprocal(tot[:, :], tot[:, :]))
                    v.tensor_tensor(gate[:, :, 0:E], e_g[:, :, :],
                                    tot[:, :].rearrange("p (q o) -> p q o", o=1).broadcast_to([P, GT, E]),
                                    ALU.mult).then_inc(sm["gate_ready"], 1)
                    next(others, None)

                    v.wait_ge(sm["gate_ready"], g + 1)
                    for n in range(E + 1):
                        v.wait_ge(sm["f_mm"], g * (E + 1) + n + 1)
                        banks = ((p_y0, p_y1), (p_o0, p_o1))[n % 2]
                        for t in range(GT):
                            if n:
                                v.wait_ge(sm["f_acc"], g * PER_F + GT * (n - 1) + t + 1 + 1)
                            part = banks[t // 2][:, D * (t % 2):D * (t % 2) + D]
                            if order[n] == SHARE:
                                ins = v.tensor_tensor(xtile(g, t), xtile(g, t), part, ALU.add)
                            else:
                                ins = v.scalar_tensor_tensor(xtile(g, t), part, gate[:, t, order[n]:order[n] + 1],
                                                             xtile(g, t), ALU.mult, ALU.add)
                            ins.then_inc(sm["f_acc"], 1)
                        if order[n + 1:n + 2] == [SHARE]:
                            v.wait_ge(sm["gate_t"], g + 1)
                            v.tensor_copy(gT[:, :], p_o1[0:E + 1, :]).then_inc(sm["gt_ready"], 1)
                        for _ in range(DVE_PARTS[n]):
                            next(others, None)

                groups(v, prepare, mamba, experts, ch, CHAIN_D)


_INS = ["x", "ctx_1024", "L0_attn_W_in", "L0_attn_conv_w", "L0_attn_conv_b", "L0_attn_A_log", "L0_attn_D_param",
        "L0_attn_dt_bias", "L0_attn_norm_w", "L0_attn_W_out", "L0_ffn_gate_W", "L0_ffn_W1", "L0_ffn_b1", "L0_ffn_W2",
        "L0_ffn_b2", "L0_ffn_Ws1", "L0_ffn_bs1", "L0_ffn_Ws2", "L0_ffn_bs2", "L0_ffn_route_scale"]


def kernel(**inputs):
    import numpy as _np
    import concourse.bacc as _bacc
    from concourse import mybir as _mybir
    from concourse.bass_utils import run_bass_kernel_spmd as _run

    nc = _bacc.Bacc("TRN2", target_bir_lowering=False, num_devices=1)
    arrays, args = {}, []
    for name in _INS:
        a = _np.ascontiguousarray(inputs[name])
        if name == "L0_ffn_route_scale":
            a = a.reshape(1)
        arrays[f"in_{name}_dram"] = a
        args.append(nc.dram_tensor(f"in_{name}_dram", a.shape, _mybir.dt.from_np(a.dtype), kind="ExternalInput").ap())
    args.append(nc.dram_tensor("out_dram", (NB, T, D), F32, kind="ExternalOutput").ap())
    perceiver(nc, *args)
    r = _run(nc, [arrays], core_ids=[0])
    return r.results[0]["out_dram"]
```
